# Optimizing a Trainium2 kernel written in Bass

```python
import numpy as np
import jax
import jax.numpy as jnp

def _softmax(x, axis=-1):
    return jax.nn.softmax(x, axis=axis)

def _gelu(x):
    return jax.nn.gelu(x, approximate=True)

def _silu(x):
    return jax.nn.silu(x)

def _sigmoid(x):
    return jax.nn.sigmoid(x)

def _layernorm(x, axis=-1, eps=1e-05):
    m = jnp.mean(x, axis=axis, keepdims=True)
    v = jnp.var(x, axis=axis, keepdims=True)
    return (x - m) / jnp.sqrt(v + eps)

def _scatter_add(tgt, idx, src, axis=0):
    return tgt.at[idx].add(src)

def _segment_sum(src, seg, n):
    return jax.ops.segment_sum(src, seg, n)
kernel_name = 'mk_decoder_preln_d2_seqx_r4_331555'

def setup_inputs(seed: int=0):
    np.random.seed(seed)
    _w = jnp.asarray

    def _rec_inputs():
        import jax
        import jax.numpy as jnp
        _rk = jax.random.key(seed)
        x = -0.0003929 + 0.9999 * jax.random.normal(jax.random.fold_in(_rk, 1), (4, 512, 256), jnp.float32)
        _lenS = 512 - jax.random.randint(jax.random.fold_in(_rk, 7), (4,), 0, max(1, 512 // 4) + 1, jnp.int32)
        _lenS2 = 1601 - jax.random.randint(jax.random.fold_in(_rk, 8), (4,), 0, max(1, 1601 // 4) + 1, jnp.int32)
        _ctx_512P = jax.random.normal(jax.random.fold_in(_rk, 11), (4, 16, 128), jnp.float32)
        _ctx_512c = jax.random.dirichlet(jax.random.fold_in(_rk, 511), 0.3 * jnp.ones((16,), jnp.float32), (4, 1601))
        _ctx_512t = jnp.einsum('bsk,bkd->bsd', _ctx_512c, _ctx_512P)
        _ctx_512t = _ctx_512t * jax.lax.rsqrt(jnp.mean(jnp.square(_ctx_512t)) + 1e-12) * 0.953939
        ctx_512 = 4.13588e-05 + 0.999923 * (_ctx_512t + 0.3 * jax.random.normal(jax.random.fold_in(_rk, 611), (4, 1601, 128), jnp.float32))
        return (x, ctx_512)
    x, ctx_512 = _rec_inputs()

    def _L0_attn_setup():
        import jax, jax.numpy as jnp
        import numpy as np
        B, T, D = (1, 256, 256)
        HQ, HKV, HK, HV = (16, 4, 64, 64)
        KW = 4
        N_CHEB = 2
        CHEB_DAMP = 0.25
        EPS = 1e-06

        def _gka_core(x, Wq, Wk, Wv, Wconv, Wa, Walpha, Wb, A_log, dt_bias, norm_w, Wo):
            Bx, Tx, _ = x.shape
            qkv = jnp.concatenate([x @ Wq, x @ Wk, x @ Wv], axis=-1)
            pad = jnp.pad(qkv, ((0, 0), (KW - 1, 0), (0, 0)))
            conv = sum((pad[:, i:i + Tx, :] * Wconv[:, i] for i in range(KW)))
            qkv = jax.nn.silu(conv)
            q, k, v = jnp.split(qkv, [HQ * HK, HQ * HK + HKV * HK], axis=-1)
            q = q.reshape(Bx, Tx, HQ, HK)
            k = k.reshape(Bx, Tx, HKV, HK)
            v = v.reshape(Bx, Tx, HKV, HV)
            g = -jnp.exp(A_log) * jax.nn.softplus(x @ Wa + dt_bias)
            alpha = jax.nn.sigmoid(x @ Walpha)
            beta = jax.nn.sigmoid(x @ Wb)
            v = v * beta[..., None]
            k = k / (jnp.linalg.norm(k, axis=-1, keepdims=True) + EPS)
            q = q * HK ** (-0.5)
            rep = HQ // HKV
            k = jnp.repeat(k, rep, axis=2)
            v = jnp.repeat(v, rep, axis=2)

            def step(carry, inp):
                Hkk, Hkv = carry
                qt, kt, vt, gt = inp
                d = jnp.exp(gt)[..., None, None]
                Hkk = d * Hkk + kt[..., :, None] * kt[..., None, :]
                Hkv = d * Hkv + kt[..., :, None] * vt[..., None, :]
                xq = qt
                for _ in range(N_CHEB):
                    xq = qt - CHEB_DAMP * jnp.einsum('bhk,bhkl->bhl', xq, Hkk)
                ot = jnp.einsum('bhk,bhkv->bhv', xq, Hkv)
                return ((Hkk, Hkv), ot)
            tm = lambda a: jnp.moveaxis(a, 1, 0)
            init = (jnp.zeros((Bx, HQ, HK, HK), jnp.float32), jnp.zeros((Bx, HQ, HK, HV), jnp.float32))
            _, o = jax.lax.scan(step, init, (tm(q), tm(k), tm(v), tm(g)))
            o = jnp.moveaxis(o, 0, 1)
            o = o * alpha[..., None]
            o = o * jax.lax.rsqrt(jnp.mean(o * o, axis=-1, keepdims=True) + EPS) * norm_w
            return o.reshape(Bx, Tx, HQ * HV) @ Wo
        key = jax.random.key(seed)
        ks = jax.random.split(key, 12)
        C = HQ * HK + HKV * HK + HKV * HV
        s = lambda d: 1.0 / np.sqrt(d)
        inp = {'x': jax.random.normal(ks[0], (B, T, D), jnp.float32), 'Wq': jax.random.normal(ks[1], (D, HQ * HK), jnp.float32) * s(D), 'Wk': jax.random.normal(ks[2], (D, HKV * HK), jnp.float32) * s(D), 'Wv': jax.random.normal(ks[3], (D, HKV * HV), jnp.float32) * s(D), 'Wconv': jax.random.normal(ks[4], (C, KW), jnp.float32) * 0.2, 'Wa': jax.random.normal(ks[5], (D, HQ), jnp.float32) * s(D), 'Walpha': jax.random.normal(ks[6], (D, HQ), jnp.float32) * s(D), 'Wb': jax.random.normal(ks[7], (D, HKV), jnp.float32) * s(D), 'A_log': jnp.log(jax.random.uniform(ks[8], (HQ,), jnp.float32, 1.0, 16.0)), 'dt_bias': jax.random.normal(ks[9], (HQ,), jnp.float32) * 0.5, 'norm_w': jnp.ones((HV,), jnp.float32), 'Wo': jax.random.normal(ks[10], (HQ * HV, D), jnp.float32) * s(HQ * HV)}
        return inp
    _L0_attn_all = _L0_attn_setup()
    _L0_attn_in = {k: v for k, v in _L0_attn_all.items() if k in ('Wq', 'Wk', 'Wv', 'Wconv', 'Wa', 'Walpha', 'Wb', 'A_log', 'dt_bias', 'norm_w', 'Wo')}
    del _L0_attn_all

    def _L0_xattn_setup():
        import jax, jax.numpy as jnp
        import numpy as np
        B, LQ, LK = (8, 512, 512)
        QD, KD, VD = (256, 128, 128)
        key = jax.random.key(seed)
        ks = jax.random.split(key, 9)
        s = 0.02
        return {'query': jax.random.normal(ks[0], (B, LQ, QD), jnp.float32), 'key': jax.random.normal(ks[1], (B, LK, KD), jnp.float32), 'value': jax.random.normal(ks[2], (B, LK, VD), jnp.float32), 'Wq': jax.random.normal(ks[3], (QD, QD), jnp.float32) * s, 'bq': jnp.zeros((QD,), jnp.float32), 'Wk': jax.random.normal(ks[4], (KD, QD), jnp.float32) * s, 'bk': jnp.zeros((QD,), jnp.float32), 'Wv': jax.random.normal(ks[5], (VD, QD), jnp.float32) * s, 'bv': jnp.zeros((QD,), jnp.float32)}
    _L0_xattn_all = _L0_xattn_setup()
    _L0_xattn_in = {k: v for k, v in _L0_xattn_all.items() if k in ('Wq', 'bq', 'Wk', 'bk', 'Wv', 'bv')}
    del _L0_xattn_all

    def _L0_ffn_setup():
        import jax, jax.numpy as jnp
        import numpy as np
        B, S, D, F, E = (2, 512, 256, 1024, 8)
        LN_EPS = 1e-05

        def _layer_norm(x, gamma, beta):
            mu = jnp.mean(x, axis=-1, keepdims=True)
            var = jnp.mean(jnp.square(x - mu), axis=-1, keepdims=True)
            return (x - mu) * jax.lax.rsqrt(var + LN_EPS) * gamma + beta
        key = jax.random.key(seed)
        ks = jax.random.split(key, 8)

        def xavier(k, shape):
            fan_in, fan_out = (shape[-1], shape[-2])
            a = jnp.sqrt(6.0 / (fan_in + fan_out))
            return jax.random.uniform(k, shape, jnp.float32, -a, a)
        return {'tgt': jax.random.normal(ks[0], (B, S, D), jnp.float32), 'Wr': xavier(ks[1], (E, D)), 'br': jnp.zeros((E,), jnp.float32), 'W1': xavier(ks[2], (E, F, D)), 'b1': jnp.zeros((E, F), jnp.float32), 'W2': xavier(ks[3], (E, D, F)), 'b2': jnp.zeros((E, D), jnp.float32), 'gamma': jnp.ones((D,), jnp.float32), 'beta': jnp.zeros((D,), jnp.float32)}
    _L0_ffn_all = _L0_ffn_setup()
    _L0_ffn_in = {k: v for k, v in _L0_ffn_all.items() if k in ('Wr', 'br', 'W1', 'b1', 'W2', 'b2', 'gamma', 'beta')}
    del _L0_ffn_all

    def _L1_attn_setup():
        import jax, jax.numpy as jnp
        import numpy as np
        D = 256
        H = 16
        HD = D // H
        EPS = 1e-06

        def rms_norm(x, w):
            xf = x.astype(jnp.float32)
            rms = jnp.sqrt(jnp.mean(xf * xf, axis=-1, keepdims=True) + EPS)
            return (xf / rms * w.astype(jnp.float32)).astype(x.dtype)
        key = jax.random.key(seed)
        ks = jax.random.split(key, 6)
        B, S = (2, 512)
        x = jax.random.normal(ks[0], (B, S, D), dtype=jnp.float32)
        Wqkv = jax.random.normal(ks[1], (3 * D, D), dtype=jnp.float32) * (1.0 / np.sqrt(D))
        bqkv = jax.random.normal(ks[2], (3 * D,), dtype=jnp.float32) * 0.02
        Wproj = jax.random.normal(ks[3], (D, D), dtype=jnp.float32) * (1.0 / np.sqrt(D))
        bproj = jax.random.normal(ks[4], (D,), dtype=jnp.float32) * 0.02
        qn_w = jnp.ones((HD,), dtype=jnp.float32)
        kn_w = jnp.ones((HD,), dtype=jnp.float32)
        return {'x': x, 'Wqkv': Wqkv, 'bqkv': bqkv, 'Wproj': Wproj, 'bproj': bproj, 'qn_w': qn_w, 'kn_w': kn_w}
    _L1_attn_all = _L1_attn_setup()
    _L1_attn_in = {k: v for k, v in _L1_attn_all.items() if k in ('Wqkv', 'bqkv', 'Wproj', 'bproj', 'qn_w', 'kn_w')}
    del _L1_attn_all

    def _L1_xattn_setup():
        import jax, jax.numpy as jnp
        import numpy as np
        B, T, TC, C, CC, H = (2, 512, 128, 256, 128, 16)
        D = C // H

        def _heads(t):
            b, l, _ = t.shape
            return t.reshape(b, l, H, D).transpose(0, 2, 1, 3)
        key = jax.random.key(seed)
        ks = jax.random.split(key, 18)
        w = lambda k, i, o: jax.random.normal(k, (i, o), jnp.float32) / np.sqrt(i).astype(np.float32)
        return {'x': jax.random.normal(ks[0], (B, T, C), jnp.float32), 'cross_input': jax.random.normal(ks[1], (B, TC, CC), jnp.float32), 'Wk': w(ks[2], C, C), 'bk': jnp.zeros((C,), jnp.float32), 'Wq': w(ks[3], C, C), 'bq': jnp.zeros((C,), jnp.float32), 'Wv': w(ks[4], C, C), 'bv': jnp.zeros((C,), jnp.float32), 'Wck': w(ks[5], CC, C), 'bck': jnp.zeros((C,), jnp.float32), 'Wcq': w(ks[6], C, C), 'bcq': jnp.zeros((C,), jnp.float32), 'Wcv': w(ks[7], CC, C), 'bcv': jnp.zeros((C,), jnp.float32), 'Wp': w(ks[8], C, C), 'bp': jnp.zeros((C,), jnp.float32)}
    _L1_xattn_all = _L1_xattn_setup()
    _L1_xattn_in = {k: v for k, v in _L1_xattn_all.items() if k in ('Wk', 'bk', 'Wq', 'bq', 'Wv', 'bv', 'Wck', 'bck', 'Wcq', 'bcq', 'Wcv', 'bcv', 'Wp', 'bp')}
    del _L1_xattn_all

    def _L1_ffn_setup():
        import jax, jax.numpy as jnp
        import numpy as np

        def _ste(w, w_q):
            return w + jax.lax.stop_gradient(w_q - w)

        def quantize_w8_per(w, axis):
            amax = jnp.clip(jnp.max(jnp.abs(w), axis=axis, keepdims=True), 1e-08, None)
            scale = 127.0 / amax
            w_q = jnp.clip(jnp.round(w * scale), -128.0, 127.0) / scale
            return _ste(w, w_q)

        def quantize_a16(x):
            amax = jnp.clip(jnp.max(jnp.abs(x)), 1e-08, None)
            scale = 32767.0 / amax
            x_q = jnp.clip(jnp.round(x * scale), -32768.0, 32767.0) / scale
            return _ste(x, x_q)
        key = jax.random.key(seed)
        k1, k2, k3 = jax.random.split(key, 3)
        d_model, d_ff = (256, 1024)
        x = jax.random.normal(k1, (4, 512, d_model), dtype=jnp.float32)
        W_in = jax.random.normal(k2, (d_model, d_ff), dtype=jnp.float32) / np.sqrt(d_model)
        b_in = jnp.zeros((d_ff,), dtype=jnp.float32)
        W_out = jax.random.normal(k3, (d_ff, d_model), dtype=jnp.float32) / np.sqrt(d_ff)
        b_out = jnp.zeros((d_model,), dtype=jnp.float32)
        return {'x': x, 'W_in': W_in, 'b_in': b_in, 'W_out': W_out, 'b_out': b_out}
    _L1_ffn_all = _L1_ffn_setup()
    _L1_ffn_in = {k: v for k, v in _L1_ffn_all.items() if k in ('W_in', 'b_in', 'W_out', 'b_out')}
    del _L1_ffn_all
    return {'x': x, 'ctx_512': ctx_512, 'L0_attn_Wq': _L0_attn_in['Wq'], 'L0_attn_Wk': _L0_attn_in['Wk'], 'L0_attn_Wv': _L0_attn_in['Wv'], 'L0_attn_Wconv': _L0_attn_in['Wconv'], 'L0_attn_Wa': _L0_attn_in['Wa'], 'L0_attn_Walpha': _L0_attn_in['Walpha'], 'L0_attn_Wb': _L0_attn_in['Wb'], 'L0_attn_A_log': _L0_attn_in['A_log'], 'L0_attn_dt_bias': _L0_attn_in['dt_bias'], 'L0_attn_norm_w': _L0_attn_in['norm_w'], 'L0_attn_Wo': _L0_attn_in['Wo'], 'L0_xattn_Wq': _L0_xattn_in['Wq'], 'L0_xattn_bq': _L0_xattn_in['bq'], 'L0_xattn_Wk': _L0_xattn_in['Wk'], 'L0_xattn_bk': _L0_xattn_in['bk'], 'L0_xattn_Wv': _L0_xattn_in['Wv'], 'L0_xattn_bv': _L0_xattn_in['bv'], 'L0_ffn_Wr': _L0_ffn_in['Wr'], 'L0_ffn_br': _L0_ffn_in['br'], 'L0_ffn_W1': _L0_ffn_in['W1'], 'L0_ffn_b1': _L0_ffn_in['b1'], 'L0_ffn_W2': _L0_ffn_in['W2'], 'L0_ffn_b2': _L0_ffn_in['b2'], 'L0_ffn_gamma': _L0_ffn_in['gamma'], 'L0_ffn_beta': _L0_ffn_in['beta'], 'L1_attn_Wqkv': _L1_attn_in['Wqkv'], 'L1_attn_bqkv': _L1_attn_in['bqkv'], 'L1_attn_Wproj': _L1_attn_in['Wproj'], 'L1_attn_bproj': _L1_attn_in['bproj'], 'L1_attn_qn_w': _L1_attn_in['qn_w'], 'L1_attn_kn_w': _L1_attn_in['kn_w'], 'L1_xattn_Wk': _L1_xattn_in['Wk'], 'L1_xattn_bk': _L1_xattn_in['bk'], 'L1_xattn_Wq': _L1_xattn_in['Wq'], 'L1_xattn_bq': _L1_xattn_in['bq'], 'L1_xattn_Wv': _L1_xattn_in['Wv'], 'L1_xattn_bv': _L1_xattn_in['bv'], 'L1_xattn_Wck': _L1_xattn_in['Wck'], 'L1_xattn_bck': _L1_xattn_in['bck'], 'L1_xattn_Wcq': _L1_xattn_in['Wcq'], 'L1_xattn_bcq': _L1_xattn_in['bcq'], 'L1_xattn_Wcv': _L1_xattn_in['Wcv'], 'L1_xattn_bcv': _L1_xattn_in['bcv'], 'L1_xattn_Wp': _L1_xattn_in['Wp'], 'L1_xattn_bp': _L1_xattn_in['bp'], 'L1_ffn_W_in': _L1_ffn_in['W_in'], 'L1_ffn_b_in': _L1_ffn_in['b_in'], 'L1_ffn_W_out': _L1_ffn_in['W_out'], 'L1_ffn_b_out': _L1_ffn_in['b_out']}

def reference(x, ctx_512, L0_attn_Wq, L0_attn_Wk, L0_attn_Wv, L0_attn_Wconv, L0_attn_Wa, L0_attn_Walpha, L0_attn_Wb, L0_attn_A_log, L0_attn_dt_bias, L0_attn_norm_w, L0_attn_Wo, L0_xattn_Wq, L0_xattn_bq, L0_xattn_Wk, L0_xattn_bk, L0_xattn_Wv, L0_xattn_bv, L0_ffn_Wr, L0_ffn_br, L0_ffn_W1, L0_ffn_b1, L0_ffn_W2, L0_ffn_b2, L0_ffn_gamma, L0_ffn_beta, L1_attn_Wqkv, L1_attn_bqkv, L1_attn_Wproj, L1_attn_bproj, L1_attn_qn_w, L1_attn_kn_w, L1_xattn_Wk, L1_xattn_bk, L1_xattn_Wq, L1_xattn_bq, L1_xattn_Wv, L1_xattn_bv, L1_xattn_Wck, L1_xattn_bck, L1_xattn_Wcq, L1_xattn_bcq, L1_xattn_Wcv, L1_xattn_bcv, L1_xattn_Wp, L1_xattn_bp, L1_ffn_W_in, L1_ffn_b_in, L1_ffn_W_out, L1_ffn_b_out):
    import jax
    import jax.numpy as jnp

    def _L0_attn_ref(x, Wq, Wk, Wv, Wconv, Wa, Walpha, Wb, A_log, dt_bias, norm_w, Wo):
        import jax, jax.numpy as jnp
        import numpy as np
        B, T, D = (1, 256, 256)
        HQ, HKV, HK, HV = (16, 4, 64, 64)
        KW = 4
        N_CHEB = 2
        CHEB_DAMP = 0.25
        EPS = 1e-06

        def _gka_core(x, Wq, Wk, Wv, Wconv, Wa, Walpha, Wb, A_log, dt_bias, norm_w, Wo):
            Bx, Tx, _ = x.shape
            qkv = jnp.concatenate([x @ Wq, x @ Wk, x @ Wv], axis=-1)
            pad = jnp.pad(qkv, ((0, 0), (KW - 1, 0), (0, 0)))
            conv = sum((pad[:, i:i + Tx, :] * Wconv[:, i] for i in range(KW)))
            qkv = jax.nn.silu(conv)
            q, k, v = jnp.split(qkv, [HQ * HK, HQ * HK + HKV * HK], axis=-1)
            q = q.reshape(Bx, Tx, HQ, HK)
            k = k.reshape(Bx, Tx, HKV, HK)
            v = v.reshape(Bx, Tx, HKV, HV)
            g = -jnp.exp(A_log) * jax.nn.softplus(x @ Wa + dt_bias)
            alpha = jax.nn.sigmoid(x @ Walpha)
            beta = jax.nn.sigmoid(x @ Wb)
            v = v * beta[..., None]
            k = k / (jnp.linalg.norm(k, axis=-1, keepdims=True) + EPS)
            q = q * HK ** (-0.5)
            rep = HQ // HKV
            k = jnp.repeat(k, rep, axis=2)
            v = jnp.repeat(v, rep, axis=2)

            def step(carry, inp):
                Hkk, Hkv = carry
                qt, kt, vt, gt = inp
                d = jnp.exp(gt)[..., None, None]
                Hkk = d * Hkk + kt[..., :, None] * kt[..., None, :]
                Hkv = d * Hkv + kt[..., :, None] * vt[..., None, :]
                xq = qt
                for _ in range(N_CHEB):
                    xq = qt - CHEB_DAMP * jnp.einsum('bhk,bhkl->bhl', xq, Hkk)
                ot = jnp.einsum('bhk,bhkv->bhv', xq, Hkv)
                return ((Hkk, Hkv), ot)
            tm = lambda a: jnp.moveaxis(a, 1, 0)
            init = (jnp.zeros((Bx, HQ, HK, HK), jnp.float32), jnp.zeros((Bx, HQ, HK, HV), jnp.float32))
            _, o = jax.lax.scan(step, init, (tm(q), tm(k), tm(v), tm(g)))
            o = jnp.moveaxis(o, 0, 1)
            o = o * alpha[..., None]
            o = o * jax.lax.rsqrt(jnp.mean(o * o, axis=-1, keepdims=True) + EPS) * norm_w
            return o.reshape(Bx, Tx, HQ * HV) @ Wo
        return _gka_core(x, Wq, Wk, Wv, Wconv, Wa, Walpha, Wb, A_log, dt_bias, norm_w, Wo)

    def _L0_xattn_ref(query, key, value, Wq, bq, Wk, bk, Wv, bv):
        import jax, jax.numpy as jnp
        import numpy as np
        B, LQ, LK = (8, 512, 512)
        QD, KD, VD = (256, 128, 128)
        q = jnp.einsum('bld,de->ble', query, Wq) + bq
        k = jnp.einsum('bld,de->ble', key, Wk) + bk
        v = jnp.einsum('bld,de->ble', value, Wv) + bv
        scores = jnp.einsum('bqe,bke->bqk', q, k)
        attn = jax.nn.softmax(scores, axis=-1)
        out = jnp.einsum('bqk,bke->bqe', attn, v)
        return out

    def _L0_ffn_ref(tgt, Wr, br, W1, b1, W2, b2, gamma, beta):
        import jax, jax.numpy as jnp
        import numpy as np
        B, S, D, F, E = (2, 512, 256, 1024, 8)
        LN_EPS = 1e-05

        def _layer_norm(x, gamma, beta):
            mu = jnp.mean(x, axis=-1, keepdims=True)
            var = jnp.mean(jnp.square(x - mu), axis=-1, keepdims=True)
            return (x - mu) * jax.lax.rsqrt(var + LN_EPS) * gamma + beta
        logits = jnp.einsum('bsd,ed->bse', tgt, Wr) + br
        top_v, top_i = jax.lax.top_k(logits, 2)
        top_w = jax.nn.softmax(top_v, axis=-1)
        n_exp = logits.shape[-1]
        router_w = jnp.sum(jax.nn.one_hot(top_i, n_exp, dtype=top_w.dtype) * top_w[..., None], axis=-2)
        h = jnp.einsum('bsd,efd->bsef', tgt, W1) + b1
        h = jax.nn.relu(h)
        o = jnp.einsum('bsef,edf->bsed', h, W2) + b2
        tgt2 = jnp.einsum('bsed,bse->bsd', o, router_w)
        return _layer_norm(tgt + tgt2, gamma, beta)

    def _L1_attn_ref(x, Wqkv, bqkv, Wproj, bproj, qn_w, kn_w):
        import jax, jax.numpy as jnp
        import numpy as np
        D = 256
        H = 16
        HD = D // H
        EPS = 1e-06

        def rms_norm(x, w):
            xf = x.astype(jnp.float32)
            rms = jnp.sqrt(jnp.mean(xf * xf, axis=-1, keepdims=True) + EPS)
            return (xf / rms * w.astype(jnp.float32)).astype(x.dtype)
        B, S, _ = x.shape
        qkv = x @ Wqkv.T + bqkv
        qkv = qkv.reshape(B, S, 3, H, HD)
        q, k, v = (qkv[:, :, 0], qkv[:, :, 1], qkv[:, :, 2])
        q = rms_norm(q, qn_w)
        k = rms_norm(k, kn_w)
        q = q.transpose(0, 2, 1, 3)
        k = k.transpose(0, 2, 1, 3)
        v = v.transpose(0, 2, 1, 3)
        scale = 1.0 / np.sqrt(HD)
        scores = jnp.einsum('bhsd,bhtd->bhst', q, k) * scale
        attn = jax.nn.softmax(scores, axis=-1)
        out = jnp.einsum('bhst,bhtd->bhsd', attn, v)
        out = out.transpose(0, 2, 1, 3).reshape(B, S, D)
        return out @ Wproj.T + bproj

    def _L1_xattn_ref(x, cross_input, Wk, bk, Wq, bq, Wv, bv, Wck, bck, Wcq, bcq, Wcv, bcv, Wp, bp):
        import jax, jax.numpy as jnp
        import numpy as np
        B, T, TC, C, CC, H = (2, 512, 128, 256, 128, 16)
        D = C // H

        def _heads(t):
            b, l, _ = t.shape
            return t.reshape(b, l, H, D).transpose(0, 2, 1, 3)
        scale = np.float32(1.0 / np.sqrt(D))
        q = _heads(x @ Wq + bq)
        k = _heads(x @ Wk + bk)
        v = _heads(x @ Wv + bv)
        att = jnp.einsum('bhqd,bhkd->bhqk', q, k) * scale
        causal = jnp.tril(jnp.ones((T, T), bool))
        att = jnp.where(causal[None, None], att, -jnp.inf)
        y = jnp.einsum('bhqk,bhkd->bhqd', jax.nn.softmax(att, axis=-1), v)
        qc = _heads(x @ Wcq + bcq)
        kc = _heads(cross_input @ Wck + bck)
        vc = _heads(cross_input @ Wcv + bcv)
        attc = jnp.einsum('bhqd,bhkd->bhqk', qc, kc) * scale
        y = y + jnp.einsum('bhqk,bhkd->bhqd', jax.nn.softmax(attc, axis=-1), vc)
        y = y.transpose(0, 2, 1, 3).reshape(x.shape[0], T, C)
        return y @ Wp + bp

    def _L1_ffn_ref(x, W_in, b_in, W_out, b_out):
        import jax, jax.numpy as jnp
        import numpy as np

        def _ste(w, w_q):
            return w + jax.lax.stop_gradient(w_q - w)

        def quantize_w8_per(w, axis):
            amax = jnp.clip(jnp.max(jnp.abs(w), axis=axis, keepdims=True), 1e-08, None)
            scale = 127.0 / amax
            w_q = jnp.clip(jnp.round(w * scale), -128.0, 127.0) / scale
            return _ste(w, w_q)

        def quantize_a16(x):
            amax = jnp.clip(jnp.max(jnp.abs(x)), 1e-08, None)
            scale = 32767.0 / amax
            x_q = jnp.clip(jnp.round(x * scale), -32768.0, 32767.0) / scale
            return _ste(x, x_q)
        W_in_sim = quantize_w8_per(W_in, axis=0)
        W_out_sim = quantize_w8_per(W_out, axis=1)
        x_sim = quantize_a16(x)
        hidden = jax.nn.gelu(x_sim @ W_in_sim + b_in, approximate=False)
        hidden_sim = quantize_a16(hidden)
        out = hidden_sim @ W_out_sim + b_out
        return out
    x = x + _L0_attn_ref(_layernorm(x, axis=-1), L0_attn_Wq, L0_attn_Wk, L0_attn_Wv, L0_attn_Wconv, L0_attn_Wa, L0_attn_Walpha, L0_attn_Wb, L0_attn_A_log, L0_attn_dt_bias, L0_attn_norm_w, L0_attn_Wo)
    x = x + _L0_xattn_ref(_layernorm(x, axis=-1), ctx_512, ctx_512, L0_xattn_Wq, L0_xattn_bq, L0_xattn_Wk, L0_xattn_bk, L0_xattn_Wv, L0_xattn_bv)
    x = x + _L0_ffn_ref(_layernorm(x, axis=-1), L0_ffn_Wr, L0_ffn_br, L0_ffn_W1, L0_ffn_b1, L0_ffn_W2, L0_ffn_b2, L0_ffn_gamma, L0_ffn_beta)
    x = x + _L1_attn_ref(_layernorm(x, axis=-1), L1_attn_Wqkv, L1_attn_bqkv, L1_attn_Wproj, L1_attn_bproj, L1_attn_qn_w, L1_attn_kn_w)
    x = x + _L1_xattn_ref(_layernorm(x, axis=-1), ctx_512, L1_xattn_Wk, L1_xattn_bk, L1_xattn_Wq, L1_xattn_bq, L1_xattn_Wv, L1_xattn_bv, L1_xattn_Wck, L1_xattn_bck, L1_xattn_Wcq, L1_xattn_bcq, L1_xattn_Wcv, L1_xattn_bcv, L1_xattn_Wp, L1_xattn_bp)
    x = x + _L1_ffn_ref(_layernorm(x, axis=-1), L1_ffn_W_in, L1_ffn_b_in, L1_ffn_W_out, L1_ffn_b_out)
    return x

_drawn_inputs = setup_inputs


def setup_inputs(seed=0):
    import zlib

    import numpy as np

    out = dict(_drawn_inputs(seed))
    spreads = {'L0_attn_norm_w': (1.0, 0.2),
     'L0_xattn_bq': (0.0, 0.283),
     'L0_xattn_bk': (0.0, 0.8),
     'L0_xattn_bv': (0.0, 0.1),
     'L0_ffn_br': (0.0, 0.1),
     'L0_ffn_b1': (0.0, 0.1),
     'L0_ffn_b2': (0.0, 0.1),
     'L0_ffn_gamma': (1.0, 0.2),
     'L0_ffn_beta': (0.0, 0.1),
     'L1_attn_qn_w': (1.0, 0.6),
     'L1_attn_kn_w': (1.0, 0.6),
     'L1_xattn_bk': (0.0, 0.8),
     'L1_xattn_bq': (0.0, 0.8),
     'L1_xattn_bv': (0.0, 0.1),
     'L1_xattn_bck': (0.0, 0.8),
     'L1_xattn_bcq': (0.0, 0.755),
     'L1_xattn_bcv': (0.0, 0.1),
     'L1_xattn_bp': (0.0, 0.1),
     'L1_ffn_b_in': (0.0, 0.283),
     'L1_ffn_b_out': (0.0, 0.1)}
    factors = {'L1_attn_bqkv': 4.537, 'L1_attn_bproj': 5.809}
    for name, (base, spread) in spreads.items():
        noise = np.random.default_rng([zlib.crc32(name.encode()), seed]).standard_normal(out[name].shape)
        drawn = base * np.exp(spread * noise) if base else spread * noise
        out[name] = jnp.asarray(drawn.astype(out[name].dtype))
    for name, factor in factors.items():
        out[name] = (out[name] * factor).astype(out[name].dtype)
    return out
```

```python
from contextlib import ExitStack

import numpy as np
import concourse.bass as bass
from concourse import mybir

F32 = mybir.dt.float32
BF16 = mybir.dt.bfloat16
ALU = mybir.AluOpType
ACT = mybir.ActivationFunctionType
AX = mybir.AxisListType.X
RMAX = bass.bass_isa.ReduceOp.max

P = 128
B, T, D = 4, 512, 256
TT = T // P
NT = B * TT
KD = D // P
LN_EPS = 1e-5
EPS = 1e-6
EXP_LN = "natural_log_exp_and_others"
NEG = -1e30

HQ, HKV, HK, KW = 16, 4, 64, 4
G4 = HQ // HKV
CW = G4 * HK + 3 * HK
SMALL = 2 * G4 + 1
DAMP = 0.25

LC, CD = 1601, 128
CT = -(-LC // P)
CLAST = LC - (CT - 1) * P

H, HD, SH = 16, 16, 32
NG = 4
SW = 4 * SH

E, F = 8, 1024
FT = F // P


class Chain:

    def __init__(self, eng, sem, per):
        self.eng, self.sem, self.per, self.n, self.k = eng, sem, per, 0, 0

    def begin(self, n):
        self.n, self.k = n, 0

    def done(self, ins):
        ins.then_inc(self.sem, 1)
        self.k += 1

    def wait(self):
        self.eng.wait_ge(self.sem, self.n * self.per + self.k)

    def link(self, ins):
        self.done(ins)
        self.wait()

    def end(self):
        assert self.k == self.per, (self.sem, self.k)


class Core:
    pass


def bc(ap, shape):
    return ap.to_broadcast(shape)


def tools(nc, ctx, stage):
    def sb(name, shape, dt=F32):
        return ctx.enter_context(nc.sbuf_tensor(f"{stage}_{name}", shape, dt))

    def ps(name, shape, dt=F32):
        return ctx.enter_context(nc.psum_tensor(f"{stage}_{name}", shape, dt))

    def sem(name):
        return nc.alloc_semaphore(f"{stage}_{name}")

    return sb, ps, sem


def constants(nc, k, x_in, ctx):
    sb, ps, sem = tools(nc, ctx, "c")
    k.x = sb("x", [P, NT, D])
    k.ident = sb("ident", [P, P])
    k.identb = sb("identb", [P, P], BF16)
    k.mask_kq = sb("mask_kq", [P, P], BF16)
    k.mask_qk = sb("mask_qk", [P, P], BF16)
    k.tri = sb("tri", [P, P])
    k.ln_eps = sb("ln_eps", [P, 1])
    k.eps = sb("eps", [P, 1])
    k.tiny = sb("tiny", [P, 1])
    loaded, filled, made = sem("loaded"), sem("filled"), sem("made")
    with nc.Block() as block:
        @block.sync
        def _(sp):
            sp.dma_start(k.x[:], x_in.rearrange("b (t p) d -> p (b t) d", p=P)).then_inc(loaded, 16)
            sp.wait_ge(loaded, 16)

        @block.gpsimd
        def _(pool):
            for tile, value in ((k.ident, 0.0), (k.identb, 0.0), (k.mask_kq, 0.0), (k.mask_qk, 0.0), (k.tri, 1.0),
                                (k.ln_eps, LN_EPS), (k.eps, EPS), (k.tiny, 1e-18)):
                pool.memset(tile[:], value).then_inc(filled, 1)
            pool.wait_ge(filled, 8)
            for tile in (k.ident, k.identb):
                pool.affine_select(out=tile[:], in_=tile[:], compare_op=ALU.not_equal, fill=1.0, base=0,
                                   pattern=[[-1, P]], channel_multiplier=1).then_inc(made, 1)
            for tile, fill in ((k.mask_kq, NEG), (k.tri, 0.0)):
                pool.affine_select(out=tile[:], in_=tile[:], compare_op=ALU.is_ge, fill=fill, base=0,
                                   pattern=[[1, P]], channel_multiplier=-1).then_inc(made, 1)
            pool.affine_select(out=k.mask_qk[:], in_=k.mask_qk[:], compare_op=ALU.is_ge, fill=NEG, base=0,
                               pattern=[[-1, P]], channel_multiplier=1).then_inc(made, 1)
            pool.wait_ge(made, 5)


class Norm:

    def __init__(self, nc, k, sb, sem):
        self.nc, self.k = nc, k
        self.st = sb("ln_st", [P, TT, 6])
        self.mv = sb("ln_mv", [P, TT, 2])
        self.spare = sb("ln_spare", [P, 1])
        self.lnv = sb("ln_lnv", [P, TT])
        self.rstd = sb("ln_rstd", [P, TT])
        self.xn = sb("ln_xn", [P, TT, D])
        self.xT = sb("ln_xT", [P, KD, T])
        self.s_bn, self.s_mv, self.s_ln, self.s_rstd = (sem(f"ln_{x}") for x in ("bn", "mv", "log", "rstd"))
        self.s_xn, self.s_turned, self.s_xT = (sem(f"ln_{x}") for x in ("xn", "turned", "xT"))

    def stats(self, dve, b, n):
        for t in range(TT):
            dve.bn_stats(self.st[:, t, :], self.k.x[:, b * TT + t, :]).then_inc(self.s_bn, 1)
        dve.wait_ge(self.s_bn, n * TT + TT)
        dve.memset(self.spare[:], 0.0)
        for t in range(TT):
            dve.bn_aggr(self.mv[:, t, :], self.st[:, t, :]).then_inc(self.s_mv, 1)

    def rstd_of(self, act, n):
        act.wait_ge(self.s_mv, n * TT + TT)
        act.activation(self.lnv[:], self.mv[:, :, 1], ACT.Ln, bias=self.k.ln_eps[:]).then_inc(self.s_ln, 1)
        act.wait_ge(self.s_ln, n + 1)
        act.activation(self.rstd[:], self.lnv[:], ACT.Exp, scale=-0.5).then_inc(self.s_rstd, 1)

    def scale(self, dve, b, n):
        dve.wait_ge(self.s_rstd, n + 1)
        for t in range(TT):
            dve.tensor_scalar(self.xn[:, t, :], self.k.x[:, b * TT + t, :], self.mv[:, t, 0:1],
                              self.rstd[:, t:t + 1], ALU.subtract, ALU.mult).then_inc(self.s_xn, 1)

    def turn(self, pe, n, two_banks):
        pe.wait_ge(self.s_xn, n * TT + TT)
        for h in range(KD):
            for t in range(TT):
                pe.transpose(two_banks[:, h, t * P:(t + 1) * P], self.xn[:, t, h * P:(h + 1) * P],
                             self.k.ident[:]).then_inc(self.s_turned, 1)

    def keep(self, dve, n, two_banks):
        dve.wait_ge(self.s_turned, n * TT * KD + TT * KD)
        dve.tensor_copy(self.xT[:], two_banks[:]).then_inc(self.s_xT, 1)


def gated_attention(nc, k, d):
    ctx = ExitStack()
    with ctx:
        sb, ps, sem = tools(nc, ctx, "ga")
        ln = Norm(nc, k, sb, sem)
        w = sb("w", [P, KD, CW + SMALL])
        taps = sb("taps", [P, 4, KW])
        rows = sb("rows", [P, 2 * G4])
        wo = sb("wo", [P, 2, D])
        wos = sb("wos", [P, 2, D])
        normw = sb("normw", [P, 1])
        cv = sb("cv", [P, 4, T])
        small = sb("small", [P, TT, SMALL])
        z, az, e1, l1, sp_ = (sb(x, [P, TT, G4]) for x in ("z", "az", "e1", "l1", "sp"))
        ea = sb("ea", [P, G4])
        eab = sb("eab", [P, TT, G4 + 1])
        den = sb("den", [P, TT, G4 + 1])
        gates = sb("gates", [P, TT, G4 + 1])
        alpha = sb("alpha", [P, TT, G4])
        g = sb("g", [P, TT, G4])
        gd = sb("gd", [P, TT, G4, HK])
        negG = sb("negG", [P, TT, G4])
        X0 = sb("X0", [P, TT, 2, P])
        X1 = sb("X1", [P, TT, 2, P])
        Xs = sb("Xs", [P, TT, 2, P])
        kT = sb("kT", [P, T])
        vT = sb("vT", [HK, T])
        sq = sb("sq", [P, G4 * TT * HK])
        ssk, lnk, nk, nke, rk = (sb(x, [P, TT]) for x in ("ssk", "lnk", "nk", "nke", "rk"))
        KKV = sb("KKV", [P, TT, 3 * HK])
        kTn = sb("kTn", [P, TT, P])
        Ed = sb("Ed", [P, TT, 2, P])
        Dm = sb("Dm", [P, 2, 2, 2, 2, P])
        KVw = sb("KVw", [P, TT - 1, 2, 2, 2 * HK])
        Hs = sb("Hs", [P, TT - 1, 2, 2 * HK])
        Wm = sb("Wm", [P, 2, 2, 2, 2, P])
        o = sb("o", [P, TT, G4, HK])
        on = sb("on", [P, TT, G4, HK])
        sso, lno, ro = (sb(x, [P, TT * G4]) for x in ("sso", "lno", "ro"))
        oT = sb("oT", [P, 2, TT, P])
        bank = ps("bank", [P, 8, 512])

        s_w, s_t, s_r, s_wo, s_nw = (sem(x) for x in ("w", "taps", "rows", "wo", "normw"))
        s_proj, s_small, s_conv, s_smallc, s_az, s_es, s_l1 = (
            sem(x) for x in ("proj", "small", "conv", "smallc", "az", "es", "l1"))
        s_g, s_G, s_Gc, s_E, s_Ee, s_D, s_De = (sem(x) for x in ("g", "G", "Gc", "E", "Ee", "D", "De"))
        s_silu, s_kvt, s_ssk, s_nk, s_kn, s_v, s_kT, s_kTc = (
            sem(x) for x in ("silu", "kvt", "ssk", "nk", "kn", "v", "kT", "kTc"))
        s_KVw, s_st, s_H, s_W, s_Wm, s_Y, s_X, s_Xs = (
            sem(x) for x in ("KVw", "st", "H", "W", "Wm", "Y", "X", "Xs"))
        s_O, s_o, s_sq, s_ss, s_ro, s_on, s_oT, s_oTc, s_out, s_x = (
            sem(x) for x in ("O", "o", "sq", "ss", "ro", "on", "oT", "oTc", "out", "x"))
        s_gd, s_wos, c_dve, c_act = sem("gd"), sem("wos"), sem("c_dve"), sem("c_act")

        turned = bank[:, 6:8, :]
        kps = bank[:, 4, :].rearrange("p (c f) -> p c f", c=TT)
        vps = bank[:, 5, 0:TT * HK].rearrange("p (c f) -> p c f", c=TT)
        Eps = bank[:, 6:8, :].rearrange("p a (c i t) -> p (a c) i t", c=2, i=2)
        st = bank[:, 6:8, :].rearrange("p a (c i f) -> p (a c) i f", c=2, i=2)

        def pair(cc):
            return bank[:, 2 * cc:2 * cc + 2, :].rearrange("p q (c i t) -> p q c i t", c=2, i=2)

        def Y(cc):
            return bank[:, 4 + cc, :].rearrange("p (c i t) -> p c i t", c=2, i=2)

        O = bank[:, 6:8, :].rearrange("p q (c i f) -> p q c i f", c=TT, i=2)

        with nc.Block() as block:
            @block.sync
            def _(sp):
                sp.dma_start(normw[:], d["ga_normw"]).then_inc(s_nw, 16)
                with sp.Fori(0, B) as b:
                    with sp.Fori(0, HKV) as j:
                        n = b * HKV + j
                        sp.wait_ge(s_small, n)
                        sp.dma_start(w[:], d["ga_w"][j].rearrange("(h p) n -> p h n", p=P)).then_inc(s_w, 16)
                        sp.wait_ge(s_conv, n * 4)
                        sp.dma_start(taps[:], d["ga_taps"][j]).then_inc(s_t, 16)
                        sp.wait_ge(s_g, n)
                        sp.dma_start(rows[:], d["ga_rows"][j]).then_inc(s_r, 16)
                        sp.wait_ge(s_wos, n)
                        sp.dma_start(wo[:], d["ga_wo"][j].rearrange("(h p) n -> p h n", p=P)).then_inc(s_wo, 16)

            @block.tensor
            def _(pe):
                with pe.Fori(0, B) as b:
                    pe.wait_ge(s_x, b * HKV)
                    ln.turn(pe, b, turned)
                    with pe.Fori(0, HKV) as j:
                        n = b * HKV + j
                        pe.wait_ge(ln.s_xT, b + 1)
                        pe.wait_ge(s_w, n * 16 + 16)
                        pe.wait_ge(s_x, n)
                        for m in (2, 3, 0, 1):
                            M = P if m < 3 else HK
                            for h in range(KD):
                                mm = pe.matmul(bank[0:M, m, :], w[:, h, m * P:m * P + M], ln.xT[:, h, :],
                                               start=h == 0, stop=h == KD - 1)
                            mm.then_inc(s_proj, 1)
                        for t in range(TT):
                            for h in range(KD):
                                mm = pe.matmul(bank[:, 4, t * 16:t * 16 + SMALL], ln.xT[:, h, t * P:(t + 1) * P],
                                               w[:, h, CW:], start=h == 0, stop=h == KD - 1)
                        mm.then_inc(s_small, 1)
                        pe.wait_ge(s_silu, n * 4 + 2)
                        pe.wait_ge(s_smallc, n + 1)
                        for c in range(TT):
                            pe.transpose(kps[:, c, :], kT[:, c * P:(c + 1) * P], k.ident[:]).then_inc(s_kvt, 1)
                        for c in range(TT):
                            pe.transpose(vps[:, c, :], vT[:, c * P:(c + 1) * P], k.ident[0:HK, 0:HK])\
                              .then_inc(s_kvt, 1)
                        pe.wait_ge(s_g, n + 1)
                        pe.wait_ge(s_silu, n * 4 + 4)
                        pe.wait_ge(s_conv, n * 4 + 4)
                        pe.matmul(bank[:, 3, 0:TT * G4], k.tri[:], g[:].rearrange("p c h -> p (c h)"),
                                  start=True, stop=True).then_inc(s_G, 1)
                        pe.wait_ge(s_gd, n + 1)
                        for c in range(TT):
                            for i in range(2):
                                pe.matmul(Eps[:, c, i, :], gd[:, c, 2 * i:2 * i + 2, :].rearrange("p a f -> p (a f)"),
                                          k.tri[:], start=True, stop=True).then_inc(s_E, 1)
                        for cc in range(2):
                            if cc == 1:
                                pe.wait_ge(s_Gc, n + 1)
                            for q in range(2):
                                pe.matmul(bank[:, 2 * cc + q, :], k.identb[:],
                                          bc(k.mask_kq[:].unsqueeze(1), [P, 4, P]), start=True, stop=False)
                                for c in range(2):
                                    for i in range(2):
                                        mm = pe.matmul(pair(cc)[:, q, c, i, :],
                                                       bc(g[:, 2 * cc + c, 2 * i + q:2 * i + q + 1], [P, P]),
                                                       k.tri[:], start=False, stop=c == 1 and i == 1)
                            mm.then_inc(s_D, 1)
                        pe.wait_ge(s_kn, n + 1)
                        for c in range(TT):
                            pe.transpose(kps[:, c, :], KKV[:, c, 0:P], k.ident[:]).then_inc(s_kT, 1)
                        pe.wait_ge(s_Ee, n + 1)
                        for c in range(TT - 1):
                            pe.wait_ge(s_KVw, n * (TT - 1) + c + 1)
                            for q in range(2):
                                mm = pe.matmul(st[q * HK:(q + 1) * HK, c], KKV[:, c, 0:HK],
                                               KVw[:, c, q], start=True, stop=True)
                        mm.then_inc(s_st, 1)
                        pe.wait_ge(s_kTc, n + 1)
                        pe.wait_ge(s_De, n * 2 + 2)
                        for r in range(3):
                            X = X0 if r == 0 else X1
                            for cc in range(2):
                                if r:
                                    pe.wait_ge(s_X, n * 4 + 2 * (r - 1) + cc + 1)
                                for c in range(2 * cc, 2 * cc + 2):
                                    for q in range(2):
                                        part = slice(q * HK, (q + 1) * HK)
                                        mm = pe.matmul(pair(cc)[:, q, c % 2], kTn[part, c, :], X[part, c],
                                                       start=True, stop=True)
                                mm.then_inc(s_W, 1)
                            for cc in range(2):
                                pe.wait_ge(s_Wm, n * 6 + 2 * r + cc + 1)
                                if cc == 0:
                                    pe.wait_ge(s_H, n + 1)
                                    pe.wait_ge(s_Xs, n * 6 + 2 * r + 1)
                                else:
                                    pe.wait_ge(s_Xs, n * 6 + 2 * r + 2)
                                for c in range(2 * cc, 2 * cc + 2):
                                    for q in range(2):
                                        part = slice(q * HK, (q + 1) * HK)
                                        if r < 2:
                                            mm = pe.matmul(Y(cc)[part, c % 2], KKV[:, c, 0:HK],
                                                           Wm[:, cc, q, c % 2], start=True, stop=c == 0)
                                            for i in range(2 if c else 0):
                                                mm = pe.matmul(Y(cc)[part, c % 2, i, :], Hs[part, c - 1, i, 0:HK],
                                                               Xs[part, c, i, :], start=False, stop=i == 1)
                                        else:
                                            for i in range(2):
                                                mm = pe.matmul(O[:, q, c, i, :], Wm[:, cc, q, c % 2, i, :],
                                                               KKV[:, c, P:], start=True, stop=c == 0)
                                                if c:
                                                    mm = pe.matmul(O[:, q, c, i, :], Xs[part, c, i, :],
                                                                   Hs[part, c - 1, i, HK:], start=False, stop=True)
                                mm.then_inc(s_Y if r < 2 else s_O, 1)
                        pe.wait_ge(s_on, n + 1)
                        for h in range(2):
                            for c in range(TT):
                                pe.transpose(bank[:, h, c * P:(c + 1) * P],
                                             on[:, c, 2 * h:2 * h + 2, :].rearrange("p a f -> p (a f)"),
                                             k.ident[:]).then_inc(s_oT, 1)
                        pe.wait_ge(s_oTc, n + 1)
                        pe.wait_ge(s_wos, n + 1)
                        for c in range(TT):
                            for h in range(2):
                                mm = pe.matmul(bank[:, 2 + c // 2, (c % 2) * D:(c % 2 + 1) * D], oT[:, h, c, :],
                                               wos[:, h, :], start=h == 0, stop=h == 1)
                        mm.then_inc(s_out, 1)

            @block.vector
            def _(dve):
                own = Chain(dve, c_dve, 11)
                dve.wait_ge(s_nw, 16)
                with dve.Fori(0, B) as b:
                    dve.wait_ge(s_x, b * HKV)
                    ln.stats(dve, b, b)
                    ln.scale(dve, b, b)
                    ln.keep(dve, b, turned)
                    with dve.Fori(0, HKV) as j:
                        n = b * HKV + j
                        own.begin(n)
                        dve.wait_ge(s_t, n * 16 + 16)
                        order = (2, 3, 0, 1)
                        for at, m in enumerate(order):
                            M = P if m < 3 else HK
                            dve.wait_ge(s_proj, n * 4 + at + 1)
                            ins = dve.tensor_scalar(cv[0:M, m, :], bank[0:M, m, :], taps[0:M, m, KW - 1:KW], None,
                                                    ALU.mult)
                            if at == 3:
                                own.link(ins)
                        for lag in range(1, KW):
                            for at, m in enumerate(order):
                                M = P if m < 3 else HK
                                ins = dve.scalar_tensor_tensor(
                                    cv[0:M, m, lag:], bank[0:M, m, 0:T - lag], taps[0:M, m, KW - 1 - lag:KW - lag],
                                    cv[0:M, m, lag:], ALU.mult, ALU.add)
                                if lag == KW - 1:
                                    ins.then_inc(s_conv, 1)
                                elif at == 3:
                                    own.link(ins)
                        dve.wait_ge(s_small, n + 1)
                        dve.tensor_copy(small[:], bank[:, 4, 0:TT * 16].rearrange("p (t s) -> p t s", t=TT)
                                        [:, :, 0:SMALL]).then_inc(s_smallc, 1)
                        dve.wait_ge(s_smallc, n + 1)
                        dve.wait_ge(s_r, n * 16 + 16)
                        own.link(dve.tensor_tensor(z[:], small[:, :, 0:G4],
                                                   bc(rows[:, G4:].unsqueeze(1), [P, TT, G4]), ALU.add))
                        dve.scalar_tensor_tensor(az[:], z[:], -1.0, z[:], ALU.mult, ALU.max).then_inc(s_az, 1)
                        dve.wait_ge(s_es, n + 1)
                        own.link(dve.tensor_scalar(den[:], eab[:], 1.0, None, ALU.add))
                        own.link(dve.reciprocal(gates[:], den[:]))
                        dve.tensor_scalar(alpha[:], gates[:, :, 0:G4], HK ** -0.5, None, ALU.mult)
                        dve.wait_ge(s_l1, n + 1)
                        own.link(dve.scalar_tensor_tensor(sp_[:], z[:], 0.0, l1[:], ALU.max, ALU.add))
                        dve.scalar_tensor_tensor(g[:], sp_[:], -1.0, bc(ea[:].unsqueeze(1), [P, TT, G4]),
                                                 ALU.mult, ALU.mult).then_inc(s_g, 1)
                        dve.wait_ge(s_g, n + 1)
                        dve.tensor_copy(gd[:], bc(g[:].unsqueeze(3), [P, TT, G4, HK])).then_inc(s_gd, 1)
                        dve.wait_ge(s_kvt, n * 8 + 8)
                        dve.tensor_tensor(KKV[:, :, P:], vps, bc(gates[:, :, G4:], [P, TT, HK]), ALU.mult)\
                           .then_inc(s_v, 1)
                        dve.wait_ge(s_nk, n + 1)
                        own.link(dve.tensor_scalar(nke[:], nk[:], EPS, None, ALU.add))
                        own.link(dve.reciprocal(rk[:], nke[:]))
                        dve.tensor_tensor(KKV[:, :, 0:P], kps, bc(rk[:].unsqueeze(2), [P, TT, P]), ALU.mult)\
                           .then_inc(s_kn, 1)
                        dve.wait_ge(s_G, n + 1)
                        dve.tensor_scalar(negG[:].rearrange("p c h -> p (c h)"), bank[:, 3, 0:TT * G4], -1.0, None,
                                          ALU.mult).then_inc(s_Gc, 1)
                        dve.wait_ge(s_wo, n * 16 + 16)
                        dve.tensor_scalar(wos[:], wo[:], normw[:], None, ALU.mult).then_inc(s_wos, 1)
                        dve.wait_ge(s_kn, n + 1)
                        dve.wait_ge(s_v, n + 1)
                        for c in range(TT - 1):
                            if c % 2 == 0:
                                dve.wait_ge(s_De, n * 2 + c // 2 + 1)
                            for q in range(2):
                                ins = dve.tensor_tensor(
                                    KVw[:, c, q], bc(KKV[:, c, HK:].unsqueeze(1), [P, 2, P]),
                                    bc(Dm[:, c // 2, q, c % 2, :, P - 1:P], [P, 2, P]), ALU.mult)
                            ins.then_inc(s_KVw, 1)
                        dve.wait_ge(s_silu, n * 4 + 4)
                        dve.tensor_tensor(Xs[:, 1], X0[:, 1], Ed[:, 1], ALU.mult).then_inc(s_Xs, 1)
                        dve.tensor_tensor(Xs[:, 2:4], X0[:, 2:4], Ed[:, 2:4], ALU.mult).then_inc(s_Xs, 1)
                        dve.wait_ge(s_st, n + 1)
                        own.link(dve.tensor_copy(Hs[:, 0], st[:, 0]))
                        for c in range(1, TT - 1):
                            for i in range(2):
                                ins = dve.scalar_tensor_tensor(Hs[:, c, i, :], Hs[:, c - 1, i, :],
                                                               Ed[:, c, i, P - 1:P], st[:, c, i, :],
                                                               ALU.mult, ALU.add)
                            if c == 1:
                                own.link(ins)
                            else:
                                ins.then_inc(s_H, 1)
                        for r in range(3):
                            for cc in range(2):
                                dve.wait_ge(s_W, n * 6 + 2 * r + cc + 1)
                                dve.tensor_tensor(Wm[:, cc], pair(cc), Dm[:, cc], ALU.mult).then_inc(s_Wm, 1)
                            for cc in range(2 if r < 2 else 0):
                                dve.wait_ge(s_Y, n * 4 + 2 * r + cc + 1)
                                dve.scalar_tensor_tensor(
                                    X1[:, 2 * cc:2 * cc + 2].rearrange("p c i t -> p (c i t)"), bank[:, 4 + cc, :],
                                    -DAMP, X0[:, 2 * cc:2 * cc + 2].rearrange("p c i t -> p (c i t)"),
                                    ALU.mult, ALU.add).then_inc(s_X, 1)
                                dve.wait_ge(s_X, n * 4 + 2 * r + cc + 1)
                                lo = max(1, 2 * cc)
                                dve.tensor_tensor(Xs[:, lo:2 * cc + 2], X1[:, lo:2 * cc + 2], Ed[:, lo:2 * cc + 2],
                                                  ALU.mult).then_inc(s_Xs, 1)
                        dve.wait_ge(s_O, n * 2 + 2)
                        for q in range(2):
                            ins = dve.tensor_tensor(o[:, :, q::2, :], O[:, q],
                                                    bc(alpha[:, :, q::2].unsqueeze(3), [P, TT, 2, HK]), ALU.mult)
                        ins.then_inc(s_o, 1)
                        dve.wait_ge(s_sq, n + 1)
                        dve.reduce_sum(sso[:], sq[:].rearrange("p (a f) -> p a f", f=HK), axis=AX).then_inc(s_ss, 1)
                        dve.wait_ge(s_ro, n + 1)
                        dve.tensor_tensor(on[:].rearrange("p c h f -> p (c h) f"),
                                          o[:].rearrange("p c h f -> p (c h) f"),
                                          bc(ro[:].unsqueeze(2), [P, TT * G4, HK]), ALU.mult).then_inc(s_on, 1)
                        dve.wait_ge(s_oT, n * 8 + 8)
                        dve.tensor_copy(oT[:], bank[:, 0:2, :].rearrange("p h (c t) -> p h c t", c=TT))\
                           .then_inc(s_oTc, 1)
                        dve.wait_ge(s_out, n + 1)
                        xb = k.x[:, bass.ds(b * TT, TT), :].rearrange("p t n -> p (t n)")
                        dve.tensor_tensor(xb, bank[:, 2:4, :].rearrange("p a n -> p (a n)"), xb,
                                          ALU.add).then_inc(s_x, 1)
                        dve.wait_ge(s_x, n + 1)
                        own.end()

            @block.scalar
            def _(act):
                own = Chain(act, c_act, 4)
                with act.Fori(0, B) as b:
                    ln.rstd_of(act, b)
                    with act.Fori(0, HKV) as j:
                        n = b * HKV + j
                        own.begin(n)
                        for at, m in enumerate((2, 3, 0, 1)):
                            act.wait_ge(s_conv, n * 4 + at + 1)
                            if m < 2:
                                act.activation(X0[:, :, m, :], cv[:, m, :].rearrange("p (c t) -> p c t", c=TT),
                                               ACT.Silu).then_inc(s_silu, 1)
                            else:
                                M, to = (P, kT) if m == 2 else (HK, vT)
                                act.activation(to[:], cv[0:M, m, :], ACT.Silu).then_inc(s_silu, 1)
                        act.preload_act_table_set(EXP_LN)
                        act.wait_ge(s_az, n + 1)
                        own.link(act.activation(e1[:], az[:], ACT.Exp, scale=-1.0))
                        act.activation(ea[:], rows[:, 0:G4], ACT.Exp)
                        act.activation(eab[:], small[:, :, G4:], ACT.Exp, scale=-1.0).then_inc(s_es, 1)
                        act.activation(l1[:], e1[:], ACT.Ln, bias=1.0).then_inc(s_l1, 1)
                        act.wait_ge(s_kvt, n * 8 + 4)
                        for c in range(TT):
                            ins = act.activation(sq[:, c * HK:(c + 1) * HK], kps[:, c, 0:HK], ACT.Square,
                                                 accum_out=ssk[:, c:c + 1])
                        own.link(ins)
                        own.link(act.activation(lnk[:], ssk[:], ACT.Ln, bias=k.tiny[:]))
                        act.activation(nk[:], lnk[:], ACT.Exp, scale=0.5).then_inc(s_nk, 1)
                        act.wait_ge(s_E, n * 8 + 8)
                        act.activation(Ed[:].rearrange("p c i t -> p (c i t)"),
                                       bank[:, 6:8, :].rearrange("p a n -> p (a n)"), ACT.Exp).then_inc(s_Ee, 1)
                        act.wait_ge(s_Gc, n + 1)
                        for cc in range(2):
                            act.wait_ge(s_D, n * 2 + cc + 1)
                            for q in range(2):
                                for c in range(2):
                                    for i in range(2):
                                        h = 2 * i + q
                                        ins = act.activation(Dm[:, cc, q, c, i, :], pair(cc)[:, q, c, i, :], ACT.Exp,
                                                             bias=negG[:, 2 * cc + c, h:h + 1])
                            ins.then_inc(s_De, 1)
                        act.wait_ge(s_kT, n * 4 + 4)
                        act.activation(kTn[:], kps, ACT.Copy).then_inc(s_kTc, 1)
                        act.wait_ge(s_o, n + 1)
                        act.activation(sq[:], o[:].rearrange("p c h f -> p (c h f)"), ACT.Square).then_inc(s_sq, 1)
                        act.wait_ge(s_ss, n + 1)
                        own.link(act.activation(lno[:], sso[:], ACT.Ln, bias=k.eps[:], scale=1.0 / HK))
                        act.activation(ro[:], lno[:], ACT.Exp, scale=-0.5).then_inc(s_ro, 1)
                        own.end()


def context_attention(nc, k, d):
    ctx = ExitStack()
    with ctx:
        sb, ps, sem = tools(nc, ctx, "ca")
        ln = Norm(nc, k, sb, sem)
        wq = sb("wq", [P, KD, D])
        wk, wv = sb("wk", [P, D]), sb("wv", [P, D])
        bq, bk = sb("bq", [P, KD]), sb("bk", [P, KD])
        bv = sb("bv", [P, D])
        cT = sb("cT", [P, LC])
        qT = sb("qT", [P, KD, T])
        kT = sb("kT", [P, KD, LC])
        V = sb("V", [P, CT + 1, D])
        Pr = sb("Pr", [P, LC])
        PT = sb("PT", [P, CT, P])
        nm = sb("nm", [P, NT])
        rsum, rinv = sb("rsum", [P, TT]), sb("rinv", [P, TT])
        bank = ps("bank", [P, 8, 512])
        s_w, s_c = sem("w"), sem("c")
        s_kp, s_k, s_qp, s_q, s_vp, s_v = (sem(x) for x in ("kp", "k", "qp", "q", "vp", "v"))
        s_S, s_m, s_e, s_tp, s_t, s_o, s_r, s_x = (sem(x) for x in ("S", "m", "e", "tp", "t", "o", "r", "x"))
        chunks = [(c * 512, min(512, LC - c * 512)) for c in range(4)]
        groups = [(g * 4, min(4, CT - g * 4)) for g in range(4)]
        VG = (CT + 1) // 2
        vbank = [6, 7, 4, 5]

        with nc.Block() as block:
            @block.sync
            def _(sp):
                sp.dma_start(wk[:], d["ca_wk"]).then_inc(s_w, 16)
                sp.dma_start(bk[:], d["ca_bk"]).then_inc(s_w, 16)
                sp.dma_start(wq[:], d["ca_wq"].rearrange("(h p) n -> p h n", p=P)).then_inc(s_w, 16)
                sp.dma_start(bq[:], d["ca_bq"]).then_inc(s_w, 16)
                sp.dma_start(wv[:], d["ca_wv"]).then_inc(s_w, 16)
                sp.dma_start(bv[:], d["ca_bv"]).then_inc(s_w, 16)
                with sp.Fori(0, B) as b:
                    sp.wait_ge(s_vp, b * VG)
                    sp.dma_start(cT[:], d["ctxT"][b]).then_inc(s_c, 16)

            @block.tensor
            def _(pe):
                pe.wait_ge(s_w, 6 * 16)
                with pe.Fori(0, B) as b:
                    pe.wait_ge(s_x, b * TT)
                    pe.wait_ge(s_c, b * 16 + 16)
                    for h in range(KD):
                        if h:
                            pe.wait_ge(s_k, b * 2 + 1)
                        for c, (at, N) in enumerate(chunks):
                            mm = pe.matmul(bank[:, c, 0:N], wk[:, h * P:(h + 1) * P], cT[:, at:at + N],
                                           start=True, stop=True)
                        mm.then_inc(s_kp, 1)
                    ln.turn(pe, b, bank[:, 6:8, :])
                    pe.wait_ge(ln.s_xT, b + 1)
                    for h in range(KD):
                        for g in range(KD):
                            mm = pe.matmul(bank[:, 4 + h, :], wq[:, g, h * P:(h + 1) * P], ln.xT[:, g, :],
                                           start=g == 0, stop=g == KD - 1)
                        mm.then_inc(s_qp, 1)
                    for g in range(VG):
                        if g in (2, 3):
                            pe.wait_ge(s_q, b * 2 + g - 1)
                        if g >= 4:
                            pe.wait_ge(s_v, b * VG + g - 3)
                        for t in range(2 * g, min(2 * g + 2, CT)):
                            kn = P if t < CT - 1 else CLAST
                            mm = pe.matmul(bank[0:kn, vbank[g % 4], (t % 2) * D:(t % 2 + 1) * D],
                                           cT[:, t * P:t * P + kn], wv[:], start=True, stop=True)
                        mm.then_inc(s_vp, 1)
                    pe.wait_ge(s_k, b * 2 + 2)
                    pe.wait_ge(s_q, b * 2 + 2)

                    def scores(t):
                        if t:
                            pe.wait_ge(s_e, b * TT + t)
                        for c, (at, N) in enumerate(chunks):
                            for h in range(KD):
                                mm = pe.matmul(bank[:, c, 0:N], qT[:, h, t * P:(t + 1) * P], kT[:, h, at:at + N],
                                               start=h == 0, stop=h == KD - 1)
                        mm.then_inc(s_S, 1)

                    scores(0)
                    for t in range(TT):
                        if t + 1 < TT:
                            scores(t + 1)
                        pe.wait_ge(s_e, b * TT + t + 1)
                        if t == 0:
                            pe.wait_ge(s_v, b * VG + VG)
                        for g, (at, count) in enumerate(groups):
                            if t or g >= 2:
                                pe.wait_ge(s_t, (b * TT + t) * 4 + g - 1)
                            for a in range(count):
                                kt = at + a
                                kn = P if kt < CT - 1 else CLAST
                                mm = pe.transpose(bank[0:kn, 4 + g % 2, a * P:(a + 1) * P],
                                                  Pr[:, kt * P:kt * P + kn], k.ident[:])
                            mm.then_inc(s_tp, 1)
                        for g, (at, count) in enumerate(groups):
                            pe.wait_ge(s_t, (b * TT + t) * 4 + g + 1)
                            if g == 0 and t:
                                pe.wait_ge(s_x, b * TT + t)
                            for kt in range(at, at + count):
                                kn = P if kt < CT - 1 else CLAST
                                mm = pe.matmul(bank[:, 6, 0:D], PT[0:kn, kt, :], V[0:kn, kt, :],
                                               start=kt == 0, stop=kt == CT - 1)
                        mm.then_inc(s_o, 1)

            @block.vector
            def _(dve):
                dve.wait_ge(s_w, 6 * 16)
                with dve.Fori(0, B) as b:
                    ln.stats(dve, b, b)
                    ln.scale(dve, b, b)
                    ln.keep(dve, b, bank[:, 6:8, :])
                    for g in range(VG):
                        dve.wait_ge(s_vp, b * VG + g + 1)
                        if g < VG - 1:
                            dve.tensor_tensor(V[:, 2 * g:2 * g + 2, :],
                                              bank[:, vbank[g % 4], :].rearrange("p (a n) -> p a n", a=2),
                                              bc(bv[:].unsqueeze(1), [P, 2, D]), ALU.add).then_inc(s_v, 1)
                        else:
                            dve.tensor_tensor(V[0:CLAST, 2 * g, :], bank[0:CLAST, vbank[g % 4], 0:D], bv[0:CLAST],
                                              ALU.add).then_inc(s_v, 1)

                    def top(t):
                        dve.wait_ge(s_S, b * TT + t + 1)
                        dve.reduce_max(nm[:, t:t + 1], bank[:, 0:4, :].rearrange("p a n -> p (a n)")[:, 0:LC],
                                       axis=AX, negate=True).then_inc(s_m, 1)

                    top(0)
                    for t in range(TT):
                        if t + 1 < TT:
                            top(t + 1)
                        for g in (0, 2):
                            at, count = groups[g]
                            dve.wait_ge(s_tp, (b * TT + t) * 4 + g + 1)
                            if g == 2:
                                dve.wait_ge(s_t, (b * TT + t) * 4 + 2)
                            dve.tensor_copy(PT[:, at:at + count, :],
                                            bank[:, 4, :].rearrange("p (a n) -> p a n", a=4)).then_inc(s_t, 1)
                        dve.wait_ge(s_e, b * TT + t + 1)
                        dve.reciprocal(rinv[:, t:t + 1], rsum[:, t:t + 1]).then_inc(s_r, 1)
                        dve.wait_ge(s_r, b * TT + t + 1)
                        dve.wait_ge(s_o, b * TT + t + 1)
                        dve.scalar_tensor_tensor(k.x[:, b * TT + t, :], bank[:, 6, 0:D], rinv[:, t:t + 1],
                                                 k.x[:, b * TT + t, :], ALU.mult, ALU.add).then_inc(s_x, 1)
                    dve.wait_ge(s_x, b * TT + TT)

            @block.scalar
            def _(act):
                act.preload_act_table_set(EXP_LN)
                act.wait_ge(s_w, 6 * 16)
                with act.Fori(0, B) as b:
                    for h in range(KD):
                        act.wait_ge(s_kp, b * 2 + h + 1)
                        act.activation(kT[:, h, :], bank[:, 0:4, :].rearrange("p a n -> p (a n)")[:, 0:LC],
                                       ACT.Identity, bias=bk[:, h:h + 1]).then_inc(s_k, 1)
                    ln.rstd_of(act, b)
                    for h in range(KD):
                        act.wait_ge(s_qp, b * 2 + h + 1)
                        act.activation(qT[:, h, :], bank[:, 4 + h, :], ACT.Identity,
                                       bias=bq[:, h:h + 1]).then_inc(s_q, 1)

                    def exps(t):
                        act.wait_ge(s_m, b * TT + t + 1)
                        if t:
                            act.wait_ge(s_tp, (b * TT + t) * 4)
                        act.activation(Pr[:], bank[:, 0:4, :].rearrange("p a n -> p (a n)")[:, 0:LC], ACT.Exp,
                                       bias=nm[:, t:t + 1], accum_out=rsum[:, t:t + 1]).then_inc(s_e, 1)

                    exps(0)
                    for t in range(TT):
                        for g in (1, 3):
                            at, count = groups[g]
                            kn = P if g == 1 else CLAST
                            act.wait_ge(s_tp, (b * TT + t) * 4 + g + 1)
                            act.wait_ge(s_t, (b * TT + t) * 4 + g)
                            act.activation(PT[0:kn, at:at + count, :],
                                           bank[0:kn, 5, 0:count * P].rearrange("p (a n) -> p a n", n=P),
                                           ACT.Copy).then_inc(s_t, 1)
                        if t + 1 < TT:
                            exps(t + 1)


def experts(nc, k, d):
    ctx = ExitStack()
    with ctx:
        sb, ps, sem = tools(nc, ctx, "ex")
        ln = Norm(nc, k, sb, sem)
        xT = sb("xT", [P, KD, NT * P])
        acc = sb("acc", [P, NT, D])
        wr = sb("wr", [P, KD, E])
        br = sb("br", [P, E])
        b2 = sb("b2", [E, D])
        b1 = [sb(f"b1_{i}", [P, FT]) for i in range(2)]
        gamma, beta = sb("gamma", [P, D]), sb("beta", [P, D])
        iota = sb("iota", [P, E])
        iotaw = sb("iotaw", [P, E], mybir.dt.int32)
        lg = sb("lg", [P, NT, E])
        top = sb("top", [P, NT, E])
        idx = sb("idx", [P, NT, E], mybir.dt.uint32)
        idf = sb("idf", [P, NT, 2])
        dif, ex, de, w1s, w2s = (sb(x, [P, NT]) for x in ("dif", "exp", "den", "w1s", "w2s"))
        oh = sb("oh", [P, 2, NT, E])
        rw = sb("rw", [P, NT, E])
        rT = sb("rT", [E, NT, P])
        W1 = [sb(f"W1_{i}", [P, KD, F]) for i in range(2)]
        W2 = [sb(f"W2_{i}", [P, FT, D]) for i in range(2)]
        hT = [sb(f"hT_{i}", [P, FT, T]) for i in range(2)]
        gst, gmv = sb("gst", [P, NT, 6]), sb("gmv", [P, NT, 2])
        gln, grs = sb("gln", [P, NT]), sb("grs", [P, NT])
        spare = sb("spare", [P, 1])
        bank = ps("bank", [P, 8, 512])
        s_w = sem("w")
        s_w1, s_w2 = ([sem(f"{x}_{i}") for i in range(2)] for x in ("w1", "w2"))
        s_keep, s_lg, s_lgs, s_rw, s_rtp, s_rT, s_b2, s_acc0 = (
            sem(x) for x in ("keep", "lg", "lgs", "rw", "rtp", "rT", "b2", "acc0"))
        s_dif, s_ex, s_io = sem("dif"), sem("ex"), sem("iota")
        s_h, s_hr, s_o, s_acc = sem("h"), sem("hr"), sem("o"), sem("acc")
        s_gmv, s_gln, s_grs = sem("gmv"), sem("gln"), sem("grs")
        c_dve = sem("c_dve")

        with nc.Block() as block:
            @block.sync
            def _(sp):
                for tile, name in ((br, "ex_br"), (b2, "ex_b2"), (gamma, "ex_gamma"),
                                   (beta, "ex_beta"), (wr, "ex_wr")):
                    sp.dma_start(tile[:], d[name]).then_inc(s_w, 16)
                def load(e, par):
                    sp.dma_start(W1[par][:], d["ex_w1"][e].rearrange("(h p) f -> p h f", p=P)).then_inc(s_w1[par], 16)
                    sp.dma_start(b1[par][:], d["ex_b1"][e]).then_inc(s_w1[par], 16)
                    sp.dma_start(W2[par][:], d["ex_w2"][e].rearrange("(f p) n -> p f n", p=P)).then_inc(s_w2[par], 16)

                for par in range(2):
                    load(par, par)
                with sp.Fori(0, E // 2 - 1) as e2:
                    for par in range(2):
                        sp.wait_ge(s_o, e2 * (2 * B * TT) + (par + 1) * B * TT)
                        load(e2 * 2 + 2 + par, par)

            @block.gpsimd
            def _(pool):
                pool.iota(iotaw[:], pattern=[[1, E]], base=0, channel_multiplier=0).then_inc(s_io, 1)
                pool.wait_ge(s_io, 1)
                pool.tensor_copy(iota[:], iotaw[:]).then_inc(s_io, 1)

            @block.tensor
            def _(pe):
                pe.wait_ge(s_w, 5 * 16)
                with pe.Fori(0, B) as b:
                    pe.wait_ge(s_keep, b)
                    ln.turn(pe, b, bank[:, 6:8, :])
                    pe.wait_ge(ln.s_xT, b + 1)
                    pe.wait_ge(s_lgs, b)
                    for t in range(TT):
                        for h in range(KD):
                            mm = pe.matmul(bank[:, 5, t * E:(t + 1) * E], ln.xT[:, h, t * P:(t + 1) * P], wr[:, h, :],
                                           start=h == 0, stop=h == KD - 1)
                    mm.then_inc(s_lg, 1)
                pe.wait_ge(s_rw, 1)
                pe.wait_ge(s_keep, B)
                for t in range(NT):
                    mm = pe.transpose(bank[0:E, t // 4, (t % 4) * P:(t % 4 + 1) * P], rw[:, t, :], k.ident[:])
                mm.then_inc(s_rtp, 1)
                pe.wait_ge(s_rT, 1)
                for t in range(NT):
                    mm = pe.matmul(bank[:, t // 2, (t % 2) * D:(t % 2 + 1) * D], rT[:, t, :], b2[:],
                                   start=True, stop=True)
                mm.then_inc(s_b2, 1)
                pe.wait_ge(s_acc0, 1)
                with pe.Fori(0, E // 2) as e2:
                    for par in range(2):
                        pe.wait_ge(s_w1[par], e2 * 32 + 32)
                        pe.wait_ge(s_w2[par], e2 * 16 + 16)
                        for b in range(B):
                                u = b % 2
                                n = e2 * (2 * B) + par * B + b
                                for f in range(FT):
                                    if f < 4:
                                        pe.wait_ge(s_hr, n * FT)
                                    else:
                                        pe.wait_ge(s_hr, n * FT + f - 3)
                                    for h in range(KD):
                                        mm = pe.matmul(bank[:, f % 4, :], W1[par][:, h, f * P:(f + 1) * P],
                                                       xT[:, h, b * T:(b + 1) * T], start=h == 0, stop=h == KD - 1)
                                    mm.then_inc(s_h, 1)
                                pe.wait_ge(s_acc, n * TT)
                                for t in range(TT):
                                    for f in range(FT):
                                        if t == 0:
                                            pe.wait_ge(s_hr, n * FT + f + 1)
                                        mm = pe.matmul(bank[:, 4 + t, 0:D], hT[u][:, f, t * P:(t + 1) * P],
                                                       W2[par][:, f, :], start=f == 0, stop=f == FT - 1)
                                    mm.then_inc(s_o, 1)

            @block.vector
            def _(dve):
                own = Chain(dve, c_dve, 17)
                dve.wait_ge(s_w, 5 * 16)
                with dve.Fori(0, B) as b:
                    ln.stats(dve, b, b)
                    ln.scale(dve, b, b)
                    ln.keep(dve, b, bank[:, 6:8, :])
                    dve.wait_ge(ln.s_xT, b + 1)
                    dve.tensor_copy(xT[:, :, bass.ds(b * T, T)], ln.xT[:])
                    dve.tensor_copy(acc[:, bass.ds(b * TT, TT), :], ln.xn[:]).then_inc(s_keep, 1)
                    dve.wait_ge(s_lg, b + 1)
                    dve.tensor_tensor(lg[:, bass.ds(b * TT, TT), :],
                                      bank[:, 5, 0:TT * E].rearrange("p (t e) -> p t e", e=E),
                                      bc(br[:].unsqueeze(1), [P, TT, E]), ALU.add).then_inc(s_lgs, 1)
                    dve.wait_ge(s_keep, b + 1)
                own.begin(0)
                dve.wait_ge(s_lgs, B)
                for t in range(NT):
                    ins = dve.max(top[:, t, :], lg[:, t, :])
                own.link(ins)
                for t in range(NT):
                    ins = dve.max_index(idx[:, t, :], top[:, t, :], lg[:, t, :])
                own.link(ins)
                own.link(dve.tensor_copy(idf[:], idx[:, :, 0:2]))
                dve.tensor_tensor(dif[:], top[:, :, 1], top[:, :, 0], ALU.subtract).then_inc(s_dif, 1)
                dve.wait_ge(s_ex, 1)
                own.link(dve.tensor_scalar(de[:], ex[:], 1.0, None, ALU.add))
                own.link(dve.reciprocal(w1s[:], de[:]))
                own.link(dve.tensor_tensor(w2s[:], w1s[:], ex[:], ALU.mult))
                dve.wait_ge(s_io, 2)
                for a in range(2):
                    own.link(dve.tensor_tensor(oh[:, a], bc(iota[:].unsqueeze(1), [P, NT, E]),
                                               bc(idf[:, :, a:a + 1], [P, NT, E]), ALU.is_equal))
                for a, ws in enumerate((w1s, w2s)):
                    own.link(dve.tensor_tensor(oh[:, a], oh[:, a], bc(ws[:].unsqueeze(2), [P, NT, E]), ALU.mult))
                dve.tensor_tensor(rw[:], oh[:, 0], oh[:, 1], ALU.add).then_inc(s_rw, 1)
                dve.wait_ge(s_rtp, 1)
                dve.tensor_copy(rT[:], bank[0:E, 0:4, :].rearrange("p a (t q) -> p (a t) q", q=P)).then_inc(s_rT, 1)
                dve.wait_ge(s_b2, 1)
                dve.tensor_tensor(acc[:].rearrange("p t n -> p (t n)"), bank[:].rearrange("p a n -> p (a n)"),
                                  acc[:].rearrange("p t n -> p (t n)"), ALU.add).then_inc(s_acc0, 1)
                dve.wait_ge(s_acc0, 1)
                with dve.Fori(0, E // 2) as e2:
                    for par in range(2):
                        for b in range(B):
                                n = e2 * (2 * B) + par * B + b
                                dve.wait_ge(s_acc, n * TT)
                                for t in range(TT):
                                    dve.wait_ge(s_o, n * TT + t + 1)
                                    tile = b * TT + t
                                    dve.scalar_tensor_tensor(
                                        acc[:, tile, :], bank[:, 4 + t, 0:D],
                                        rw[:, tile, bass.ds(e2 * 2 + par, 1)],
                                        acc[:, tile, :], ALU.mult, ALU.add).then_inc(s_acc, 1)
                dve.wait_ge(s_acc, 2 * B * TT * (E // 2))
                for t in range(NT):
                    ins = dve.bn_stats(gst[:, t, :], acc[:, t, :])
                own.link(ins)
                for t in range(NT):
                    ins = dve.bn_aggr(gmv[:, t, :], gst[:, t, :])
                ins.then_inc(s_gmv, 1)
                dve.wait_ge(s_grs, 1)
                for t in range(NT):
                    ins = dve.tensor_scalar(acc[:, t, :], acc[:, t, :], gmv[:, t, 0:1], grs[:, t:t + 1],
                                            ALU.subtract, ALU.mult)
                own.link(ins)
                own.link(dve.tensor_tensor(acc[:], acc[:], bc(gamma[:].unsqueeze(1), [P, NT, D]), ALU.mult))
                own.link(dve.tensor_tensor(acc[:], acc[:], bc(beta[:].unsqueeze(1), [P, NT, D]), ALU.add))
                own.link(dve.tensor_tensor(k.x[:], k.x[:], acc[:], ALU.add))

            @block.scalar
            def _(act):
                act.preload_act_table_set(EXP_LN)
                act.wait_ge(s_w, 5 * 16)
                with act.Fori(0, B) as b:
                    ln.rstd_of(act, b)
                act.wait_ge(s_dif, 1)
                act.activation(ex[:], dif[:], ACT.Exp).then_inc(s_ex, 1)
                with act.Fori(0, E // 2) as e2:
                    for par in range(2):
                        for b in range(B):
                                u = b % 2
                                n = e2 * (2 * B) + par * B + b
                                for f in range(FT):
                                    act.wait_ge(s_h, n * FT + f + 1)
                                    act.activation(hT[u][:, f, :], bank[:, f % 4, :], ACT.Relu,
                                                   bias=b1[par][:, f:f + 1])\
                                       .then_inc(s_hr, 1)
                act.wait_ge(s_gmv, 1)
                act.activation(gln[:], gmv[:, :, 1], ACT.Ln, bias=k.ln_eps[:]).then_inc(s_gln, 1)
                act.wait_ge(s_gln, 1)
                act.activation(grs[:], gln[:], ACT.Exp, scale=-0.5).then_inc(s_grs, 1)


class Attend:

    RING = 3
    PROBS = 4
    SCALE = HD ** -0.5

    def __init__(self, nc, k, sb, sem, bank, name, keys, causal, qT, kT, V, out_bank):
        self.k, self.bank, self.causal = k, bank, causal
        self.qT, self.kT, self.V, self.out = qT, kT, V, bank[:, out_bank, :]
        self.keys = keys
        self.tiles = [(at, min(P, keys - at)) for at in range(0, keys, P)]
        self.U = 2 * len(self.tiles)
        self.wide = keys > T
        self.NM = 4 * TT if self.wide else TT
        self.M = sb(f"{name}_M", [P, TT, 4, SH])
        self.qa = sb(f"{name}_qa", [P, T])
        self.pr = sb(f"{name}_pr", [P, self.PROBS, 2, T])
        self.yT = sb(f"{name}_yT", [P, T])
        self.rec = sb(f"{name}_rec", [P, TT, 4])
        (self.s_m, self.s_mx, self.s_mt, self.s_q, self.s_s, self.s_e, self.s_pv, self.s_yT, self.s_yt,
         self.s_rec, self.s_y, self.s_M0) = (sem(f"{name}_{x}") for x in (
             "m", "mx", "mt", "q", "s", "e", "pv", "yT", "yt", "rec", "y", "M0"))

    def clear(self, dve):
        dve.memset(self.M[:], 0.0).then_inc(self.s_M0, 1)
        dve.wait_ge(self.s_M0, 1)

    def rows(self, h, size):
        return slice(h * SH, h * SH + size)

    def pe_max(self, pe, n):
        for m in range(self.NM):
            half = 4 * (m % 2)
            if m >= 2:
                pe.wait_ge(self.s_mx, n * self.NM + m - 1)
            if self.wide:
                t, h = divmod(m, 4)
                for c in range(4):
                    N = min(512, self.keys - c * 512)
                    mm = pe.matmul(self.bank[:, half + c, 0:N], self.qT[self.rows(h, HD), t * P:(t + 1) * P],
                                   self.kT[self.rows(h, HD), c * 512:c * 512 + N], start=True, stop=True)
            else:
                N = P * (m + 1) if self.causal else self.keys
                for h in range(4):
                    mm = pe.matmul(self.bank[:, half + h, 0:N], self.qT[self.rows(h, HD), m * P:(m + 1) * P],
                                   self.kT[self.rows(h, HD), 0:N], start=True, stop=True)
                if self.causal:
                    for h in range(4):
                        mm = pe.matmul(self.bank[:, half + h, N - P:N], self.k.identb[:], self.k.mask_qk[:],
                                       start=False, stop=True, skip_group_check=True)
            mm.then_inc(self.s_m, 1)

    def dve_max(self, dve, n):
        for m in range(self.NM):
            half = 4 * (m % 2)
            dve.wait_ge(self.s_m, n * self.NM + m + 1)
            if self.wide:
                t, h = divmod(m, 4)
                src = self.bank[:, half:half + 4, :].rearrange("p a n -> p (a n)")[:, 0:self.keys]
                dve.reduce_max(self.M[:, t, h, HD:HD + 1], src, axis=AX, negate=True).then_inc(self.s_mx, 1)
            else:
                N = P * (m + 1) if self.causal else self.keys
                dve.reduce_max(self.M[:, m, :, HD], self.bank[:, half:half + 4, 0:N], axis=AX, negate=True)\
                   .then_inc(self.s_mx, 1)

    def pe_turn_max(self, pe, n):
        pe.wait_ge(self.s_mx, (n + 1) * self.NM)
        for t in range(TT):
            mm = pe.transpose(self.bank[:, 0, t * P:(t + 1) * P], self.M[:, t].rearrange("p h f -> p (h f)"),
                              self.k.ident[:])
        mm.then_inc(self.s_mt, 1)

    def dve_queries(self, dve, n):
        dve.wait_ge(self.s_mt, n + 1)
        dve.tensor_tensor(self.qa[:], self.bank[:, 0, :], self.qT[:], ALU.add).then_inc(self.s_q, 1)

    def span(self, kt):
        return (kt * P, T) if self.causal else (0, T)

    def pe_attend(self, pe, n):
        pe.wait_ge(self.s_q, n + 1)

        def scores(u):
            kt, pp = divmod(u, 2)
            at, kn = self.tiles[kt]
            lo, hi = self.span(kt)
            if u >= self.RING:
                pe.wait_ge(self.s_e, n * self.U + u - self.RING + 1)
            for a in range(2):
                h = 2 * pp + a
                dst = self.bank[0:kn, 2 * (u % self.RING) + a, 0:hi - lo]
                mm = pe.matmul(dst, self.kT[self.rows(h, HD + 1), at:at + kn], self.qa[self.rows(h, HD + 1), lo:hi],
                               start=True, stop=True)
            if self.causal:
                for a in range(2):
                    mm = pe.matmul(self.bank[:, 2 * (u % self.RING) + a, 0:P], self.k.identb[:], self.k.mask_kq[:],
                                   start=False, stop=True, skip_group_check=True)
            mm.then_inc(self.s_s, 1)

        def values(u):
            kt, pp = divmod(u, 2)
            _, kn = self.tiles[kt]
            lo, hi = self.span(kt)
            pe.wait_ge(self.s_e, n * self.U + u + 1)
            for a in range(2):
                h = 2 * pp + a
                mm = pe.matmul(self.out[self.rows(h, SH), lo:hi], self.V[0:kn, kt, self.rows(h, SH)],
                               self.pr[0:kn, u % self.PROBS, a, 0:hi - lo], start=kt == 0,
                               stop=kt == len(self.tiles) - 1, skip_group_check=True)
            mm.then_inc(self.s_pv, 1)

        LAG = 2
        for u in range(self.U + LAG):
            if u < self.U:
                scores(u)
            if u >= LAG:
                values(u - LAG)

    def act_attend(self, act, n):
        for u in range(self.U):
            kt, pp = divmod(u, 2)
            _, kn = self.tiles[kt]
            lo, hi = self.span(kt)
            act.wait_ge(self.s_s, n * self.U + u + 1)
            if u >= self.PROBS:
                act.wait_ge(self.s_pv, n * self.U + u - self.PROBS + 1)
            r = 2 * (u % self.RING)
            act.activation(self.pr[0:kn, u % self.PROBS, :, 0:hi - lo], self.bank[0:kn, r:r + 2, 0:hi - lo],
                           ACT.Exp, scale=self.SCALE).then_inc(self.s_e, 1)

    def dve_out(self, dve, n):
        dve.wait_ge(self.s_pv, (n + 1) * self.U)
        dve.tensor_copy(self.yT[:], self.out).then_inc(self.s_yT, 1)

    def pe_out(self, pe, n):
        pe.wait_ge(self.s_yT, n + 1)
        for t in range(TT):
            mm = pe.transpose(self.bank[:, 0, t * P:(t + 1) * P], self.yT[:, t * P:(t + 1) * P], self.k.ident[:])
        mm.then_inc(self.s_yt, 1)

    def dve_divide(self, dve, n, y):
        dve.wait_ge(self.s_yt, n + 1)
        src = self.bank[:, 0, :].rearrange("p (t h f) -> p t h f", t=TT, h=4)
        dve.reciprocal(self.rec[:], src[:, :, :, HD]).then_inc(self.s_rec, 1)
        dve.wait_ge(self.s_rec, n + 1)
        dve.tensor_tensor(y, src[:, :, :, 0:HD], bc(self.rec[:].unsqueeze(3), [P, TT, 4, HD]), ALU.mult)\
           .then_inc(self.s_y, 1)


class Project:

    def __init__(self, nc, k, sb, sem, bank, name):
        self.k, self.bank = k, bank
        self.w, self.bias = sb(f"{name}_w", [P, KD, D]), sb(f"{name}_b", [P, D])
        self.yT = sb(f"{name}_yT", [P, KD, T])
        self.s_w, self.s_t, self.s_c, self.s_p, self.s_b, self.s_x = (
            sem(f"{name}_{x}") for x in ("w", "t", "c", "p", "b", "x"))

    def load(self, sp, w, bias):
        sp.dma_start(self.w[:], w.rearrange("(h p) n -> p h n", p=P)).then_inc(self.s_w, 16)
        sp.dma_start(self.bias[:], bias).then_inc(self.s_w, 16)

    def pe(self, pe, n, y):
        pe.wait_ge(self.s_w, 32)
        for h in range(KD):
            for t in range(TT):
                mm = pe.transpose(self.bank[:, 2 + h, t * P:(t + 1) * P], y[:, t, h * P:(h + 1) * P], self.k.ident[:])
        mm.then_inc(self.s_t, 1)
        pe.wait_ge(self.s_c, n + 1)
        for t in range(TT):
            for h in range(KD):
                mm = pe.matmul(self.bank[:, 4 + t // 2, (t % 2) * D:(t % 2 + 1) * D],
                               self.yT[:, h, t * P:(t + 1) * P], self.w[:, h, :], start=h == 0, stop=h == KD - 1)
        mm.then_inc(self.s_p, 1)

    def dve(self, dve, b, n):
        x = self.k.x[:, bass.ds(b * TT, TT), :]
        dve.wait_ge(self.s_w, 32)
        dve.tensor_tensor(x, x, bc(self.bias[:].unsqueeze(1), [P, TT, D]), ALU.add).then_inc(self.s_b, 1)
        dve.wait_ge(self.s_t, n + 1)
        dve.tensor_copy(self.yT[:], self.bank[:, 2:4, :]).then_inc(self.s_c, 1)
        dve.wait_ge(self.s_b, n + 1)
        dve.wait_ge(self.s_p, n + 1)
        dve.tensor_tensor(x.rearrange("p t n -> p (t n)"), self.bank[:, 4:6, :].rearrange("p a n -> p (a n)"),
                          x.rearrange("p t n -> p (t n)"), ALU.add).then_inc(self.s_x, 1)
        dve.wait_ge(self.s_x, n + 1)


def self_attention(nc, k, d):
    ctx = ExitStack()
    with ctx:
        sb, ps, sem = tools(nc, ctx, "sa")
        bank = ps("bank", [P, 8, 512])
        ln = Norm(nc, k, sb, sem)
        WC = 2 * 4 * HD + SW
        w, bias = sb("w", [P, KD, WC]), sb("bias", [P, WC])
        nw = sb("nw", [P, 2, 4, HD])
        qk = sb("qk", [P, TT, 2 * 4 * HD])
        sq = sb("sq", [P, TT, 2 * 4 * HD])
        ss, lg, rs = (sb(x, [P, TT, 8]) for x in ("ss", "lg", "rs"))
        pad = sb("pad", [P, 2, TT, 4, SH])
        qT, kT = sb("qT", [P, T]), sb("kT", [P, T])
        V = sb("V", [P, TT, SW])
        y = sb("y", [P, TT, D])
        at = Attend(nc, k, sb, sem, bank, "at", T, False, qT, kT, V, 6)
        pr = Project(nc, k, sb, sem, bank, "pr")
        s_w, s_nw, s_p, s_qk, s_v, s_sq, s_ss, s_lg, s_rs, s_nm, s_pad, s_pt, s_qT = (
            sem(x) for x in ("w", "nw", "p", "qk", "v", "sq", "ss", "lg", "rs", "nm", "pad", "pt", "qT"))
        s_clear = sem("clear")

        with nc.Block() as block:
            @block.sync
            def _(sp):
                sp.dma_start(nw[:], d["sa_nw"].rearrange("p (a h f) -> p a h f", a=2, h=4)).then_inc(s_nw, 16)
                pr.load(sp, d["sa_wp"], d["sa_bp"])
                with sp.Fori(0, B) as b:
                    with sp.Fori(0, NG) as g:
                        n = b * NG + g
                        sp.wait_ge(s_p, n)
                        sp.wait_ge(s_v, n)
                        sp.dma_start(w[:], d["sa_w"][g].rearrange("(h p) n -> p h n", p=P)).then_inc(s_w, 16)
                        sp.dma_start(bias[:], d["sa_b"][g]).then_inc(s_w, 16)

            @block.tensor
            def _(pe):
                with pe.Fori(0, B) as b:
                    pe.wait_ge(pr.s_x, b)
                    ln.turn(pe, b, bank[:, 6:8, :])
                    with pe.Fori(0, NG) as g:
                        n = b * NG + g
                        pe.wait_ge(ln.s_xT, b + 1)
                        pe.wait_ge(at.s_y, n)
                        pe.wait_ge(s_w, n * 32 + 32)
                        for t in range(TT):
                            for h in range(KD):
                                mm = pe.matmul(bank[:, t // 2, (t % 2) * WC:(t % 2 + 1) * WC],
                                               ln.xT[:, h, t * P:(t + 1) * P], w[:, h, :],
                                               start=h == 0, stop=h == KD - 1)
                        mm.then_inc(s_p, 1)
                        pe.wait_ge(s_pad, n + 1)
                        for a in range(2):
                            for t in range(TT):
                                mm = pe.transpose(bank[:, 2 + a, t * P:(t + 1) * P],
                                                  pad[:, a, t].rearrange("p h f -> p (h f)"), k.ident[:])
                        mm.then_inc(s_pt, 1)
                        pe.wait_ge(s_qT, n * 2 + 2)
                        pe.wait_ge(s_v, n + 1)
                        at.pe_max(pe, n)
                        at.pe_turn_max(pe, n)
                        at.pe_attend(pe, n)
                        at.pe_out(pe, n)
                    pe.wait_ge(at.s_y, b * NG + NG)
                    pr.pe(pe, b, y)

            @block.vector
            def _(dve):
                at.clear(dve)
                dve.memset(pad[:], 0.0).then_inc(s_clear, 1)
                dve.wait_ge(s_clear, 1)
                dve.memset(pad[:, 1, :, :, HD:HD + 1], 1.0).then_inc(s_clear, 1)
                dve.wait_ge(s_clear, 2)
                dve.wait_ge(s_nw, 16)
                with dve.Fori(0, B) as b:
                    ln.stats(dve, b, b)
                    ln.scale(dve, b, b)
                    ln.keep(dve, b, bank[:, 6:8, :])
                    with dve.Fori(0, NG) as g:
                        n = b * NG + g
                        dve.wait_ge(s_p, n + 1)
                        dve.wait_ge(s_w, n * 32 + 32)
                        src = bank[:, 0:2, :].rearrange("p a (t n) -> p (a t) n", n=WC)
                        dve.tensor_tensor(qk[:], src[:, :, 0:P], bc(bias[:, 0:P].unsqueeze(1), [P, TT, P]), ALU.add)\
                           .then_inc(s_qk, 1)
                        dve.tensor_tensor(V[:], src[:, :, P:], bc(bias[:, P:].unsqueeze(1), [P, TT, SW]), ALU.add)\
                           .then_inc(s_v, 1)
                        dve.wait_ge(s_sq, n + 1)
                        dve.reduce_sum(ss[:], sq[:].rearrange("p t (a f) -> p t a f", f=HD), axis=AX).then_inc(s_ss, 1)
                        dve.wait_ge(s_rs, n + 1)
                        dve.tensor_tensor(sq[:].rearrange("p t (a f) -> p t a f", f=HD),
                                          qk[:].rearrange("p t (a f) -> p t a f", f=HD),
                                          bc(rs[:].unsqueeze(3), [P, TT, 8, HD]), ALU.mult).then_inc(s_nm, 1)
                        dve.wait_ge(s_nm, n + 1)
                        for a in range(2):
                            ins = dve.tensor_tensor(
                                pad[:, a, :, :, 0:HD],
                                sq[:, :, a * 64:(a + 1) * 64].rearrange("p t (h f) -> p t h f", f=HD),
                                bc(nw[:, a].unsqueeze(1), [P, TT, 4, HD]), ALU.mult)
                        ins.then_inc(s_pad, 1)
                        dve.wait_ge(s_pt, n + 1)
                        dve.tensor_copy(qT[:], bank[:, 2, :]).then_inc(s_qT, 1)
                        dve.tensor_copy(kT[:], bank[:, 3, :]).then_inc(s_qT, 1)
                        at.dve_max(dve, n)
                        dve.wait_ge(s_qT, n * 2 + 2)
                        at.dve_queries(dve, n)
                        at.dve_out(dve, n)
                        at.dve_divide(dve, n, y[:, :, bass.ds(g * 4 * HD, 4 * HD)]
                                      .rearrange("p t (h f) -> p t h f", f=HD))
                    pr.dve(dve, b, b)

            @block.scalar
            def _(act):
                act.preload_act_table_set(EXP_LN)
                with act.Fori(0, B) as b:
                    ln.rstd_of(act, b)
                    with act.Fori(0, NG) as g:
                        n = b * NG + g
                        act.wait_ge(s_qk, n + 1)
                        act.activation(sq[:], qk[:], ACT.Square).then_inc(s_sq, 1)
                        act.wait_ge(s_ss, n + 1)
                        act.activation(lg[:], ss[:], ACT.Ln, bias=k.eps[:], scale=1.0 / HD).then_inc(s_lg, 1)
                        act.wait_ge(s_lg, n + 1)
                        act.activation(rs[:], lg[:], ACT.Exp, scale=-0.5).then_inc(s_rs, 1)
                        at.act_attend(act, n)


def cross_attention(nc, k, d):
    ctx = ExitStack()
    with ctx:
        sb, ps, sem = tools(nc, ctx, "xa")
        bank = ps("bank", [P, 8, 512])
        ln = Norm(nc, k, sb, sem)
        w = sb("w", [P, KD, 4 * SW])
        wc = sb("wc", [P, 2 * SW])
        bcol = sb("bcol", [P, 4])
        brow = sb("brow", [P, 2 * SW])
        cT = sb("cT", [P, LC])
        qT, kT, cqT = sb("qT", [P, T]), sb("kT", [P, T]), sb("cqT", [P, T])
        ckT = sb("ckT", [P, LC])
        V, cV = sb("V", [P, TT, SW]), sb("cV", [P, CT, SW])
        y, yc = sb("y", [P, TT, D]), sb("yc", [P, TT, 4 * HD])
        own_at = Attend(nc, k, sb, sem, bank, "own", T, True, qT, kT, V, 6)
        ctx_at = Attend(nc, k, sb, sem, bank, "ctx", LC, False, cqT, ckT, cV, 7)
        pr = Project(nc, k, sb, sem, bank, "pr")
        s_w, s_c, s_p, s_b, s_cp, s_cb, s_y = (sem(x) for x in ("w", "c", "p", "b", "cp", "cb", "y"))
        chunks = [(c * 512, min(512, LC - c * 512)) for c in range(4)]
        NCV = 4

        with nc.Block() as block:
            @block.sync
            def _(sp):
                pr.load(sp, d["xa_wp"], d["xa_bp"])
                with sp.Fori(0, B) as b:
                    sp.wait_ge(s_cp, b * NG * 5)
                    sp.dma_start(cT[:], d["ctxT"][b]).then_inc(s_c, 16)
                    with sp.Fori(0, NG) as g:
                        n = b * NG + g
                        sp.wait_ge(s_cb, n * 5)
                        sp.dma_start(w[:], d["xa_w"][g].rearrange("(h p) n -> p h n", p=P)).then_inc(s_w, 16)
                        sp.dma_start(wc[:], d["xa_wc"][g]).then_inc(s_w, 16)
                        sp.dma_start(bcol[:], d["xa_bcol"][g]).then_inc(s_w, 16)
                        sp.dma_start(brow[:], d["xa_brow"][g]).then_inc(s_w, 16)

            @block.tensor
            def _(pe):
                with pe.Fori(0, B) as b:
                    pe.wait_ge(pr.s_x, b)
                    ln.turn(pe, b, bank[:, 6:8, :])
                    with pe.Fori(0, NG) as g:
                        n = b * NG + g
                        pe.wait_ge(ln.s_xT, b + 1)
                        pe.wait_ge(s_c, b * 16 + 16)
                        pe.wait_ge(s_y, n)
                        pe.wait_ge(s_w, n * 64 + 64)
                        for a, col in enumerate((0, 1, 3)):
                            for h in range(KD):
                                mm = pe.matmul(bank[:, a, :], w[:, h, col * SW:(col + 1) * SW], ln.xT[:, h, :],
                                               start=h == 0, stop=h == KD - 1)
                            mm.then_inc(s_p, 1)
                        for t in range(TT):
                            for h in range(KD):
                                mm = pe.matmul(bank[:, 3, t * P:(t + 1) * P], ln.xT[:, h, t * P:(t + 1) * P],
                                               w[:, h, 2 * SW:3 * SW], start=h == 0, stop=h == KD - 1)
                        mm.then_inc(s_p, 1)
                        for c, (at, N) in enumerate(chunks):
                            mm = pe.matmul(bank[:, 4 + c, 0:N], wc[:, 0:SW], cT[:, at:at + N], start=True, stop=True)
                        mm.then_inc(s_cp, 1)
                        for v in range(NCV):
                            pe.wait_ge(s_b, n * 4 + v + 1)
                            for t in range(4 * v, min(4 * v + 4, CT)):
                                kn = P if t < CT - 1 else CLAST
                                mm = pe.matmul(bank[0:kn, v, (t % 4) * P:(t % 4 + 1) * P], cT[:, t * P:t * P + kn],
                                               wc[:, SW:], start=True, stop=True)
                            mm.then_inc(s_cp, 1)
                        pe.wait_ge(s_cb, n * 5 + 5)
                        own_at.pe_max(pe, n)
                        pe.wait_ge(own_at.s_mx, (n + 1) * own_at.NM)
                        ctx_at.pe_max(pe, n)
                        pe.wait_ge(ctx_at.s_mx, (n + 1) * ctx_at.NM)
                        own_at.pe_turn_max(pe, n)
                        pe.wait_ge(own_at.s_q, n + 1)
                        ctx_at.pe_turn_max(pe, n)
                        pe.wait_ge(ctx_at.s_q, n + 1)
                        own_at.pe_attend(pe, n)
                        ctx_at.pe_attend(pe, n)
                        own_at.pe_out(pe, n)
                        pe.wait_ge(own_at.s_y, n + 1)
                        ctx_at.pe_out(pe, n)
                    pe.wait_ge(s_y, b * NG + NG)
                    pr.pe(pe, b, y)

            @block.vector
            def _(dve):
                own_at.clear(dve)
                ctx_at.clear(dve)
                with dve.Fori(0, B) as b:
                    ln.stats(dve, b, b)
                    ln.scale(dve, b, b)
                    ln.keep(dve, b, bank[:, 6:8, :])
                    with dve.Fori(0, NG) as g:
                        n = b * NG + g
                        dve.wait_ge(s_w, n * 64 + 64)
                        for a, (to, col) in enumerate(((qT, 0), (kT, 1), (cqT, 2))):
                            dve.wait_ge(s_p, n * 4 + a + 1)
                            dve.tensor_scalar(to[:], bank[:, a, :], bcol[:, col:col + 1], None, ALU.add)\
                               .then_inc(s_b, 1)
                        dve.wait_ge(s_p, n * 4 + 4)
                        dve.tensor_tensor(V[:], bank[:, 3, :].rearrange("p (t n) -> p t n", t=TT),
                                          bc(brow[:, 0:SW].unsqueeze(1), [P, TT, SW]), ALU.add).then_inc(s_b, 1)
                        dve.wait_ge(s_cb, n * 5 + 1)
                        for v in range(NCV):
                            kn = P if v < NCV - 1 else CLAST
                            count = min(4, CT - 4 * v)
                            dve.wait_ge(s_cp, n * 5 + v + 2)
                            dve.tensor_tensor(cV[0:kn, 4 * v:4 * v + count, :],
                                              bank[0:kn, v, 0:count * P].rearrange("p (t n) -> p t n", n=P),
                                              bc(brow[0:kn, SW:].unsqueeze(1), [kn, count, SW]), ALU.add)\
                               .then_inc(s_cb, 1)
                        own_at.dve_max(dve, n)
                        ctx_at.dve_max(dve, n)
                        dve.wait_ge(s_b, n * 4 + 4)
                        own_at.dve_queries(dve, n)
                        ctx_at.dve_queries(dve, n)
                        own_at.dve_out(dve, n)
                        ctx_at.dve_out(dve, n)
                        yg = y[:, :, bass.ds(g * 4 * HD, 4 * HD)]
                        own_at.dve_divide(dve, n, yg.rearrange("p t (h f) -> p t h f", f=HD))
                        ctx_at.dve_divide(dve, n, yc[:].rearrange("p t (h f) -> p t h f", f=HD))
                        dve.wait_ge(ctx_at.s_y, n + 1)
                        dve.tensor_tensor(yg, yg, yc[:], ALU.add).then_inc(s_y, 1)
                    pr.dve(dve, b, b)

            @block.scalar
            def _(act):
                act.preload_act_table_set(EXP_LN)
                with act.Fori(0, B) as b:
                    ln.rstd_of(act, b)
                    with act.Fori(0, NG) as g:
                        n = b * NG + g
                        act.wait_ge(s_w, n * 64 + 64)
                        act.wait_ge(s_cp, n * 5 + 1)
                        act.activation(ckT[:], bank[:, 4:8, :].rearrange("p a n -> p (a n)")[:, 0:LC], ACT.Identity,
                                       bias=bcol[:, 3:4]).then_inc(s_cb, 1)
                        own_at.act_attend(act, n)
                        ctx_at.act_attend(act, n)


def quantized_ffn(nc, k, d):
    ROUND = 1.5 * 2.0 ** 23
    ctx = ExitStack()
    with ctx:
        sb, ps, sem = tools(nc, ctx, "qf")
        ln = Norm(nc, k, sb, sem)
        xq = sb("xq", [P, KD, NT * P])
        wi = sb("wi", [P, FT, D])
        wiq = sb("wiq", [P, KD, F])
        wo = sb("wo", [P, FT, D])
        bi = sb("bi", [P, FT])
        bo = sb("bo", [P, D])
        am, cl, rc, sc, isc = (sb(x, [P, 2, FT]) for x in ("am", "cl", "rc", "sc", "isc"))
        xm, xmf, xa = sb("xm", [P, 1]), sb("xmf", [P, 4]), sb("xa", [P, 1])
        xs, xis = sb("xs", [P, 1]), sb("xis", [P, 1])
        ha, hmf, hs, his = sb("ha", [P, 1]), sb("hmf", [P, 4]), sb("hs", [P, 1]), sb("his", [P, 1])
        hm = sb("hm", [P, B * FT])
        hm1 = sb("hm1", [P, 1])
        isf = sb("isf", [P, FT])
        hT = sb("hT", [P, B, FT, T])
        bank = ps("bank", [P, 8, 512])
        s_w, s_keep, s_wt, s_wtc = sem("w"), sem("keep"), sem("wt"), sem("wtc")
        s_xm, s_xa, s_xq, s_is, s_h, s_g, s_hm, s_hm1, s_ha, s_hq, s_o, s_x = (
            sem(x) for x in ("xm", "xa", "xq", "is", "h", "g", "hm", "hm1", "ha", "hq", "o", "x"))
        c_dve = sem("c_dve")

        with nc.Block() as block:
            @block.sync
            def _(sp):
                sp.dma_start(wi[:], d["qf_wi"].rearrange("(f p) n -> p f n", p=P)).then_inc(s_w, 16)
                sp.dma_start(wo[:], d["qf_wo"].rearrange("(f p) n -> p f n", p=P)).then_inc(s_w, 16)
                sp.dma_start(bi[:], d["qf_bi"]).then_inc(s_w, 16)
                sp.dma_start(bo[:], d["qf_bo"]).then_inc(s_w, 16)

            @block.gpsimd
            def _(pool):
                pool.wait_ge(s_xm, 1)
                pool.partition_all_reduce(xa[:], xm[:], P, RMAX).then_inc(s_xa, 1)
                pool.wait_ge(s_hm1, 1)
                pool.partition_all_reduce(ha[:], hm1[:], P, RMAX).then_inc(s_ha, 1)

            def scales(own, dve, amax, floor_to, rec, scale, inv, top):
                own.link(dve.tensor_scalar(floor_to, amax, 1e-8, None, ALU.max))
                own.link(dve.reciprocal(rec, floor_to))
                dve.tensor_scalar(inv, floor_to, 1.0 / top, None, ALU.mult)
                own.link(dve.tensor_scalar(scale, rec, top, None, ALU.mult))

            def quantize(own, dve, x, scale, low, high):
                own.link(dve.tensor_scalar(x, x, scale, ROUND, ALU.mult, ALU.add))
                own.link(dve.tensor_scalar(x, x, ROUND, high, ALU.subtract, ALU.min))
                own.link(dve.tensor_scalar(x, x, low, None, ALU.max))

            @block.tensor
            def _(pe):
                with pe.Fori(0, B) as b:
                    pe.wait_ge(s_keep, b)
                    ln.turn(pe, b, bank[:, 6:8, :])
                pe.wait_ge(s_wt, 1)
                for f in range(FT):
                    for h in range(KD):
                        mm = pe.transpose(bank[:, 2 * h + f // 4, (f % 4) * P:(f % 4 + 1) * P],
                                          wi[:, f, h * P:(h + 1) * P], k.ident[:])
                mm.then_inc(s_wtc, 1)
                pe.wait_ge(s_wtc, 2)
                pe.wait_ge(s_xq, 1)
                for b in range(B):
                    for f in range(FT):
                        i = b * FT + f
                        if i >= 4:
                            pe.wait_ge(s_g, i - 3)
                        for h in range(KD):
                            mm = pe.matmul(bank[:, 4 + i % 4, :], wiq[:, h, f * P:(f + 1) * P],
                                           xq[:, h, b * T:(b + 1) * T], start=h == 0, stop=h == KD - 1)
                        mm.then_inc(s_h, 1)
                for t in range(NT):
                    if t % TT == 0:
                        pe.wait_ge(s_hq, t // TT + 1)
                    if t >= 8:
                        pe.wait_ge(s_x, t - 7)
                    for f in range(FT):
                        mm = pe.matmul(bank[:, t % 8, 0:D], hT[:, t // TT, f, (t % TT) * P:(t % TT + 1) * P],
                                       wo[:, f, :], start=f == 0, stop=f == FT - 1)
                    mm.then_inc(s_o, 1)

            @block.vector
            def _(dve):
                own = Chain(dve, c_dve, 34)
                with dve.Fori(0, B) as b:
                    ln.stats(dve, b, b)
                    ln.scale(dve, b, b)
                    ln.keep(dve, b, bank[:, 6:8, :])
                    dve.wait_ge(ln.s_xT, b + 1)
                    dve.tensor_copy(xq[:, :, bass.ds(b * T, T)], ln.xT[:])
                    dve.reduce_max(xmf[:, bass.ds(b, 1)], ln.xT[:], axis=mybir.AxisListType.XY,
                                   apply_absolute_value=True).then_inc(s_keep, 1)
                    dve.wait_ge(s_keep, b + 1)
                own.begin(0)
                dve.wait_ge(s_keep, B)
                dve.reduce_max(xm[:], xmf[:], axis=AX).then_inc(s_xm, 1)
                dve.wait_ge(s_w, 64)
                dve.reduce_max(am[:, 0], wi[:], axis=AX, apply_absolute_value=True)
                own.link(dve.reduce_max(am[:, 1], wo[:], axis=AX, apply_absolute_value=True))
                scales(own, dve, am[:], cl[:], rc[:], sc[:], isc[:], 127.0)
                for f in range(FT):
                    for w, a in ((wi, 0), (wo, 1)):
                        ins = dve.tensor_scalar(w[:, f, :], w[:, f, :], sc[:, a, f:f + 1], ROUND, ALU.mult, ALU.add)
                own.link(ins)
                for w in (wi, wo):
                    ins = dve.tensor_scalar(w[:], w[:], ROUND, 127.0, ALU.subtract, ALU.min)
                own.link(ins)
                own.link(dve.tensor_scalar(wo[:], wo[:], -128.0, None, ALU.max))
                dve.tensor_scalar(wi[:], wi[:], -128.0, None, ALU.max).then_inc(s_wt, 1)
                for f in range(FT):
                    ins = dve.tensor_scalar(wo[:, f, :], wo[:, f, :], isc[:, 1, f:f + 1], None, ALU.mult)
                own.link(ins)
                dve.wait_ge(s_wtc, 1)
                dve.tensor_copy(wiq[:], bank[:, 0:4, :].rearrange("p (h a) n -> p h (a n)", h=KD)).then_inc(s_wtc, 1)
                dve.wait_ge(s_xa, 1)
                scales(own, dve, xa[:], xm[:], xis[:], xs[:], his[:], 32767.0)
                dve.tensor_scalar(isf[:], isc[:, 0], his[:], None, ALU.mult).then_inc(s_is, 1)
                flat = xq[:].rearrange("p h n -> p (h n)")
                quantize(own, dve, flat, xs[:], -32768.0, 32767.0)
                own.link(dve.memset(xm[:], 0.0))
                dve.memset(xm[:], 0.0).then_inc(s_xq, 1)
                for i in range(B * FT):
                    dve.wait_ge(s_g, i + 1)
                    dve.reduce_max(hm[:, i:i + 1], hT[:, i // FT, i % FT, :], axis=AX,
                                   apply_absolute_value=True).then_inc(s_hm, 1)
                dve.wait_ge(s_hm, B * FT)
                dve.reduce_max(hm1[:], hm[:], axis=AX).then_inc(s_hm1, 1)
                for t in range(TT * B // 4):
                    own.link(dve.tensor_tensor(k.x[:, 4 * t:4 * t + 4, :], k.x[:, 4 * t:4 * t + 4, :],
                                               bc(bo[:].unsqueeze(1), [P, 4, D]), ALU.add))
                dve.wait_ge(s_ha, 1)
                scales(own, dve, ha[:], hmf[:, 0:1], hmf[:, 1:2], hs[:], his[:], 32767.0)
                for b in range(B):
                    h = hT[:, b].rearrange("p f n -> p (f n)")
                    own.link(dve.tensor_scalar(h, h, hs[:], ROUND, ALU.mult, ALU.add))
                    own.link(dve.tensor_scalar(h, h, ROUND, 32767.0, ALU.subtract, ALU.min))
                    own.link(dve.tensor_scalar(h, h, -32768.0, his[:], ALU.max, ALU.mult))
                    dve.memset(xm[:], 0.0).then_inc(s_hq, 1)
                for t in range(NT):
                    dve.wait_ge(s_o, t + 1)
                    dve.tensor_tensor(k.x[:, t, :], bank[:, t % 8, 0:D], k.x[:, t, :], ALU.add).then_inc(s_x, 1)
                dve.wait_ge(s_x, NT)
                own.end()

            @block.scalar
            def _(act):
                act.preload_act_table_set(EXP_LN)
                with act.Fori(0, B) as b:
                    ln.rstd_of(act, b)
                act.wait_ge(s_is, 1)
                for b in range(B):
                    for f in range(FT):
                        i = b * FT + f
                        act.wait_ge(s_h, i + 1)
                        act.activation(hT[:, b, f, :], bank[:, 4 + i % 4, :], ACT.Gelu, bias=bi[:, f:f + 1],
                                       scale=isf[:, f:f + 1]).then_inc(s_g, 1)


STAGES = [gated_attention, context_attention, experts, self_attention, cross_attention, quantized_ffn]


def program(nc, d, out, stages):
    k = Core()
    ctx = ExitStack()
    with ctx:
        constants(nc, k, d["x"], ctx)
        for stage in stages:
            taken = nc.snapshot_sems()
            stage(nc, k, d)
            nc.all_engine_barrier()
            nc.clear_and_free_semaphores(nc.allocated_since(taken))
            nc.all_engine_barrier()
        stored = nc.alloc_semaphore("stored")
        with nc.Block() as block:
            @block.sync
            def _(sp):
                sp.dma_start(out.rearrange("b (t p) d -> p (b t) d", p=P), k.x[:]).then_inc(stored, 16)
                sp.wait_ge(stored, 16)


def layout(i):
    f = {n: np.asarray(a) for n, a in i.items()}
    d = {"x": f["x"]}
    wq, wk, wv = f["L0_attn_Wq"], f["L0_attn_Wk"], f["L0_attn_Wv"]
    d["ga_w"] = np.stack([np.concatenate(
        [wq[:, 256 * j:256 * j + 256], wk[:, 64 * j:64 * j + 64], wk[:, 64 * j:64 * j + 64],
         wv[:, 64 * j:64 * j + 64], f["L0_attn_Wa"][:, 4 * j:4 * j + 4], f["L0_attn_Walpha"][:, 4 * j:4 * j + 4],
         f["L0_attn_Wb"][:, j:j + 1]], 1) for j in range(HKV)])
    c = f["L0_attn_Wconv"]
    d["ga_taps"] = np.stack([np.stack(
        [c[256 * j:256 * j + 128], c[256 * j + 128:256 * j + 256],
         np.concatenate([c[1024 + 64 * j:1088 + 64 * j]] * 2), np.concatenate([c[1280 + 64 * j:1344 + 64 * j]] * 2)],
        1) for j in range(HKV)])
    d["ga_rows"] = np.stack([np.tile(np.concatenate(
        [f["L0_attn_A_log"][4 * j:4 * j + 4], f["L0_attn_dt_bias"][4 * j:4 * j + 4]])[None], (P, 1))
        for j in range(HKV)])
    d["ga_wo"] = f["L0_attn_Wo"].reshape(HKV, 256, D)
    d["ga_normw"] = np.tile(f["L0_attn_norm_w"], 2)[:, None]
    d["ctxT"] = f["ctx_512"].transpose(0, 2, 1)
    d["ca_wq"], d["ca_wk"], d["ca_wv"] = (f[f"L0_xattn_W{x}"] for x in "qkv")
    d["ca_bq"], d["ca_bk"] = (f[f"L0_xattn_b{x}"].reshape(KD, P).T for x in "qk")
    d["ca_bv"] = np.tile(f["L0_xattn_bv"], (P, 1))
    d["ex_wr"] = f["L0_ffn_Wr"].T.reshape(KD, P, E).transpose(1, 0, 2)
    d["ex_br"] = np.tile(f["L0_ffn_br"], (P, 1))
    d["ex_b2"] = f["L0_ffn_b2"]
    d["ex_b1"] = f["L0_ffn_b1"].reshape(E, FT, P).transpose(0, 2, 1)
    d["ex_gamma"], d["ex_beta"] = (np.tile(f[f"L0_ffn_{x}"], (P, 1)) for x in ("gamma", "beta"))
    d["ex_w1"] = f["L0_ffn_W1"].transpose(0, 2, 1)
    d["ex_w2"] = f["L0_ffn_W2"].transpose(0, 2, 1)

    def strips(a, one=None):
        a = a.reshape(*a.shape[:-1], 4, HD)
        pad = np.zeros((*a.shape[:-1], SH - HD), a.dtype)
        if one is not None:
            pad[..., 0] = one
        return np.concatenate([a, pad], -1).reshape(*a.shape[:-2], SW)

    wqkv, bqkv = f["L1_attn_Wqkv"].T, f["L1_attn_bqkv"]
    gs = [slice(64 * g, 64 * g + 64) for g in range(NG)]
    at = [slice(256 * a, 256 * a + 256) for a in range(3)]
    d["sa_w"] = np.stack([np.concatenate([wqkv[:, at[0]][:, g], wqkv[:, at[1]][:, g], strips(wqkv[:, at[2]][:, g])], 1)
                          for g in gs])
    d["sa_b"] = np.stack([np.tile(np.concatenate([bqkv[at[0]][g], bqkv[at[1]][g], strips(bqkv[at[2]][g], 1)]), (P, 1))
                          for g in gs])
    d["sa_nw"] = np.tile(np.concatenate([np.tile(f["L1_attn_qn_w"], 4), np.tile(f["L1_attn_kn_w"], 4)]), (P, 1))
    d["sa_wp"] = f["L1_attn_Wproj"].T
    d["sa_bp"] = np.tile(f["L1_attn_bproj"], (P, 1))
    x = {n: f[f"L1_xattn_{n}"] for n in ("Wq", "bq", "Wk", "bk", "Wv", "bv", "Wcq", "bcq", "Wck", "bck", "Wcv", "bcv")}
    d["xa_w"] = np.stack([np.concatenate([strips(x[n][:, g]) for n in ("Wq", "Wk", "Wv", "Wcq")], 1) for g in gs])
    d["xa_wc"] = np.stack([np.concatenate([strips(x["Wck"][:, g]), strips(x["Wcv"][:, g])], 1) for g in gs])
    d["xa_bcol"] = np.stack([np.stack([strips(x["bq"][g]), strips(x["bk"][g], 1), strips(x["bcq"][g]),
                                       strips(x["bck"][g], 1)], 1) for g in gs])
    d["xa_brow"] = np.stack([np.tile(np.concatenate([strips(x["bv"][g], 1), strips(x["bcv"][g], 1)]), (P, 1))
                             for g in gs])
    d["xa_wp"] = f["L1_xattn_Wp"]
    d["xa_bp"] = np.tile(f["L1_xattn_bp"], (P, 1))
    d["qf_wi"] = f["L1_ffn_W_in"].T
    d["qf_wo"] = f["L1_ffn_W_out"]
    d["qf_bi"] = f["L1_ffn_b_in"].reshape(FT, P).T
    d["qf_bo"] = np.tile(f["L1_ffn_b_out"], (P, 1))
    return {n: np.ascontiguousarray(a) for n, a in d.items()}


def kernel(**inputs):
    import concourse.bacc as _bacc
    from concourse.bass_utils import run_bass_kernel_spmd as _run

    nc = _bacc.Bacc("TRN2", target_bir_lowering=False, num_devices=1)
    d = layout(inputs)
    arrays = {f"in_{n}": a for n, a in d.items()}
    aps = {n: nc.dram_tensor(f"in_{n}", a.shape, mybir.dt.from_np(a.dtype), kind="ExternalInput").ap()
           for n, a in d.items()}
    out = nc.dram_tensor("out_x", (B, T, D), F32, kind="ExternalOutput").ap()
    program(nc, aps, out, STAGES)
    r = _run(nc, [arrays], core_ids=[0])
    return r.results[0]["out_x"]
```

```python
from contextlib import ExitStack

import numpy as np
import concourse.bass as bass
from concourse import mybir

F32 = mybir.dt.float32
BF16 = mybir.dt.bfloat16
ALU = mybir.AluOpType
ACT = mybir.ActivationFunctionType
AX = mybir.AxisListType.X
RMAX = bass.bass_isa.ReduceOp.max

P = 128
B, T, D = 4, 512, 256
TT = T // P
NT = B * TT
KD = D // P
LN_EPS = 1e-5
EPS = 1e-6
EXP_LN = "natural_log_exp_and_others"
NEG = -1e30
PRIMED = 1

HQ, HKV, HK, KW = 16, 4, 64, 4
G4 = HQ // HKV
CW = G4 * HK + 3 * HK
SMALL = 2 * G4 + 1
DAMP = 0.25

LC, CD = 1601, 128
CT = -(-LC // P)
CLAST = LC - (CT - 1) * P

H, HD, SH = 16, 16, 32
NG = 4
SW = 4 * SH

E, F = 8, 1024
FT = F // P


class Chain:

    def __init__(self, eng, sem, per):
        self.eng, self.sem, self.per, self.n, self.k = eng, sem, per, 0, 0

    def begin(self, n):
        self.n, self.k = n, 0

    def done(self, ins):
        ins.then_inc(self.sem, 1)
        self.k += 1

    def wait(self):
        self.eng.wait_ge(self.sem, self.n * self.per + self.k)

    def link(self, ins):
        self.done(ins)
        self.wait()

    def end(self):
        assert self.k == self.per, (self.sem, self.k)


class Core:
    pass


def bc(ap, shape):
    return ap.to_broadcast(shape)


def tools(nc, ctx, stage):
    def sb(name, shape, dt=F32):
        return ctx.enter_context(nc.sbuf_tensor(f"{stage}_{name}", shape, dt))

    def ps(name, shape, dt=F32):
        return ctx.enter_context(nc.psum_tensor(f"{stage}_{name}", shape, dt))

    def sem(name):
        return nc.alloc_semaphore(f"{stage}_{name}")

    return sb, ps, sem


def constants(nc, k, x_in, ctx):
    sb, ps, sem = tools(nc, ctx, "c")
    k.x = sb("x", [P, NT, D])
    k.ident = sb("ident", [P, P])
    k.identb = sb("identb", [P, P], BF16)
    k.mask_kq = sb("mask_kq", [P, P], BF16)
    k.mask_qk = sb("mask_qk", [P, P], BF16)
    k.tri = sb("tri", [P, P])
    k.ln_eps = sb("ln_eps", [P, 1])
    k.eps = sb("eps", [P, 1])
    k.tiny = sb("tiny", [P, 1])
    loaded, filled, made = sem("loaded"), sem("filled"), sem("made")
    with nc.Block() as block:
        @block.sync
        def _(sp):
            sp.dma_start(k.x[:], x_in.rearrange("b (t p) d -> p (b t) d", p=P)).then_inc(loaded, 16)
            sp.wait_ge(loaded, 16)

        @block.gpsimd
        def _(pool):
            for tile, value in ((k.ident, 0.0), (k.identb, 0.0), (k.mask_kq, 0.0), (k.mask_qk, 0.0), (k.tri, 1.0),
                                (k.ln_eps, LN_EPS), (k.eps, EPS), (k.tiny, 1e-18)):
                pool.memset(tile[:], value).then_inc(filled, 1)
            pool.wait_ge(filled, 8)
            for tile in (k.ident, k.identb):
                pool.affine_select(out=tile[:], in_=tile[:], compare_op=ALU.not_equal, fill=1.0, base=0,
                                   pattern=[[-1, P]], channel_multiplier=1).then_inc(made, 1)
            for tile, fill in ((k.mask_kq, NEG), (k.tri, 0.0)):
                pool.affine_select(out=tile[:], in_=tile[:], compare_op=ALU.is_ge, fill=fill, base=0,
                                   pattern=[[1, P]], channel_multiplier=-1).then_inc(made, 1)
            pool.affine_select(out=k.mask_qk[:], in_=k.mask_qk[:], compare_op=ALU.is_ge, fill=NEG, base=0,
                               pattern=[[-1, P]], channel_multiplier=1).then_inc(made, 1)
            pool.wait_ge(made, 5)


class Norm:

    def __init__(self, nc, k, sb, sem):
        self.nc, self.k = nc, k
        self.st = sb("ln_st", [P, TT, 6])
        self.mv = sb("ln_mv", [P, TT, 2])
        self.spare = sb("ln_spare", [P, 1])
        self.lnv = sb("ln_lnv", [P, TT])
        self.rstd = sb("ln_rstd", [P, TT])
        self.xn = sb("ln_xn", [P, TT, D])
        self.xT = sb("ln_xT", [P, KD, T])
        self.s_bn, self.s_mv, self.s_ln, self.s_rstd = (sem(f"ln_{x}") for x in ("bn", "mv", "log", "rstd"))
        self.s_xn, self.s_turned, self.s_xT = (sem(f"ln_{x}") for x in ("xn", "turned", "xT"))

    def stats(self, dve, b, n):
        for t in range(TT):
            dve.bn_stats(self.st[:, t, :], self.k.x[:, b * TT + t, :]).then_inc(self.s_bn, 1)
        dve.wait_ge(self.s_bn, n * TT + TT)
        dve.memset(self.spare[:], 0.0)
        for t in range(TT):
            dve.bn_aggr(self.mv[:, t, :], self.st[:, t, :]).then_inc(self.s_mv, 1)

    def rstd_of(self, act, n):
        act.wait_ge(self.s_mv, n * TT + TT)
        act.activation(self.lnv[:], self.mv[:, :, 1], ACT.Ln, bias=self.k.ln_eps[:]).then_inc(self.s_ln, 1)
        act.wait_ge(self.s_ln, n + 1)
        act.activation(self.rstd[:], self.lnv[:], ACT.Exp, scale=-0.5).then_inc(self.s_rstd, 1)

    def scale(self, dve, b, n):
        dve.wait_ge(self.s_rstd, n + 1)
        for t in range(TT):
            dve.tensor_scalar(self.xn[:, t, :], self.k.x[:, b * TT + t, :], self.mv[:, t, 0:1],
                              self.rstd[:, t:t + 1], ALU.subtract, ALU.mult).then_inc(self.s_xn, 1)

    def turn(self, pe, n, two_banks):
        pe.wait_ge(self.s_xn, n * TT + TT)
        for h in range(KD):
            for t in range(TT):
                pe.transpose(two_banks[:, h, t * P:(t + 1) * P], self.xn[:, t, h * P:(h + 1) * P],
                             self.k.ident[:]).then_inc(self.s_turned, 1)

    def keep(self, dve, n, two_banks):
        dve.wait_ge(self.s_turned, n * TT * KD + TT * KD)
        dve.tensor_copy(self.xT[:], two_banks[:]).then_inc(self.s_xT, 1)


def gated_attention(nc, k, d):
    ctx = ExitStack()
    with ctx:
        sb, ps, sem = tools(nc, ctx, "ga")
        ln = Norm(nc, k, sb, sem)
        w = sb("w", [P, KD, CW + SMALL])
        taps = sb("taps", [P, 4, KW])
        rows = sb("rows", [P, 2 * G4])
        wo = sb("wo", [P, 2, D])
        wos = sb("wos", [P, 2, D])
        normw = sb("normw", [P, 1])
        cv = sb("cv", [P, 4, T])
        small = sb("small", [P, TT, SMALL])
        z, az, e1, l1, sp_ = (sb(x, [P, TT, G4]) for x in ("z", "az", "e1", "l1", "sp"))
        ea = sb("ea", [P, G4])
        eab = sb("eab", [P, TT, G4 + 1])
        den = sb("den", [P, TT, G4 + 1])
        gates = sb("gates", [P, TT, G4 + 1])
        alpha = sb("alpha", [P, TT, G4])
        g = sb("g", [P, TT, G4])
        gd = sb("gd", [P, TT, G4, HK])
        negG = sb("negG", [P, TT, G4])
        X0 = sb("X0", [P, TT, 2, P])
        X1 = sb("X1", [P, TT, 2, P])
        Xs = sb("Xs", [P, TT, 2, P])
        kT = sb("kT", [P, T])
        vT = sb("vT", [HK, T])
        sq = sb("sq", [P, G4 * TT * HK])
        ssk, lnk, nk, nke, rk = (sb(x, [P, TT]) for x in ("ssk", "lnk", "nk", "nke", "rk"))
        KKV = sb("KKV", [P, TT, 3 * HK])
        kTn = sb("kTn", [P, TT, P])
        Ed = sb("Ed", [P, TT, 2, P])
        Dm = sb("Dm", [P, 2, 2, 2, 2, P])
        KVw = sb("KVw", [P, TT - 1, 2, 2, 2 * HK])
        Hs = sb("Hs", [P, TT - 1, 2, 2 * HK])
        Wm = sb("Wm", [P, 2, 2, 2, 2, P])
        o = sb("o", [P, TT, G4, HK])
        on = sb("on", [P, TT, G4, HK])
        sso, lno, ro = (sb(x, [P, TT * G4]) for x in ("sso", "lno", "ro"))
        oT = sb("oT", [P, 2, TT, P])
        bank = ps("bank", [P, 8, 512])

        s_w, s_t, s_r, s_wo, s_nw = (sem(x) for x in ("w", "taps", "rows", "wo", "normw"))
        s_proj, s_small, s_conv, s_smallc, s_az, s_es, s_l1 = (
            sem(x) for x in ("proj", "small", "conv", "smallc", "az", "es", "l1"))
        s_g, s_G, s_Gc, s_E, s_Ee, s_D, s_De = (sem(x) for x in ("g", "G", "Gc", "E", "Ee", "D", "De"))
        s_silu, s_kvt, s_ssk, s_nk, s_kn, s_v, s_kT, s_kTc = (
            sem(x) for x in ("silu", "kvt", "ssk", "nk", "kn", "v", "kT", "kTc"))
        s_KVw, s_st, s_H, s_W, s_Wm, s_Y, s_X, s_Xs = (
            sem(x) for x in ("KVw", "st", "H", "W", "Wm", "Y", "X", "Xs"))
        s_O, s_o, s_sq, s_ss, s_ro, s_on, s_oT, s_oTc, s_out, s_x = (
            sem(x) for x in ("O", "o", "sq", "ss", "ro", "on", "oT", "oTc", "out", "x"))
        s_gd, s_wos, c_dve, c_act = sem("gd"), sem("wos"), sem("c_dve"), sem("c_act")

        turned = bank[:, 6:8, :]
        kps = bank[:, 4, :].rearrange("p (c f) -> p c f", c=TT)
        vps = bank[:, 5, 0:TT * HK].rearrange("p (c f) -> p c f", c=TT)
        Eps = bank[:, 6:8, :].rearrange("p a (c i t) -> p (a c) i t", c=2, i=2)
        st = bank[:, 6:8, :].rearrange("p a (c i f) -> p (a c) i f", c=2, i=2)

        def pair(cc):
            return bank[:, 2 * cc:2 * cc + 2, :].rearrange("p q (c i t) -> p q c i t", c=2, i=2)

        def Y(cc):
            return bank[:, 4 + cc, :].rearrange("p (c i t) -> p c i t", c=2, i=2)

        O = bank[:, 6:8, :].rearrange("p q (c i f) -> p q c i f", c=TT, i=2)

        with nc.Block() as block:
            @block.sync
            def _(sp):
                sp.dma_start(normw[:], d["ga_normw"]).then_inc(s_nw, 16)
                with sp.Fori(0, B) as b:
                    with sp.Fori(0, HKV) as j:
                        n = b * HKV + j
                        sp.wait_ge(s_small, n + PRIMED)
                        sp.dma_start(w[:], d["ga_w"][j].rearrange("(h p) n -> p h n", p=P)).then_inc(s_w, 16)
                        sp.wait_ge(s_conv, n * 4 + PRIMED)
                        sp.dma_start(taps[:], d["ga_taps"][j]).then_inc(s_t, 16)
                        sp.wait_ge(s_g, n + PRIMED)
                        sp.dma_start(rows[:], d["ga_rows"][j]).then_inc(s_r, 16)
                        sp.wait_ge(s_wos, n + PRIMED)
                        sp.dma_start(wo[:], d["ga_wo"][j].rearrange("(h p) n -> p h n", p=P)).then_inc(s_wo, 16)

            @block.tensor
            def _(pe):
                pe.sem_inc(s_small, PRIMED)
                with pe.Fori(0, B) as b:
                    pe.wait_ge(s_x, b * HKV + PRIMED)
                    ln.turn(pe, b, turned)
                    with pe.Fori(0, HKV) as j:
                        n = b * HKV + j
                        pe.wait_ge(ln.s_xT, b + 1)
                        pe.wait_ge(s_w, n * 16 + 16)
                        pe.wait_ge(s_x, n + PRIMED)
                        for m in (2, 3, 0, 1):
                            M = P if m < 3 else HK
                            for h in range(KD):
                                mm = pe.matmul(bank[0:M, m, :], w[:, h, m * P:m * P + M], ln.xT[:, h, :],
                                               start=h == 0, stop=h == KD - 1)
                            mm.then_inc(s_proj, 1)
                        for t in range(TT):
                            for h in range(KD):
                                mm = pe.matmul(bank[:, 4, t * 16:t * 16 + SMALL], ln.xT[:, h, t * P:(t + 1) * P],
                                               w[:, h, CW:], start=h == 0, stop=h == KD - 1)
                        mm.then_inc(s_small, 1)
                        pe.wait_ge(s_silu, n * 4 + 2)
                        pe.wait_ge(s_smallc, n + 1)
                        for c in range(TT):
                            pe.transpose(kps[:, c, :], kT[:, c * P:(c + 1) * P], k.ident[:]).then_inc(s_kvt, 1)
                        for c in range(TT):
                            pe.transpose(vps[:, c, :], vT[:, c * P:(c + 1) * P], k.ident[0:HK, 0:HK])\
                              .then_inc(s_kvt, 1)
                        pe.wait_ge(s_g, n + 1 + PRIMED)
                        pe.wait_ge(s_silu, n * 4 + 4)
                        pe.wait_ge(s_conv, n * 4 + 4 + PRIMED)
                        pe.matmul(bank[:, 3, 0:TT * G4], k.tri[:], g[:].rearrange("p c h -> p (c h)"),
                                  start=True, stop=True).then_inc(s_G, 1)
                        pe.wait_ge(s_gd, n + 1)
                        for c in range(TT):
                            for i in range(2):
                                pe.matmul(Eps[:, c, i, :], gd[:, c, 2 * i:2 * i + 2, :].rearrange("p a f -> p (a f)"),
                                          k.tri[:], start=True, stop=True).then_inc(s_E, 1)
                        for cc in range(2):
                            if cc == 1:
                                pe.wait_ge(s_Gc, n + 1)
                            for q in range(2):
                                pe.matmul(bank[:, 2 * cc + q, :], k.identb[:],
                                          bc(k.mask_kq[:].unsqueeze(1), [P, 4, P]), start=True, stop=False)
                                for c in range(2):
                                    for i in range(2):
                                        mm = pe.matmul(pair(cc)[:, q, c, i, :],
                                                       bc(g[:, 2 * cc + c, 2 * i + q:2 * i + q + 1], [P, P]),
                                                       k.tri[:], start=False, stop=c == 1 and i == 1)
                            mm.then_inc(s_D, 1)
                        pe.wait_ge(s_kn, n + 1)
                        for c in range(TT):
                            pe.transpose(kps[:, c, :], KKV[:, c, 0:P], k.ident[:]).then_inc(s_kT, 1)
                        pe.wait_ge(s_Ee, n + 1)
                        for c in range(TT - 1):
                            pe.wait_ge(s_KVw, n * (TT - 1) + c + 1)
                            for q in range(2):
                                mm = pe.matmul(st[q * HK:(q + 1) * HK, c], KKV[:, c, 0:HK],
                                               KVw[:, c, q], start=True, stop=True)
                        mm.then_inc(s_st, 1)
                        pe.wait_ge(s_kTc, n + 1)
                        pe.wait_ge(s_De, n * 2 + 2)
                        for r in range(3):
                            X = X0 if r == 0 else X1
                            for cc in range(2):
                                if r:
                                    pe.wait_ge(s_X, n * 4 + 2 * (r - 1) + cc + 1)
                                for c in range(2 * cc, 2 * cc + 2):
                                    for q in range(2):
                                        part = slice(q * HK, (q + 1) * HK)
                                        mm = pe.matmul(pair(cc)[:, q, c % 2], kTn[part, c, :], X[part, c],
                                                       start=True, stop=True)
                                mm.then_inc(s_W, 1)
                            for cc in range(2):
                                pe.wait_ge(s_Wm, n * 6 + 2 * r + cc + 1)
                                if cc == 0:
                                    pe.wait_ge(s_H, n + 1)
                                    pe.wait_ge(s_Xs, n * 6 + 2 * r + 1)
                                else:
                                    pe.wait_ge(s_Xs, n * 6 + 2 * r + 2)
                                for c in range(2 * cc, 2 * cc + 2):
                                    for q in range(2):
                                        part = slice(q * HK, (q + 1) * HK)
                                        if r < 2:
                                            mm = pe.matmul(Y(cc)[part, c % 2], KKV[:, c, 0:HK],
                                                           Wm[:, cc, q, c % 2], start=True, stop=c == 0)
                                            for i in range(2 if c else 0):
                                                mm = pe.matmul(Y(cc)[part, c % 2, i, :], Hs[part, c - 1, i, 0:HK],
                                                               Xs[part, c, i, :], start=False, stop=i == 1)
                                        else:
                                            for i in range(2):
                                                mm = pe.matmul(O[:, q, c, i, :], Wm[:, cc, q, c % 2, i, :],
                                                               KKV[:, c, P:], start=True, stop=c == 0)
                                                if c:
                                                    mm = pe.matmul(O[:, q, c, i, :], Xs[part, c, i, :],
                                                                   Hs[part, c - 1, i, HK:], start=False, stop=True)
                                mm.then_inc(s_Y if r < 2 else s_O, 1)
                        pe.wait_ge(s_on, n + 1)
                        for h in range(2):
                            for c in range(TT):
                                pe.transpose(bank[:, h, c * P:(c + 1) * P],
                                             on[:, c, 2 * h:2 * h + 2, :].rearrange("p a f -> p (a f)"),
                                             k.ident[:]).then_inc(s_oT, 1)
                        pe.wait_ge(s_oTc, n + 1)
                        pe.wait_ge(s_wos, n + 1 + PRIMED)
                        for c in range(TT):
                            for h in range(2):
                                mm = pe.matmul(bank[:, 2 + c // 2, (c % 2) * D:(c % 2 + 1) * D], oT[:, h, c, :],
                                               wos[:, h, :], start=h == 0, stop=h == 1)
                        mm.then_inc(s_out, 1)

            @block.vector
            def _(dve):
                dve.sem_inc(s_conv, PRIMED)
                dve.sem_inc(s_g, PRIMED)
                dve.sem_inc(s_wos, PRIMED)
                dve.sem_inc(s_x, PRIMED)
                own = Chain(dve, c_dve, 11)
                dve.wait_ge(s_nw, 16)
                with dve.Fori(0, B) as b:
                    dve.wait_ge(s_x, b * HKV + PRIMED)
                    ln.stats(dve, b, b)
                    ln.scale(dve, b, b)
                    ln.keep(dve, b, turned)
                    with dve.Fori(0, HKV) as j:
                        n = b * HKV + j
                        own.begin(n)
                        dve.wait_ge(s_t, n * 16 + 16)
                        order = (2, 3, 0, 1)
                        for at, m in enumerate(order):
                            M = P if m < 3 else HK
                            dve.wait_ge(s_proj, n * 4 + at + 1)
                            ins = dve.tensor_scalar(cv[0:M, m, :], bank[0:M, m, :], taps[0:M, m, KW - 1:KW], None,
                                                    ALU.mult)
                            if at == 3:
                                own.link(ins)
                        for lag in range(1, KW):
                            for at, m in enumerate(order):
                                M = P if m < 3 else HK
                                ins = dve.scalar_tensor_tensor(
                                    cv[0:M, m, lag:], bank[0:M, m, 0:T - lag], taps[0:M, m, KW - 1 - lag:KW - lag],
                                    cv[0:M, m, lag:], ALU.mult, ALU.add)
                                if lag == KW - 1:
                                    ins.then_inc(s_conv, 1)
                                elif at == 3:
                                    own.link(ins)
                        dve.wait_ge(s_small, n + 1 + PRIMED)
                        dve.tensor_copy(small[:], bank[:, 4, 0:TT * 16].rearrange("p (t s) -> p t s", t=TT)
                                        [:, :, 0:SMALL]).then_inc(s_smallc, 1)
                        dve.wait_ge(s_smallc, n + 1)
                        dve.wait_ge(s_r, n * 16 + 16)
                        own.link(dve.tensor_tensor(z[:], small[:, :, 0:G4],
                                                   bc(rows[:, G4:].unsqueeze(1), [P, TT, G4]), ALU.add))
                        dve.scalar_tensor_tensor(az[:], z[:], -1.0, z[:], ALU.mult, ALU.max).then_inc(s_az, 1)
                        dve.wait_ge(s_es, n + 1)
                        own.link(dve.tensor_scalar(den[:], eab[:], 1.0, None, ALU.add))
                        own.link(dve.reciprocal(gates[:], den[:]))
                        dve.tensor_scalar(alpha[:], gates[:, :, 0:G4], HK ** -0.5, None, ALU.mult)
                        dve.wait_ge(s_l1, n + 1)
                        own.link(dve.scalar_tensor_tensor(sp_[:], z[:], 0.0, l1[:], ALU.max, ALU.add))
                        dve.scalar_tensor_tensor(g[:], sp_[:], -1.0, bc(ea[:].unsqueeze(1), [P, TT, G4]),
                                                 ALU.mult, ALU.mult).then_inc(s_g, 1)
                        dve.wait_ge(s_g, n + 1 + PRIMED)
                        dve.tensor_copy(gd[:], bc(g[:].unsqueeze(3), [P, TT, G4, HK])).then_inc(s_gd, 1)
                        dve.wait_ge(s_kvt, n * 8 + 8)
                        dve.tensor_tensor(KKV[:, :, P:], vps, bc(gates[:, :, G4:], [P, TT, HK]), ALU.mult)\
                           .then_inc(s_v, 1)
                        dve.wait_ge(s_nk, n + 1)
                        own.link(dve.tensor_scalar(nke[:], nk[:], EPS, None, ALU.add))
                        own.link(dve.reciprocal(rk[:], nke[:]))
                        dve.tensor_tensor(KKV[:, :, 0:P], kps, bc(rk[:].unsqueeze(2), [P, TT, P]), ALU.mult)\
                           .then_inc(s_kn, 1)
                        dve.wait_ge(s_G, n + 1)
                        dve.tensor_scalar(negG[:].rearrange("p c h -> p (c h)"), bank[:, 3, 0:TT * G4], -1.0, None,
                                          ALU.mult).then_inc(s_Gc, 1)
                        dve.wait_ge(s_wo, n * 16 + 16)
                        dve.tensor_scalar(wos[:], wo[:], normw[:], None, ALU.mult).then_inc(s_wos, 1)
                        dve.wait_ge(s_kn, n + 1)
                        dve.wait_ge(s_v, n + 1)
                        for c in range(TT - 1):
                            if c % 2 == 0:
                                dve.wait_ge(s_De, n * 2 + c // 2 + 1)
                            for q in range(2):
                                ins = dve.tensor_tensor(
                                    KVw[:, c, q], bc(KKV[:, c, HK:].unsqueeze(1), [P, 2, P]),
                                    bc(Dm[:, c // 2, q, c % 2, :, P - 1:P], [P, 2, P]), ALU.mult)
                            ins.then_inc(s_KVw, 1)
                        dve.wait_ge(s_silu, n * 4 + 4)
                        dve.tensor_tensor(Xs[:, 1], X0[:, 1], Ed[:, 1], ALU.mult).then_inc(s_Xs, 1)
                        dve.tensor_tensor(Xs[:, 2:4], X0[:, 2:4], Ed[:, 2:4], ALU.mult).then_inc(s_Xs, 1)
                        dve.wait_ge(s_st, n + 1)
                        own.link(dve.tensor_copy(Hs[:, 0], st[:, 0]))
                        for c in range(1, TT - 1):
                            for i in range(2):
                                ins = dve.scalar_tensor_tensor(Hs[:, c, i, :], Hs[:, c - 1, i, :],
                                                               Ed[:, c, i, P - 1:P], st[:, c, i, :],
                                                               ALU.mult, ALU.add)
                            if c == 1:
                                own.link(ins)
                            else:
                                ins.then_inc(s_H, 1)
                        for r in range(3):
                            for cc in range(2):
                                dve.wait_ge(s_W, n * 6 + 2 * r + cc + 1)
                                dve.tensor_tensor(Wm[:, cc], pair(cc), Dm[:, cc], ALU.mult).then_inc(s_Wm, 1)
                            for cc in range(2 if r < 2 else 0):
                                dve.wait_ge(s_Y, n * 4 + 2 * r + cc + 1)
                                dve.scalar_tensor_tensor(
                                    X1[:, 2 * cc:2 * cc + 2].rearrange("p c i t -> p (c i t)"), bank[:, 4 + cc, :],
                                    -DAMP, X0[:, 2 * cc:2 * cc + 2].rearrange("p c i t -> p (c i t)"),
                                    ALU.mult, ALU.add).then_inc(s_X, 1)
                                dve.wait_ge(s_X, n * 4 + 2 * r + cc + 1)
                                lo = max(1, 2 * cc)
                                dve.tensor_tensor(Xs[:, lo:2 * cc + 2], X1[:, lo:2 * cc + 2], Ed[:, lo:2 * cc + 2],
                                                  ALU.mult).then_inc(s_Xs, 1)
                        dve.wait_ge(s_O, n * 2 + 2)
                        for q in range(2):
                            ins = dve.tensor_tensor(o[:, :, q::2, :], O[:, q],
                                                    bc(alpha[:, :, q::2].unsqueeze(3), [P, TT, 2, HK]), ALU.mult)
                        ins.then_inc(s_o, 1)
                        dve.wait_ge(s_sq, n + 1)
                        dve.reduce_sum(sso[:], sq[:].rearrange("p (a f) -> p a f", f=HK), axis=AX).then_inc(s_ss, 1)
                        dve.wait_ge(s_ro, n + 1)
                        dve.tensor_tensor(on[:].rearrange("p c h f -> p (c h) f"),
                                          o[:].rearrange("p c h f -> p (c h) f"),
                                          bc(ro[:].unsqueeze(2), [P, TT * G4, HK]), ALU.mult).then_inc(s_on, 1)
                        dve.wait_ge(s_oT, n * 8 + 8)
                        dve.tensor_copy(oT[:], bank[:, 0:2, :].rearrange("p h (c t) -> p h c t", c=TT))\
                           .then_inc(s_oTc, 1)
                        dve.wait_ge(s_out, n + 1)
                        xb = k.x[:, bass.ds(b * TT, TT), :].rearrange("p t n -> p (t n)")
                        dve.tensor_tensor(xb, bank[:, 2:4, :].rearrange("p a n -> p (a n)"), xb,
                                          ALU.add).then_inc(s_x, 1)
                        dve.wait_ge(s_x, n + 1 + PRIMED)
                        own.end()

            @block.scalar
            def _(act):
                own = Chain(act, c_act, 4)
                with act.Fori(0, B) as b:
                    ln.rstd_of(act, b)
                    with act.Fori(0, HKV) as j:
                        n = b * HKV + j
                        own.begin(n)
                        for at, m in enumerate((2, 3, 0, 1)):
                            act.wait_ge(s_conv, n * 4 + at + 1 + PRIMED)
                            if m < 2:
                                act.activation(X0[:, :, m, :], cv[:, m, :].rearrange("p (c t) -> p c t", c=TT),
                                               ACT.Silu).then_inc(s_silu, 1)
                            else:
                                M, to = (P, kT) if m == 2 else (HK, vT)
                                act.activation(to[:], cv[0:M, m, :], ACT.Silu).then_inc(s_silu, 1)
                        act.preload_act_table_set(EXP_LN)
                        act.wait_ge(s_az, n + 1)
                        own.link(act.activation(e1[:], az[:], ACT.Exp, scale=-1.0))
                        act.activation(ea[:], rows[:, 0:G4], ACT.Exp)
                        act.activation(eab[:], small[:, :, G4:], ACT.Exp, scale=-1.0).then_inc(s_es, 1)
                        act.activation(l1[:], e1[:], ACT.Ln, bias=1.0).then_inc(s_l1, 1)
                        act.wait_ge(s_kvt, n * 8 + 4)
                        for c in range(TT):
                            ins = act.activation(sq[:, c * HK:(c + 1) * HK], kps[:, c, 0:HK], ACT.Square,
                                                 accum_out=ssk[:, c:c + 1])
                        own.link(ins)
                        own.link(act.activation(lnk[:], ssk[:], ACT.Ln, bias=k.tiny[:]))
                        act.activation(nk[:], lnk[:], ACT.Exp, scale=0.5).then_inc(s_nk, 1)
                        act.wait_ge(s_E, n * 8 + 8)
                        act.activation(Ed[:].rearrange("p c i t -> p (c i t)"),
                                       bank[:, 6:8, :].rearrange("p a n -> p (a n)"), ACT.Exp).then_inc(s_Ee, 1)
                        act.wait_ge(s_Gc, n + 1)
                        for cc in range(2):
                            act.wait_ge(s_D, n * 2 + cc + 1)
                            for q in range(2):
                                for c in range(2):
                                    for i in range(2):
                                        h = 2 * i + q
                                        ins = act.activation(Dm[:, cc, q, c, i, :], pair(cc)[:, q, c, i, :], ACT.Exp,
                                                             bias=negG[:, 2 * cc + c, h:h + 1])
                            ins.then_inc(s_De, 1)
                        act.wait_ge(s_kT, n * 4 + 4)
                        act.activation(kTn[:], kps, ACT.Copy).then_inc(s_kTc, 1)
                        act.wait_ge(s_o, n + 1)
                        act.activation(sq[:], o[:].rearrange("p c h f -> p (c h f)"), ACT.Square).then_inc(s_sq, 1)
                        act.wait_ge(s_ss, n + 1)
                        own.link(act.activation(lno[:], sso[:], ACT.Ln, bias=k.eps[:], scale=1.0 / HK))
                        act.activation(ro[:], lno[:], ACT.Exp, scale=-0.5).then_inc(s_ro, 1)
                        own.end()


def context_attention(nc, k, d):
    ctx = ExitStack()
    with ctx:
        sb, ps, sem = tools(nc, ctx, "ca")
        ln = Norm(nc, k, sb, sem)
        wq = sb("wq", [P, KD, D])
        wk, wv = sb("wk", [P, D]), sb("wv", [P, D])
        bq, bk = sb("bq", [P, KD]), sb("bk", [P, KD])
        bv = sb("bv", [P, D])
        cT = sb("cT", [P, LC])
        qT = sb("qT", [P, KD, T])
        kT = sb("kT", [P, KD, LC])
        V = sb("V", [P, CT + 1, D])
        Pr = sb("Pr", [P, LC])
        PT = sb("PT", [P, CT, P])
        nm = sb("nm", [P, NT])
        rsum, rinv = sb("rsum", [P, TT]), sb("rinv", [P, TT])
        bank = ps("bank", [P, 8, 512])
        s_w, s_c = sem("w"), sem("c")
        s_kp, s_k, s_qp, s_q, s_vp, s_v = (sem(x) for x in ("kp", "k", "qp", "q", "vp", "v"))
        s_S, s_m, s_e, s_tp, s_t, s_o, s_r, s_x = (sem(x) for x in ("S", "m", "e", "tp", "t", "o", "r", "x"))
        chunks = [(c * 512, min(512, LC - c * 512)) for c in range(4)]
        groups = [(g * 4, min(4, CT - g * 4)) for g in range(4)]
        VG = (CT + 1) // 2
        vbank = [6, 7, 4, 5]

        with nc.Block() as block:
            @block.sync
            def _(sp):
                sp.dma_start(wk[:], d["ca_wk"]).then_inc(s_w, 16)
                sp.dma_start(bk[:], d["ca_bk"]).then_inc(s_w, 16)
                sp.dma_start(wq[:], d["ca_wq"].rearrange("(h p) n -> p h n", p=P)).then_inc(s_w, 16)
                sp.dma_start(bq[:], d["ca_bq"]).then_inc(s_w, 16)
                sp.dma_start(wv[:], d["ca_wv"]).then_inc(s_w, 16)
                sp.dma_start(bv[:], d["ca_bv"]).then_inc(s_w, 16)
                with sp.Fori(0, B) as b:
                    sp.wait_ge(s_vp, b * VG + PRIMED)
                    sp.dma_start(cT[:], d["ctxT"][b]).then_inc(s_c, 16)

            @block.tensor
            def _(pe):
                pe.sem_inc(s_vp, PRIMED)
                pe.wait_ge(s_w, 6 * 16)
                with pe.Fori(0, B) as b:
                    pe.wait_ge(s_x, b * TT + PRIMED)
                    pe.wait_ge(s_c, b * 16 + 16)
                    for h in range(KD):
                        if h:
                            pe.wait_ge(s_k, b * 2 + 1)
                        for c, (at, N) in enumerate(chunks):
                            mm = pe.matmul(bank[:, c, 0:N], wk[:, h * P:(h + 1) * P], cT[:, at:at + N],
                                           start=True, stop=True)
                        mm.then_inc(s_kp, 1)
                    ln.turn(pe, b, bank[:, 6:8, :])
                    pe.wait_ge(ln.s_xT, b + 1)
                    for h in range(KD):
                        for g in range(KD):
                            mm = pe.matmul(bank[:, 4 + h, :], wq[:, g, h * P:(h + 1) * P], ln.xT[:, g, :],
                                           start=g == 0, stop=g == KD - 1)
                        mm.then_inc(s_qp, 1)
                    for g in range(VG):
                        if g in (2, 3):
                            pe.wait_ge(s_q, b * 2 + g - 1)
                        if g >= 4:
                            pe.wait_ge(s_v, b * VG + g - 3)
                        for t in range(2 * g, min(2 * g + 2, CT)):
                            kn = P if t < CT - 1 else CLAST
                            mm = pe.matmul(bank[0:kn, vbank[g % 4], (t % 2) * D:(t % 2 + 1) * D],
                                           cT[:, t * P:t * P + kn], wv[:], start=True, stop=True)
                        mm.then_inc(s_vp, 1)
                    pe.wait_ge(s_k, b * 2 + 2)
                    pe.wait_ge(s_q, b * 2 + 2)

                    def scores(t):
                        if t:
                            pe.wait_ge(s_e, b * TT + t)
                        for c, (at, N) in enumerate(chunks):
                            for h in range(KD):
                                mm = pe.matmul(bank[:, c, 0:N], qT[:, h, t * P:(t + 1) * P], kT[:, h, at:at + N],
                                               start=h == 0, stop=h == KD - 1)
                        mm.then_inc(s_S, 1)

                    scores(0)
                    for t in range(TT):
                        if t + 1 < TT:
                            scores(t + 1)
                        pe.wait_ge(s_e, b * TT + t + 1)
                        if t == 0:
                            pe.wait_ge(s_v, b * VG + VG)
                        for g, (at, count) in enumerate(groups):
                            if t or g >= 2:
                                pe.wait_ge(s_t, (b * TT + t) * 4 + g - 1)
                            for a in range(count):
                                kt = at + a
                                kn = P if kt < CT - 1 else CLAST
                                mm = pe.transpose(bank[0:kn, 4 + g % 2, a * P:(a + 1) * P],
                                                  Pr[:, kt * P:kt * P + kn], k.ident[:])
                            mm.then_inc(s_tp, 1)
                        for g, (at, count) in enumerate(groups):
                            pe.wait_ge(s_t, (b * TT + t) * 4 + g + 1)
                            if g == 0 and t:
                                pe.wait_ge(s_x, b * TT + t + PRIMED)
                            for kt in range(at, at + count):
                                kn = P if kt < CT - 1 else CLAST
                                mm = pe.matmul(bank[:, 6, 0:D], PT[0:kn, kt, :], V[0:kn, kt, :],
                                               start=kt == 0, stop=kt == CT - 1)
                        mm.then_inc(s_o, 1)

            @block.vector
            def _(dve):
                dve.sem_inc(s_x, PRIMED)
                dve.wait_ge(s_w, 6 * 16)
                with dve.Fori(0, B) as b:
                    ln.stats(dve, b, b)
                    ln.scale(dve, b, b)
                    ln.keep(dve, b, bank[:, 6:8, :])
                    for g in range(VG):
                        dve.wait_ge(s_vp, b * VG + g + 1 + PRIMED)
                        if g < VG - 1:
                            dve.tensor_tensor(V[:, 2 * g:2 * g + 2, :],
                                              bank[:, vbank[g % 4], :].rearrange("p (a n) -> p a n", a=2),
                                              bc(bv[:].unsqueeze(1), [P, 2, D]), ALU.add).then_inc(s_v, 1)
                        else:
                            dve.tensor_tensor(V[0:CLAST, 2 * g, :], bank[0:CLAST, vbank[g % 4], 0:D], bv[0:CLAST],
                                              ALU.add).then_inc(s_v, 1)

                    def top(t):
                        dve.wait_ge(s_S, b * TT + t + 1)
                        dve.reduce_max(nm[:, t:t + 1], bank[:, 0:4, :].rearrange("p a n -> p (a n)")[:, 0:LC],
                                       axis=AX, negate=True).then_inc(s_m, 1)

                    top(0)
                    for t in range(TT):
                        if t + 1 < TT:
                            top(t + 1)
                        for g in (0, 2):
                            at, count = groups[g]
                            dve.wait_ge(s_tp, (b * TT + t) * 4 + g + 1)
                            if g == 2:
                                dve.wait_ge(s_t, (b * TT + t) * 4 + 2)
                            dve.tensor_copy(PT[:, at:at + count, :],
                                            bank[:, 4, :].rearrange("p (a n) -> p a n", a=4)).then_inc(s_t, 1)
                        dve.wait_ge(s_e, b * TT + t + 1)
                        dve.reciprocal(rinv[:, t:t + 1], rsum[:, t:t + 1]).then_inc(s_r, 1)
                        dve.wait_ge(s_r, b * TT + t + 1)
                        dve.wait_ge(s_o, b * TT + t + 1)
                        dve.scalar_tensor_tensor(k.x[:, b * TT + t, :], bank[:, 6, 0:D], rinv[:, t:t + 1],
                                                 k.x[:, b * TT + t, :], ALU.mult, ALU.add).then_inc(s_x, 1)
                    dve.wait_ge(s_x, b * TT + TT + PRIMED)

            @block.scalar
            def _(act):
                act.preload_act_table_set(EXP_LN)
                act.wait_ge(s_w, 6 * 16)
                with act.Fori(0, B) as b:
                    for h in range(KD):
                        act.wait_ge(s_kp, b * 2 + h + 1)
                        act.activation(kT[:, h, :], bank[:, 0:4, :].rearrange("p a n -> p (a n)")[:, 0:LC],
                                       ACT.Identity, bias=bk[:, h:h + 1]).then_inc(s_k, 1)
                    ln.rstd_of(act, b)
                    for h in range(KD):
                        act.wait_ge(s_qp, b * 2 + h + 1)
                        act.activation(qT[:, h, :], bank[:, 4 + h, :], ACT.Identity,
                                       bias=bq[:, h:h + 1]).then_inc(s_q, 1)

                    def exps(t):
                        act.wait_ge(s_m, b * TT + t + 1)
                        if t:
                            act.wait_ge(s_tp, (b * TT + t) * 4)
                        act.activation(Pr[:], bank[:, 0:4, :].rearrange("p a n -> p (a n)")[:, 0:LC], ACT.Exp,
                                       bias=nm[:, t:t + 1], accum_out=rsum[:, t:t + 1]).then_inc(s_e, 1)

                    exps(0)
                    for t in range(TT):
                        for g in (1, 3):
                            at, count = groups[g]
                            kn = P if g == 1 else CLAST
                            act.wait_ge(s_tp, (b * TT + t) * 4 + g + 1)
                            act.wait_ge(s_t, (b * TT + t) * 4 + g)
                            act.activation(PT[0:kn, at:at + count, :],
                                           bank[0:kn, 5, 0:count * P].rearrange("p (a n) -> p a n", n=P),
                                           ACT.Copy).then_inc(s_t, 1)
                        if t + 1 < TT:
                            exps(t + 1)


def experts(nc, k, d):
    ctx = ExitStack()
    with ctx:
        sb, ps, sem = tools(nc, ctx, "ex")
        ln = Norm(nc, k, sb, sem)
        xT = sb("xT", [P, KD, NT * P])
        acc = sb("acc", [P, NT, D])
        wr = sb("wr", [P, KD, E])
        br = sb("br", [P, E])
        b2 = sb("b2", [E, D])
        b1 = [sb(f"b1_{i}", [P, FT]) for i in range(2)]
        gamma, beta = sb("gamma", [P, D]), sb("beta", [P, D])
        iota = sb("iota", [P, E])
        iotaw = sb("iotaw", [P, E], mybir.dt.int32)
        lg = sb("lg", [P, NT, E])
        top = sb("top", [P, NT, E])
        idx = sb("idx", [P, NT, E], mybir.dt.uint32)
        idf = sb("idf", [P, NT, 2])
        dif, ex, de, w1s, w2s = (sb(x, [P, NT]) for x in ("dif", "exp", "den", "w1s", "w2s"))
        oh = sb("oh", [P, 2, NT, E])
        rw = sb("rw", [P, NT, E])
        rT = sb("rT", [E, NT, P])
        W1 = [sb(f"W1_{i}", [P, KD, F]) for i in range(2)]
        W2 = [sb(f"W2_{i}", [P, FT, D]) for i in range(2)]
        hT = [sb(f"hT_{i}", [P, FT, T]) for i in range(2)]
        gst, gmv = sb("gst", [P, NT, 6]), sb("gmv", [P, NT, 2])
        gln, grs = sb("gln", [P, NT]), sb("grs", [P, NT])
        spare = sb("spare", [P, 1])
        bank = ps("bank", [P, 8, 512])
        s_w = sem("w")
        s_w1, s_w2 = ([sem(f"{x}_{i}") for i in range(2)] for x in ("w1", "w2"))
        s_keep, s_lg, s_lgs, s_rw, s_rtp, s_rT, s_b2, s_acc0 = (
            sem(x) for x in ("keep", "lg", "lgs", "rw", "rtp", "rT", "b2", "acc0"))
        s_dif, s_ex, s_io = sem("dif"), sem("ex"), sem("iota")
        s_h, s_hr, s_o, s_acc = sem("h"), sem("hr"), sem("o"), sem("acc")
        s_gmv, s_gln, s_grs = sem("gmv"), sem("gln"), sem("grs")
        c_dve = sem("c_dve")

        with nc.Block() as block:
            @block.sync
            def _(sp):
                for tile, name in ((br, "ex_br"), (b2, "ex_b2"), (gamma, "ex_gamma"),
                                   (beta, "ex_beta"), (wr, "ex_wr")):
                    sp.dma_start(tile[:], d[name]).then_inc(s_w, 16)
                def load(e, par):
                    sp.dma_start(W1[par][:], d["ex_w1"][e].rearrange("(h p) f -> p h f", p=P)).then_inc(s_w1[par], 16)
                    sp.dma_start(b1[par][:], d["ex_b1"][e]).then_inc(s_w1[par], 16)
                    sp.dma_start(W2[par][:], d["ex_w2"][e].rearrange("(f p) n -> p f n", p=P)).then_inc(s_w2[par], 16)

                for par in range(2):
                    load(par, par)
                with sp.Fori(0, E // 2 - 1) as e2:
                    for par in range(2):
                        sp.wait_ge(s_o, e2 * (2 * B * TT) + (par + 1) * B * TT)
                        load(e2 * 2 + 2 + par, par)

            @block.gpsimd
            def _(pool):
                pool.iota(iotaw[:], pattern=[[1, E]], base=0, channel_multiplier=0).then_inc(s_io, 1)
                pool.wait_ge(s_io, 1)
                pool.tensor_copy(iota[:], iotaw[:]).then_inc(s_io, 1)

            @block.tensor
            def _(pe):
                pe.wait_ge(s_w, 5 * 16)
                with pe.Fori(0, B) as b:
                    pe.wait_ge(s_keep, b + PRIMED)
                    ln.turn(pe, b, bank[:, 6:8, :])
                    pe.wait_ge(ln.s_xT, b + 1)
                    pe.wait_ge(s_lgs, b + PRIMED)
                    for t in range(TT):
                        for h in range(KD):
                            mm = pe.matmul(bank[:, 5, t * E:(t + 1) * E], ln.xT[:, h, t * P:(t + 1) * P], wr[:, h, :],
                                           start=h == 0, stop=h == KD - 1)
                    mm.then_inc(s_lg, 1)
                pe.wait_ge(s_rw, 1)
                pe.wait_ge(s_keep, B + PRIMED)
                for t in range(NT):
                    mm = pe.transpose(bank[0:E, t // 4, (t % 4) * P:(t % 4 + 1) * P], rw[:, t, :], k.ident[:])
                mm.then_inc(s_rtp, 1)
                pe.wait_ge(s_rT, 1)
                for t in range(NT):
                    mm = pe.matmul(bank[:, t // 2, (t % 2) * D:(t % 2 + 1) * D], rT[:, t, :], b2[:],
                                   start=True, stop=True)
                mm.then_inc(s_b2, 1)
                pe.wait_ge(s_acc0, 1)
                with pe.Fori(0, E // 2) as e2:
                    for par in range(2):
                        pe.wait_ge(s_w1[par], e2 * 32 + 32)
                        pe.wait_ge(s_w2[par], e2 * 16 + 16)
                        for b in range(B):
                                u = b % 2
                                n = e2 * (2 * B) + par * B + b
                                for f in range(FT):
                                    if f < 4:
                                        pe.wait_ge(s_hr, n * FT + PRIMED)
                                    else:
                                        pe.wait_ge(s_hr, n * FT + f - 3 + PRIMED)
                                    for h in range(KD):
                                        mm = pe.matmul(bank[:, f % 4, :], W1[par][:, h, f * P:(f + 1) * P],
                                                       xT[:, h, b * T:(b + 1) * T], start=h == 0, stop=h == KD - 1)
                                    mm.then_inc(s_h, 1)
                                pe.wait_ge(s_acc, n * TT + PRIMED)
                                for t in range(TT):
                                    for f in range(FT):
                                        if t == 0:
                                            pe.wait_ge(s_hr, n * FT + f + 1 + PRIMED)
                                        mm = pe.matmul(bank[:, 4 + t, 0:D], hT[u][:, f, t * P:(t + 1) * P],
                                                       W2[par][:, f, :], start=f == 0, stop=f == FT - 1)
                                    mm.then_inc(s_o, 1)

            @block.vector
            def _(dve):
                dve.sem_inc(s_keep, PRIMED)
                dve.sem_inc(s_lgs, PRIMED)
                dve.sem_inc(s_acc, PRIMED)
                own = Chain(dve, c_dve, 17)
                dve.wait_ge(s_w, 5 * 16)
                with dve.Fori(0, B) as b:
                    ln.stats(dve, b, b)
                    ln.scale(dve, b, b)
                    ln.keep(dve, b, bank[:, 6:8, :])
                    dve.wait_ge(ln.s_xT, b + 1)
                    dve.tensor_copy(xT[:, :, bass.ds(b * T, T)], ln.xT[:])
                    dve.tensor_copy(acc[:, bass.ds(b * TT, TT), :], ln.xn[:]).then_inc(s_keep, 1)
                    dve.wait_ge(s_lg, b + 1)
                    dve.tensor_tensor(lg[:, bass.ds(b * TT, TT), :],
                                      bank[:, 5, 0:TT * E].rearrange("p (t e) -> p t e", e=E),
                                      bc(br[:].unsqueeze(1), [P, TT, E]), ALU.add).then_inc(s_lgs, 1)
                    dve.wait_ge(s_keep, b + 1 + PRIMED)
                own.begin(0)
                dve.wait_ge(s_lgs, B + PRIMED)
                for t in range(NT):
                    ins = dve.max(top[:, t, :], lg[:, t, :])
                own.link(ins)
                for t in range(NT):
                    ins = dve.max_index(idx[:, t, :], top[:, t, :], lg[:, t, :])
                own.link(ins)
                own.link(dve.tensor_copy(idf[:], idx[:, :, 0:2]))
                dve.tensor_tensor(dif[:], top[:, :, 1], top[:, :, 0], ALU.subtract).then_inc(s_dif, 1)
                dve.wait_ge(s_ex, 1)
                own.link(dve.tensor_scalar(de[:], ex[:], 1.0, None, ALU.add))
                own.link(dve.reciprocal(w1s[:], de[:]))
                own.link(dve.tensor_tensor(w2s[:], w1s[:], ex[:], ALU.mult))
                dve.wait_ge(s_io, 2)
                for a in range(2):
                    own.link(dve.tensor_tensor(oh[:, a], bc(iota[:].unsqueeze(1), [P, NT, E]),
                                               bc(idf[:, :, a:a + 1], [P, NT, E]), ALU.is_equal))
                for a, ws in enumerate((w1s, w2s)):
                    own.link(dve.tensor_tensor(oh[:, a], oh[:, a], bc(ws[:].unsqueeze(2), [P, NT, E]), ALU.mult))
                dve.tensor_tensor(rw[:], oh[:, 0], oh[:, 1], ALU.add).then_inc(s_rw, 1)
                dve.wait_ge(s_rtp, 1)
                dve.tensor_copy(rT[:], bank[0:E, 0:4, :].rearrange("p a (t q) -> p (a t) q", q=P)).then_inc(s_rT, 1)
                dve.wait_ge(s_b2, 1)
                dve.tensor_tensor(acc[:].rearrange("p t n -> p (t n)"), bank[:].rearrange("p a n -> p (a n)"),
                                  acc[:].rearrange("p t n -> p (t n)"), ALU.add).then_inc(s_acc0, 1)
                dve.wait_ge(s_acc0, 1)
                with dve.Fori(0, E // 2) as e2:
                    for par in range(2):
                        for b in range(B):
                                n = e2 * (2 * B) + par * B + b
                                dve.wait_ge(s_acc, n * TT + PRIMED)
                                for t in range(TT):
                                    dve.wait_ge(s_o, n * TT + t + 1)
                                    tile = b * TT + t
                                    dve.scalar_tensor_tensor(
                                        acc[:, tile, :], bank[:, 4 + t, 0:D],
                                        rw[:, tile, bass.ds(e2 * 2 + par, 1)],
                                        acc[:, tile, :], ALU.mult, ALU.add).then_inc(s_acc, 1)
                dve.wait_ge(s_acc, 2 * B * TT * (E // 2) + PRIMED)
                for t in range(NT):
                    ins = dve.bn_stats(gst[:, t, :], acc[:, t, :])
                own.link(ins)
                for t in range(NT):
                    ins = dve.bn_aggr(gmv[:, t, :], gst[:, t, :])
                ins.then_inc(s_gmv, 1)
                dve.wait_ge(s_grs, 1)
                for t in range(NT):
                    ins = dve.tensor_scalar(acc[:, t, :], acc[:, t, :], gmv[:, t, 0:1], grs[:, t:t + 1],
                                            ALU.subtract, ALU.mult)
                own.link(ins)
                own.link(dve.tensor_tensor(acc[:], acc[:], bc(gamma[:].unsqueeze(1), [P, NT, D]), ALU.mult))
                own.link(dve.tensor_tensor(acc[:], acc[:], bc(beta[:].unsqueeze(1), [P, NT, D]), ALU.add))
                own.link(dve.tensor_tensor(k.x[:], k.x[:], acc[:], ALU.add))

            @block.scalar
            def _(act):
                act.sem_inc(s_hr, PRIMED)
                act.preload_act_table_set(EXP_LN)
                act.wait_ge(s_w, 5 * 16)
                with act.Fori(0, B) as b:
                    ln.rstd_of(act, b)
                act.wait_ge(s_dif, 1)
                act.activation(ex[:], dif[:], ACT.Exp).then_inc(s_ex, 1)
                with act.Fori(0, E // 2) as e2:
                    for par in range(2):
                        for b in range(B):
                                u = b % 2
                                n = e2 * (2 * B) + par * B + b
                                for f in range(FT):
                                    act.wait_ge(s_h, n * FT + f + 1)
                                    act.activation(hT[u][:, f, :], bank[:, f % 4, :], ACT.Relu,
                                                   bias=b1[par][:, f:f + 1])\
                                       .then_inc(s_hr, 1)
                act.wait_ge(s_gmv, 1)
                act.activation(gln[:], gmv[:, :, 1], ACT.Ln, bias=k.ln_eps[:]).then_inc(s_gln, 1)
                act.wait_ge(s_gln, 1)
                act.activation(grs[:], gln[:], ACT.Exp, scale=-0.5).then_inc(s_grs, 1)


class Split:

    Q_PARTS = (0, 0, 0, 1, 1, 2)

    @staticmethod
    def store_queries(sp, dram, b, half, parts, stored):
        for slot, part in enumerate(Split.Q_PARTS):
            sp.dma_start(dram[b, half * 8:half * 8 + 8, slot], parts[:, part, :]).then_inc(stored, 16)

    @staticmethod
    def store_keys(sp, dram, b, half, parts, stored):
        for part in range(3):
            sp.dma_start(dram[b, half * 8:half * 8 + 8, part], parts[:, part, :]).then_inc(stored, 16)

    @staticmethod
    def load_queries(sp, dram, b, g, q, loaded):
        sp.dma_start(q[0:6 * HD], dram[b, 4 * g:4 * g + 4].rearrange("h r f t -> (r f) h t")).then_inc(loaded, 16)

    @staticmethod
    def load_keys(sp, dram, b, g, kk, loaded):
        for at, count in ((0, 3), (3, 2), (5, 1)):
            sp.dma_start(kk[at * HD:(at + count) * HD],
                         dram[b, 4 * g:4 * g + 4, 0:count].rearrange("h r f t -> (r f) h t")).then_inc(loaded, 16)

    STORES = 6 + 3
    LOADS = 1 + 3


class Heads:

    ROWS, FULL = 6 * HD, 6 * HD + 3

    def __init__(self, nc, sb, sem, name, keys, causal):
        self.keys, self.causal = keys, causal
        self.tiles = [(at, min(P, keys - at)) for at in range(0, keys, P)]
        self.U = 2 * len(self.tiles)
        parts = -(-keys // 512)
        cuts = [keys * c // parts for c in range(parts + 1)]
        self.chunks = [(cuts[c], cuts[c + 1] - cuts[c]) for c in range(parts)]
        self.NM = TT * 4 * parts
        self.q = [sb(f"{name}_q{u}", [P, 4, T], BF16) for u in range(2)]
        self.k = [sb(f"{name}_k{u}", [P, 4, keys], BF16) for u in range(2)]
        self.V = sb(f"{name}_V", [P, len(self.tiles), H, SH])
        self.y = sb(f"{name}_y", [P, TT, D])
        self.dq = nc.dram_tensor(f"{name}_q_parts", (B, H, 6, HD, T), BF16, kind="Internal").ap()
        self.dk = nc.dram_tensor(f"{name}_k_parts", (B, H, 3, HD, keys), BF16, kind="Internal").ap()
        self.loaded = [sem(f"{name}_loaded{u}") for u in range(2)]
        self.s_const = sem(f"{name}_const")

    def clear(self, pool):
        for u in range(2):
            pool.memset(self.k[u][self.ROWS:self.FULL], 1.0).then_inc(self.s_const, 1)
            pool.wait_ge(self.s_const, u + 1)
        pool.memset(self.V[:], 0.0).then_inc(self.s_const, 1)
        pool.wait_ge(self.s_const, 3)
        pool.memset(self.V[:, :, :, HD:HD + 1], 1.0).then_inc(self.s_const, 1)
        pool.wait_ge(self.s_const, 4)


class Call:

    def __init__(self, kind, g):
        self.kind, self.g, self.u = kind, g, g % 2


class Attention:

    PAIRS, SIDES, PROBS = 2, 3, 4
    SCALE = HD ** -0.5
    LINKS = 4

    def __init__(self, k, sb, sem, bank, calls):
        self.k, self.bank = k, bank
        self.calls = [Call(*c) for c in calls]
        self.NC = len(calls)
        side = pairs = tiles = 0
        for i, c in enumerate(self.calls):
            c.pair0, c.tile0 = pairs, tiles
            pairs += c.kind.U
            tiles += c.kind.U // 2
            c.max0, c.turn0 = side, side + c.kind.NM
            c.turned = side = c.turn0 + 4
            if i:
                self.calls[i - 1].out0 = side
                side += 1
        self.calls[-1].out0 = side
        self.NS, self.NU, self.NK = side + 1, pairs, tiles
        self.part = sb("at_part", [P, TT, 4, 4])
        self.mx, self.rest = sb("at_mx", [P, TT * 4]), sb("at_rest", [P, TT * 4])
        self.m3 = sb("at_m3", [P, TT * 4, 3], BF16)
        self.pr = sb("at_pr", [P, self.PROBS, 2, T])
        self.yT = sb("at_yT", [P, T])
        self.rec = sb("at_rec", [P, TT, 4])
        (self.side_full, self.side_free, self.s_m3, self.s_link, self.scored, self.weighed, self.summed,
         self.s_yT, self.s_rec) = (sem(f"at_{x}") for x in (
             "side_full", "side_free", "m3", "link", "scored", "weighed", "summed", "yT", "rec"))


    def side_bank(self, pe, b, j):
        if j >= self.SIDES:
            pe.wait_ge(self.side_free, b * self.NS + j - self.SIDES + 1)
        return self.bank[:, 4 + j % self.SIDES, :]

    def maximum_of(self, c, j):
        th, chunk = divmod(j, len(c.kind.chunks))
        t, h = divmod(th, 4)
        at, N = c.kind.chunks[chunk]
        if c.kind.causal:
            N = P * (t + 1)
        return t, h, chunk, at, N

    def pe_max(self, pe, b, i, j):
        c = self.calls[i]
        t, h, chunk, at, N = self.maximum_of(c, j)
        if j == 0:
            pe.wait_ge(c.kind.loaded[c.u], (b * (NG // 2) + c.g // 2 + 1) * Split.LOADS * 16)
        dst = self.side_bank(pe, b, c.max0 + j)
        mm = pe.matmul(dst[:, 0:N], c.kind.q[c.u][0:Heads.ROWS, h, t * P:(t + 1) * P],
                       c.kind.k[c.u][0:Heads.ROWS, h, at:at + N], start=True, stop=True)
        if c.kind.causal:
            mm = pe.matmul(dst[:, N - P:N], self.k.identb[:], self.k.mask_qk[:], start=False, stop=True,
                           skip_group_check=True)
        mm.then_inc(self.side_full, 1)

    def pe_turn(self, pe, b, i):
        c = self.calls[i]
        for h in range(4):
            dst = self.side_bank(pe, b, c.turn0 + h)
            pe.wait_ge(self.s_m3, b * self.NC + i + 1)
            for t in range(TT):
                mm = pe.matmul(dst[Heads.ROWS:Heads.FULL, t * P:(t + 1) * P], self.m3[:, t * 4 + h, :],
                               self.k.identb[:], start=True, stop=True)
            mm.then_inc(self.side_full, 1)

    def span(self, c, kt):
        return (kt * P, T) if c.kind.causal else (0, T)

    def pe_scores(self, pe, b, i, s):
        c = self.calls[i]
        kt, pp = divmod(s, 2)
        at, kn = c.kind.tiles[kt]
        lo, hi = self.span(c, kt)
        pair = c.pair0 + s
        if pair >= self.PAIRS:
            pe.wait_ge(self.weighed, b * self.NU + pair - self.PAIRS + 1)
        for a in range(2):
            mm = pe.matmul(self.bank[0:kn, 2 * (pair % self.PAIRS) + a, 0:hi - lo],
                           c.kind.k[c.u][0:Heads.FULL, 2 * pp + a, at:at + kn],
                           c.kind.q[c.u][0:Heads.FULL, 2 * pp + a, lo:hi], start=True, stop=True)
        if c.kind.causal:
            for a in range(2):
                mm = pe.matmul(self.bank[:, 2 * (pair % self.PAIRS) + a, 0:P], self.k.identb[:],
                               self.k.mask_kq[:], start=False, stop=True, skip_group_check=True)
        mm.then_inc(self.scored, 1)

    def pe_values(self, pe, b, i, kt):
        c = self.calls[i]
        _, kn = c.kind.tiles[kt]
        lo, hi = self.span(c, kt)
        if kt == 0 and i:
            pe.wait_ge(self.s_yT, b * self.NC + i)
        pe.wait_ge(self.weighed, b * self.NU + c.pair0 + 2 * kt + 2)
        for h in range(4):
            pair = c.pair0 + 2 * kt + h // 2
            mm = pe.matmul(self.bank[h * SH:(h + 1) * SH, 7, lo:hi], c.kind.V[0:kn, kt, 4 * c.g + h, :],
                           self.pr[0:kn, pair % self.PROBS, h % 2, 0:hi - lo], start=kt == 0,
                           stop=kt == len(c.kind.tiles) - 1, skip_group_check=True)
        mm.then_inc(self.summed, 1)

    def pe_out(self, pe, b, i):
        dst = self.side_bank(pe, b, self.calls[i].out0)
        pe.wait_ge(self.s_yT, b * self.NC + i + 1)
        for t in range(TT):
            mm = pe.transpose(dst[:, t * P:(t + 1) * P], self.yT[:, t * P:(t + 1) * P], self.k.ident[:])
        mm.then_inc(self.side_full, 1)

    def pe_batch(self, pe, b):
        for j in range(self.calls[0].kind.NM):
            self.pe_max(pe, b, 0, j)
        self.pe_turn(pe, b, 0)
        for i, c in enumerate(self.calls):
            last = i + 1 == self.NC
            maxima = 0 if last else self.calls[i + 1].kind.NM
            pe.wait_ge(self.side_free, b * self.NS + c.turned)
            if i:
                self.pe_out(pe, b, i - 1)
            steps = c.kind.U + 2
            spread = steps - 3
            for s in range(steps):
                if s < c.kind.U:
                    self.pe_scores(pe, b, i, s)
                for j in range(min(maxima, maxima * s // spread), min(maxima, maxima * (s + 1) // spread)):
                    self.pe_max(pe, b, i + 1, j)
                if s == steps - 2 and not last:
                    self.pe_turn(pe, b, i + 1)
                if s >= 3 and s % 2:
                    self.pe_values(pe, b, i, (s - 3) // 2)
        self.pe_out(pe, b, self.NC - 1)
        pe.wait_ge(self.side_free, (b + 1) * self.NS)


    def dve_max(self, dve, b, i):
        c = self.calls[i]
        for j in range(c.kind.NM):
            t, h, chunk, at, N = self.maximum_of(c, j)
            dve.wait_ge(self.side_full, b * self.NS + c.max0 + j + 1)
            dve.reduce_max(self.part[:, t, h, chunk:chunk + 1], self.bank[:, 4 + (c.max0 + j) % self.SIDES, 0:N],
                           axis=AX).then_inc(self.side_free, 1)
        n = b * (self.NC * self.LINKS) + i * self.LINKS
        dve.wait_ge(self.side_free, b * self.NS + c.turn0)
        dve.reduce_max(self.mx[:], self.part[:, :, :, 0:len(c.kind.chunks)].rearrange("p t h c -> p (t h) c"),
                       axis=AX, negate=True).then_inc(self.s_link, 1)
        dve.wait_ge(self.s_link, n + 1)
        dve.tensor_copy(self.m3[:, :, 0], self.mx[:]).then_inc(self.s_link, 1)
        dve.wait_ge(self.s_link, n + 2)
        dve.tensor_tensor(self.rest[:], self.mx[:], self.m3[:, :, 0], ALU.subtract).then_inc(self.s_link, 1)
        dve.wait_ge(self.s_link, n + 3)
        dve.tensor_copy(self.m3[:, :, 1], self.rest[:]).then_inc(self.s_link, 1)
        dve.wait_ge(self.s_link, n + 4)
        dve.tensor_tensor(self.m3[:, :, 2], self.rest[:], self.m3[:, :, 1], ALU.subtract).then_inc(self.s_m3, 1)
        for h in range(4):
            j = c.turn0 + h
            dve.wait_ge(self.side_full, b * self.NS + j + 1)
            dve.tensor_copy(c.kind.q[c.u][Heads.ROWS:Heads.FULL, h, :],
                            self.bank[Heads.ROWS:Heads.FULL, 4 + j % self.SIDES, :]).then_inc(self.side_free, 1)

    def dve_batch(self, dve, b):
        self.dve_max(dve, b, 0)
        for i, c in enumerate(self.calls):
            if i + 1 < self.NC:
                self.dve_max(dve, b, i + 1)
            dve.wait_ge(self.summed, b * self.NK + c.tile0 + c.kind.U // 2)
            dve.tensor_copy(self.yT[:], self.bank[:, 7, :]).then_inc(self.s_yT, 1)
            dve.wait_ge(self.side_full, b * self.NS + c.out0 + 1)
            src = self.bank[:, 4 + c.out0 % self.SIDES, :].rearrange("p (t h f) -> p t h f", t=TT, h=4)
            dve.reciprocal(self.rec[:], src[:, :, :, HD]).then_inc(self.s_rec, 1)
            dve.wait_ge(self.s_rec, b * self.NC + i + 1)
            dve.tensor_tensor(c.kind.y[:, :, c.g * 64:(c.g + 1) * 64].rearrange("p t (h f) -> p t h f", f=HD),
                              src[:, :, :, 0:HD], bc(self.rec[:].unsqueeze(3), [P, TT, 4, HD]), ALU.mult)\
               .then_inc(self.side_free, 1)


    def act_batch(self, act, b):
        for c in self.calls:
            for s in range(c.kind.U):
                kt, pp = divmod(s, 2)
                _, kn = c.kind.tiles[kt]
                lo, hi = self.span(c, kt)
                pair = c.pair0 + s
                act.wait_ge(self.scored, b * self.NU + pair + 1)
                if pair >= self.PROBS:
                    act.wait_ge(self.summed, b * self.NK + (pair - self.PROBS) // 2 + 1)
                r = 2 * (pair % self.PAIRS)
                act.activation(self.pr[0:kn, pair % self.PROBS, :, 0:hi - lo], self.bank[0:kn, r:r + 2, 0:hi - lo],
                               ACT.Exp, scale=self.SCALE).then_inc(self.weighed, 1)


    def sp_load(self, sp, b, i):
        c = self.calls[i]
        for before in self.calls[:i]:
            if before.kind is c.kind and before.g == c.g - 2:
                sp.wait_ge(self.scored, b * self.NU + before.pair0 + before.kind.U)
        Split.load_queries(sp, c.kind.dq, b, c.g, c.kind.q[c.u], c.kind.loaded[c.u])
        Split.load_keys(sp, c.kind.dk, b, c.g, c.kind.k[c.u], c.kind.loaded[c.u])


class Project:

    def __init__(self, nc, k, sb, sem, bank, name):
        self.k, self.bank = k, bank
        self.w, self.bias = sb(f"{name}_w", [P, KD, D]), sb(f"{name}_b", [P, D])
        self.yT = sb(f"{name}_yT", [P, KD, T])
        self.s_w, self.s_t, self.s_c, self.s_p, self.s_b, self.s_x = (
            sem(f"{name}_{x}") for x in ("w", "t", "c", "p", "b", "x"))

    def load(self, sp, w, bias):
        sp.dma_start(self.w[:], w.rearrange("(h p) n -> p h n", p=P)).then_inc(self.s_w, 16)
        sp.dma_start(self.bias[:], bias).then_inc(self.s_w, 16)

    def pe(self, pe, n, y):
        pe.wait_ge(self.s_w, 32)
        for h in range(KD):
            for t in range(TT):
                mm = pe.transpose(self.bank[:, 2 + h, t * P:(t + 1) * P], y[:, t, h * P:(h + 1) * P], self.k.ident[:])
        mm.then_inc(self.s_t, 1)
        pe.wait_ge(self.s_c, n + 1)
        for t in range(TT):
            for h in range(KD):
                mm = pe.matmul(self.bank[:, 4 + t // 2, (t % 2) * D:(t % 2 + 1) * D],
                               self.yT[:, h, t * P:(t + 1) * P], self.w[:, h, :], start=h == 0, stop=h == KD - 1)
        mm.then_inc(self.s_p, 1)

    def dve(self, dve, b, n):
        x = self.k.x[:, bass.ds(b * TT, TT), :]
        dve.wait_ge(self.s_w, 32)
        dve.tensor_tensor(x, x, bc(self.bias[:].unsqueeze(1), [P, TT, D]), ALU.add).then_inc(self.s_b, 1)
        dve.wait_ge(self.s_t, n + 1)
        dve.tensor_copy(self.yT[:], self.bank[:, 2:4, :]).then_inc(self.s_c, 1)
        dve.wait_ge(self.s_b, n + 1)
        dve.wait_ge(self.s_p, n + 1)
        dve.tensor_tensor(x.rearrange("p t n -> p (t n)"), self.bank[:, 4:6, :].rearrange("p a n -> p (a n)"),
                          x.rearrange("p t n -> p (t n)"), ALU.add).then_inc(self.s_x, 1)
        dve.wait_ge(self.s_x, n + 1 + PRIMED)


def self_attention(nc, k, d):
    ctx = ExitStack()
    with ctx:
        sb, ps, sem = tools(nc, ctx, "sa")
        bank = ps("bank", [P, 8, 512])
        ln = Norm(nc, k, sb, sem)
        heads = Heads(nc, sb, sem, "sa", T, False)
        at = Attention(k, sb, sem, bank, [(heads, g) for g in range(NG)])
        pr = Project(nc, k, sb, sem, bank, "pr")
        w, bias = sb("w", [P, KD, 3 * D]), sb("bias", [P, 3 * D])
        nw = sb("nw", [P, 2 * D])
        qk, sq = sb("qk", [P, TT, 2 * D]), sb("sq", [P, TT, 2 * D])
        ss, lg, rs = (sb(x, [P, TT, 2 * H]) for x in ("ss", "lg", "rs"))
        parts = sb("parts", [P, 2, KD, 3, T], BF16)
        rest = sb("rest", [P, 2 * KD, T])
        s_w, s_qkv, s_qk, s_v, s_sq, s_ss, s_lg, s_rs, s_nm, s_nw, s_turned = (
            sem(x) for x in ("w", "qkv", "qk", "v", "sq", "ss", "lg", "rs", "nm", "nw", "turned"))
        s_high, s_rest, s_mid, s_low = (sem(x) for x in ("high", "rest", "mid", "low"))
        stored = [sem(f"stored{half}") for half in range(KD)]

        with nc.Block() as block:
            @block.sync
            def _(sp):
                sp.dma_start(w[:], d["sa_w"].rearrange("(h p) n -> p h n", p=P)).then_inc(s_w, 16)
                sp.dma_start(bias[:], d["sa_b"]).then_inc(s_w, 16)
                sp.dma_start(nw[:], d["sa_nw"]).then_inc(s_w, 16)
                pr.load(sp, d["sa_wp"], d["sa_bp"])
                with sp.Fori(0, B) as b:
                    sp.wait_ge(s_low, b + 1)
                    for half in range(KD):
                        Split.store_queries(sp, heads.dq, b, half, parts[:, 0, half], stored[half])
                        Split.store_keys(sp, heads.dk, b, half, parts[:, 1, half], stored[half])
                    for g in range(NG):
                        if g < KD:
                            sp.wait_ge(stored[g], b * (16 * Split.STORES) + 16 * Split.STORES)
                        at.sp_load(sp, b, g)

            @block.gpsimd
            def _(pool):
                heads.clear(pool)

            @block.tensor
            def _(pe):
                pe.wait_ge(heads.s_const, 4)
                pe.wait_ge(s_w, 48)
                with pe.Fori(0, B) as b:
                    pe.wait_ge(pr.s_x, b + PRIMED)
                    ln.turn(pe, b, bank[:, 6:8, :])
                    pe.wait_ge(ln.s_xT, b + 1)
                    for t in range(TT):
                        for dst, cols in ((bank[:, t, :], slice(0, 2 * D)),
                                          (bank[:, 4 + t // 2, (t % 2) * D:(t % 2 + 1) * D], slice(2 * D, 3 * D))):
                            for h in range(KD):
                                mm = pe.matmul(dst, ln.xT[:, h, t * P:(t + 1) * P], w[:, h, cols],
                                               start=h == 0, stop=h == KD - 1)
                    mm.then_inc(s_qkv, 1)
                    pe.wait_ge(s_nw, b + 1)
                    for a in range(2 * KD):
                        for t in range(TT):
                            mm = pe.transpose(bank[:, a, t * P:(t + 1) * P], sq[:, t, a * P:(a + 1) * P], k.ident[:])
                    mm.then_inc(s_turned, 1)
                    pe.wait_ge(s_low, b + 1)
                    pe.wait_ge(s_v, b + 1)
                    at.pe_batch(pe, b)
                    pr.pe(pe, b, heads.y)

            @block.vector
            def _(dve):
                dve.sem_inc(pr.s_x, PRIMED)
                dve.wait_ge(heads.s_const, 4)
                dve.wait_ge(s_w, 48)
                with dve.Fori(0, B) as b:
                    ln.stats(dve, b, b)
                    ln.scale(dve, b, b)
                    ln.keep(dve, b, bank[:, 6:8, :])
                    dve.wait_ge(s_qkv, b + 1)
                    dve.tensor_tensor(qk[:], bank[:, 0:4, :], bc(bias[:, 0:2 * D].unsqueeze(1), [P, TT, 2 * D]),
                                      ALU.add).then_inc(s_qk, 1)
                    for t in range(TT):
                        ins = dve.tensor_tensor(
                            heads.V[:, t, :, 0:HD],
                            bank[:, 4 + t // 2, (t % 2) * D:(t % 2 + 1) * D].rearrange("p (h f) -> p h f", f=HD),
                            bias[:, 2 * D:].rearrange("p (h f) -> p h f", f=HD), ALU.add)
                    ins.then_inc(s_v, 1)
                    by_head = "p t (a f) -> p t a f"
                    dve.wait_ge(s_sq, b + 1)
                    dve.reduce_sum(ss[:], sq[:].rearrange(by_head, f=HD), axis=AX).then_inc(s_ss, 1)
                    dve.wait_ge(s_rs, b + 1)
                    dve.tensor_tensor(sq[:].rearrange(by_head, f=HD), qk[:].rearrange(by_head, f=HD),
                                      bc(rs[:].unsqueeze(3), [P, TT, 2 * H, HD]), ALU.mult).then_inc(s_nm, 1)
                    dve.wait_ge(s_nm, b + 1)
                    dve.tensor_tensor(sq[:], sq[:], bc(nw[:].unsqueeze(1), [P, TT, 2 * D]), ALU.mult)\
                       .then_inc(s_nw, 1)
                    dve.wait_ge(s_high, b + 1)
                    dve.tensor_tensor(rest[:], bank[:, 0:4, :], parts[:, :, :, 0].rearrange("p a h t -> p (a h) t"),
                                      ALU.subtract).then_inc(s_rest, 1)
                    dve.wait_ge(s_rest, b + 1)
                    dve.wait_ge(s_mid, b + 1)
                    dve.tensor_tensor(parts[:, :, :, 2].rearrange("p a h t -> p (a h) t"), rest[:],
                                      parts[:, :, :, 1].rearrange("p a h t -> p (a h) t"),
                                      ALU.subtract).then_inc(s_low, 1)
                    at.dve_batch(dve, b)
                    pr.dve(dve, b, b)

            @block.scalar
            def _(act):
                act.preload_act_table_set(EXP_LN)
                with act.Fori(0, B) as b:
                    ln.rstd_of(act, b)
                    act.wait_ge(s_qk, b + 1)
                    act.activation(sq[:], qk[:], ACT.Square).then_inc(s_sq, 1)
                    act.wait_ge(s_ss, b + 1)
                    act.activation(lg[:], ss[:], ACT.Ln, bias=k.eps[:], scale=1.0 / HD).then_inc(s_lg, 1)
                    act.wait_ge(s_lg, b + 1)
                    act.activation(rs[:], lg[:], ACT.Exp, scale=-0.5).then_inc(s_rs, 1)
                    act.wait_ge(s_turned, b + 1)
                    act.activation(parts[:, :, :, 0].rearrange("p a h t -> p (a h) t"), bank[:, 0:4, :], ACT.Copy)\
                       .then_inc(s_high, 1)
                    act.wait_ge(s_rest, b + 1)
                    act.activation(parts[:, :, :, 1].rearrange("p a h t -> p (a h) t"), rest[:], ACT.Copy)\
                       .then_inc(s_mid, 1)
                    at.act_batch(act, b)


def cross_attention(nc, k, d):
    ctx = ExitStack()
    with ctx:
        sb, ps, sem = tools(nc, ctx, "xa")
        bank = ps("bank", [P, 8, 512])
        ln = Norm(nc, k, sb, sem)
        own = Heads(nc, sb, sem, "own", T, True)
        con = Heads(nc, sb, sem, "con", LC, False)
        at = Attention(k, sb, sem, bank, [(own, 0), (own, 1), (con, 0), (con, 1), (con, 2), (con, 3),
                                          (own, 2), (own, 3)])
        pr = Project(nc, k, sb, sem, bank, "pr")
        QKQ = 3 * T + LC
        spans = [(a * T, T) for a in range(3)] + [(3 * T, LC)]
        w = sb("w", [P, KD, 4 * D])
        wc = sb("wc", [P, 2 * D])
        bcol = sb("bcol", [P, KD, 4])
        brow = sb("brow", [P, 2, D])
        cT = sb("cT", [P, LC])
        parts = sb("parts", [P, 3, QKQ], BF16)
        rest = sb("rest", [P, QKQ])
        s_w, s_c, s_qkq, s_high, s_rest, s_mid, s_low, s_vp, s_v, s_y = (
            sem(x) for x in ("w", "c", "qkq", "high", "rest", "mid", "low", "vp", "v", "y"))
        stored = [sem(f"stored{half}") for half in range(KD)]
        VG = 4
        by_head = "p (t h f) -> p t h f"

        def source(a):
            return bank[:, a, :] if a < 3 else bank[:, 3:7, :].rearrange("p a n -> p (a n)")[:, 0:LC]

        with nc.Block() as block:
            @block.sync
            def _(sp):
                sp.dma_start(w[:], d["xa_w"].rearrange("(h p) n -> p h n", p=P)).then_inc(s_w, 16)
                sp.dma_start(wc[:], d["xa_wc"]).then_inc(s_w, 16)
                sp.dma_start(bcol[:], d["xa_bcol"]).then_inc(s_w, 16)
                sp.dma_start(brow[:], d["xa_brow"]).then_inc(s_w, 16)
                pr.load(sp, d["xa_wp"], d["xa_bp"])
                with sp.Fori(0, B) as b:
                    for half in range(KD):
                        sp.wait_ge(s_low, b * KD + half + 1)
                        for kind, q, kk in ((own, 0, 1), (con, 2, 3)):
                            for a, store, dram in ((q, Split.store_queries, kind.dq), (kk, Split.store_keys, kind.dk)):
                                at0, N = spans[a]
                                store(sp, dram, b, half, parts[:, :, at0:at0 + N], stored[half])
                    for i in range(at.NC):
                        if i < KD:
                            sp.wait_ge(stored[i], b * (32 * Split.STORES) + 32 * Split.STORES)
                        at.sp_load(sp, b, i)

            @block.gpsimd
            def _(pool):
                pool.dma_start(cT[:], d["ctxT"][0]).then_inc(s_c, 16)
                own.clear(pool)
                con.clear(pool)
                for b in range(1, B):
                    pool.wait_ge(s_vp, b * (VG + 1))
                    pool.dma_start(cT[:], d["ctxT"][b]).then_inc(s_c, 16)

            @block.tensor
            def _(pe):
                pe.wait_ge(own.s_const, 4)
                pe.wait_ge(con.s_const, 4)
                pe.wait_ge(s_w, 64)
                with pe.Fori(0, B) as b:
                    pe.wait_ge(pr.s_x, b + PRIMED)
                    ln.turn(pe, b, bank[:, 6:8, :])
                    pe.wait_ge(s_c, b * 16 + 16)
                    pe.wait_ge(ln.s_xT, b + 1)
                    for half in range(KD):
                        f = slice(half * P, (half + 1) * P)
                        if half:
                            pe.wait_ge(s_rest, b * (KD * 4) + 4)
                        for a in range(3):
                            for h in range(KD):
                                mm = pe.matmul(bank[:, a, :], w[:, h, a * D + half * P:a * D + (half + 1) * P],
                                               ln.xT[:, h, :], start=h == 0, stop=h == KD - 1)
                            mm.then_inc(s_qkq, 1)
                        for at0 in range(0, LC, 512):
                            N = min(512, LC - at0)
                            mm = pe.matmul(bank[:, 3 + at0 // 512, 0:N], wc[:, f], cT[:, at0:at0 + N],
                                           start=True, stop=True)
                        mm.then_inc(s_qkq, 1)
                    pe.wait_ge(s_rest, b * (KD * 4) + 8)
                    for t in range(TT):
                        for h in range(KD):
                            mm = pe.matmul(bank[:, t // 2, (t % 2) * D:(t % 2 + 1) * D],
                                           ln.xT[:, h, t * P:(t + 1) * P], w[:, h, 3 * D:],
                                           start=h == 0, stop=h == KD - 1)
                    mm.then_inc(s_vp, 1)
                    for v in range(VG):
                        if v == VG - 1:
                            pe.wait_ge(s_v, b * (VG + 1) + 1)
                        for t in range(4 * v, min(4 * v + 4, CT)):
                            kn = min(P, LC - t * P)
                            slot = (4 + t) % 16
                            mm = pe.matmul(bank[0:kn, slot // 2, (slot % 2) * D:(slot % 2 + 1) * D],
                                           cT[:, t * P:t * P + kn], wc[:, D:], start=True, stop=True)
                        mm.then_inc(s_vp, 1)
                    pe.wait_ge(s_v, b * (VG + 1) + VG + 1)
                    at.pe_batch(pe, b)
                    pe.wait_ge(s_y, b + 1)
                    pr.pe(pe, b, own.y)

            @block.vector
            def _(dve):
                dve.sem_inc(pr.s_x, PRIMED)
                dve.wait_ge(own.s_const, 4)
                dve.wait_ge(con.s_const, 4)
                dve.wait_ge(s_w, 64)
                with dve.Fori(0, B) as b:
                    ln.stats(dve, b, b)
                    ln.scale(dve, b, b)
                    ln.keep(dve, b, bank[:, 6:8, :])
                    for half in range(KD):
                        for a, (at0, N) in enumerate(spans):
                            dve.wait_ge(s_high, b * (KD * 4) + half * 4 + a + 1)
                            dve.scalar_tensor_tensor(rest[:, at0:at0 + N], source(a), bcol[:, half, a:a + 1],
                                                     parts[:, 0, at0:at0 + N], ALU.add, ALU.subtract)\
                               .then_inc(s_rest, 1)
                        dve.wait_ge(s_rest, b * (KD * 4) + half * 4 + 4)
                        dve.wait_ge(s_mid, b * KD + half + 1)
                        dve.tensor_tensor(parts[:, 2, :], rest[:], parts[:, 1, :], ALU.subtract).then_inc(s_low, 1)
                    dve.wait_ge(s_vp, b * (VG + 1) + 1)
                    dve.tensor_tensor(own.V[:, :, :, 0:HD],
                                      bank[:, 0:2, :].rearrange("p a n -> p (a n)").rearrange(by_head, h=H, f=HD),
                                      bc(brow[:, 0].rearrange("p (h f) -> p h f", f=HD).unsqueeze(1), [P, TT, H, HD]),
                                      ALU.add).then_inc(s_v, 1)
                    for v in range(VG):
                        dve.wait_ge(s_vp, b * (VG + 1) + v + 2)
                        tiles = min(4, CT - 4 * v)
                        kn = P if v < VG - 1 else CLAST
                        at0 = (2 + 2 * v) % 8
                        src = bank[0:kn, at0:at0 + 2, :].rearrange("p a n -> p (a n)")[:, 0:tiles * D]
                        dve.tensor_tensor(con.V[0:kn, 4 * v:4 * v + tiles, :, 0:HD], src.rearrange(by_head, h=H, f=HD),
                                          bc(brow[0:kn, 1].rearrange("p (h f) -> p h f", f=HD).unsqueeze(1),
                                             [kn, tiles, H, HD]), ALU.add).then_inc(s_v, 1)
                    at.dve_batch(dve, b)
                    dve.wait_ge(at.side_free, (b + 1) * at.NS)
                    dve.tensor_tensor(own.y[:], own.y[:], con.y[:], ALU.add).then_inc(s_y, 1)
                    pr.dve(dve, b, b)

            @block.scalar
            def _(act):
                act.preload_act_table_set(EXP_LN)
                act.wait_ge(s_w, 64)
                with act.Fori(0, B) as b:
                    ln.rstd_of(act, b)
                    for half in range(KD):
                        if half:
                            act.wait_ge(stored[0], b * (32 * Split.STORES) + 32 * Split.STORES)
                        for a, (at0, N) in enumerate(spans):
                            act.wait_ge(s_qkq, b * (KD * 4) + half * 4 + a + 1)
                            act.activation(parts[:, 0, at0:at0 + N], source(a), ACT.Identity,
                                           bias=bcol[:, half, a:a + 1]).then_inc(s_high, 1)
                        act.wait_ge(s_rest, b * (KD * 4) + half * 4 + 4)
                        act.activation(parts[:, 1, :], rest[:], ACT.Copy).then_inc(s_mid, 1)
                    at.act_batch(act, b)


def quantized_ffn(nc, k, d):
    ROUND = 1.5 * 2.0 ** 23
    ctx = ExitStack()
    with ctx:
        sb, ps, sem = tools(nc, ctx, "qf")
        ln = Norm(nc, k, sb, sem)
        xq = sb("xq", [P, KD, NT * P])
        wi = sb("wi", [P, FT, D])
        wiq = sb("wiq", [P, KD, F])
        wo = sb("wo", [P, FT, D])
        bi = sb("bi", [P, FT])
        bo = sb("bo", [P, D])
        am, cl, rc, sc, isc = (sb(x, [P, 2, FT]) for x in ("am", "cl", "rc", "sc", "isc"))
        xm, xmf, xa = sb("xm", [P, 1]), sb("xmf", [P, 4]), sb("xa", [P, 1])
        xs, xis = sb("xs", [P, 1]), sb("xis", [P, 1])
        ha, hmf, hs, his = sb("ha", [P, 1]), sb("hmf", [P, 4]), sb("hs", [P, 1]), sb("his", [P, 1])
        hm = sb("hm", [P, B * FT])
        hm1 = sb("hm1", [P, 1])
        isf = sb("isf", [P, FT])
        hT = sb("hT", [P, B, FT, T])
        bank = ps("bank", [P, 8, 512])
        s_w, s_keep, s_wt, s_wtc = sem("w"), sem("keep"), sem("wt"), sem("wtc")
        s_xm, s_xa, s_xq, s_is, s_h, s_g, s_hm, s_hm1, s_ha, s_hq, s_o, s_x = (
            sem(x) for x in ("xm", "xa", "xq", "is", "h", "g", "hm", "hm1", "ha", "hq", "o", "x"))
        c_dve = sem("c_dve")

        with nc.Block() as block:
            @block.sync
            def _(sp):
                sp.dma_start(wi[:], d["qf_wi"].rearrange("(f p) n -> p f n", p=P)).then_inc(s_w, 16)
                sp.dma_start(wo[:], d["qf_wo"].rearrange("(f p) n -> p f n", p=P)).then_inc(s_w, 16)
                sp.dma_start(bi[:], d["qf_bi"]).then_inc(s_w, 16)
                sp.dma_start(bo[:], d["qf_bo"]).then_inc(s_w, 16)

            @block.gpsimd
            def _(pool):
                pool.wait_ge(s_xm, 1)
                pool.partition_all_reduce(xa[:], xm[:], P, RMAX).then_inc(s_xa, 1)
                pool.wait_ge(s_hm1, 1)
                pool.partition_all_reduce(ha[:], hm1[:], P, RMAX).then_inc(s_ha, 1)

            def scales(own, dve, amax, floor_to, rec, scale, inv, top):
                own.link(dve.tensor_scalar(floor_to, amax, 1e-8, None, ALU.max))
                own.link(dve.reciprocal(rec, floor_to))
                dve.tensor_scalar(inv, floor_to, 1.0 / top, None, ALU.mult)
                own.link(dve.tensor_scalar(scale, rec, top, None, ALU.mult))

            def quantize(own, dve, x, scale, low, high):
                own.link(dve.tensor_scalar(x, x, scale, ROUND, ALU.mult, ALU.add))
                own.link(dve.tensor_scalar(x, x, ROUND, high, ALU.subtract, ALU.min))
                own.link(dve.tensor_scalar(x, x, low, None, ALU.max))

            @block.tensor
            def _(pe):
                with pe.Fori(0, B) as b:
                    pe.wait_ge(s_keep, b + PRIMED)
                    ln.turn(pe, b, bank[:, 6:8, :])
                pe.wait_ge(s_wt, 1)
                for f in range(FT):
                    for h in range(KD):
                        mm = pe.transpose(bank[:, 2 * h + f // 4, (f % 4) * P:(f % 4 + 1) * P],
                                          wi[:, f, h * P:(h + 1) * P], k.ident[:])
                mm.then_inc(s_wtc, 1)
                pe.wait_ge(s_wtc, 2)
                pe.wait_ge(s_xq, 1)
                for b in range(B):
                    for f in range(FT):
                        i = b * FT + f
                        if i >= 4:
                            pe.wait_ge(s_g, i - 3)
                        for h in range(KD):
                            mm = pe.matmul(bank[:, 4 + i % 4, :], wiq[:, h, f * P:(f + 1) * P],
                                           xq[:, h, b * T:(b + 1) * T], start=h == 0, stop=h == KD - 1)
                        mm.then_inc(s_h, 1)
                for t in range(NT):
                    if t % TT == 0:
                        pe.wait_ge(s_hq, t // TT + 1)
                    if t >= 8:
                        pe.wait_ge(s_x, t - 7)
                    for f in range(FT):
                        mm = pe.matmul(bank[:, t % 8, 0:D], hT[:, t // TT, f, (t % TT) * P:(t % TT + 1) * P],
                                       wo[:, f, :], start=f == 0, stop=f == FT - 1)
                    mm.then_inc(s_o, 1)

            @block.vector
            def _(dve):
                dve.sem_inc(s_keep, PRIMED)
                own = Chain(dve, c_dve, 34)
                with dve.Fori(0, B) as b:
                    ln.stats(dve, b, b)
                    ln.scale(dve, b, b)
                    ln.keep(dve, b, bank[:, 6:8, :])
                    dve.wait_ge(ln.s_xT, b + 1)
                    dve.tensor_copy(xq[:, :, bass.ds(b * T, T)], ln.xT[:])
                    dve.reduce_max(xmf[:, bass.ds(b, 1)], ln.xT[:], axis=mybir.AxisListType.XY,
                                   apply_absolute_value=True).then_inc(s_keep, 1)
                    dve.wait_ge(s_keep, b + 1 + PRIMED)
                own.begin(0)
                dve.wait_ge(s_keep, B + PRIMED)
                dve.reduce_max(xm[:], xmf[:], axis=AX).then_inc(s_xm, 1)
                dve.wait_ge(s_w, 64)
                dve.reduce_max(am[:, 0], wi[:], axis=AX, apply_absolute_value=True)
                own.link(dve.reduce_max(am[:, 1], wo[:], axis=AX, apply_absolute_value=True))
                scales(own, dve, am[:], cl[:], rc[:], sc[:], isc[:], 127.0)
                for f in range(FT):
                    for w, a in ((wi, 0), (wo, 1)):
                        ins = dve.tensor_scalar(w[:, f, :], w[:, f, :], sc[:, a, f:f + 1], ROUND, ALU.mult, ALU.add)
                own.link(ins)
                for w in (wi, wo):
                    ins = dve.tensor_scalar(w[:], w[:], ROUND, 127.0, ALU.subtract, ALU.min)
                own.link(ins)
                own.link(dve.tensor_scalar(wo[:], wo[:], -128.0, None, ALU.max))
                dve.tensor_scalar(wi[:], wi[:], -128.0, None, ALU.max).then_inc(s_wt, 1)
                for f in range(FT):
                    ins = dve.tensor_scalar(wo[:, f, :], wo[:, f, :], isc[:, 1, f:f + 1], None, ALU.mult)
                own.link(ins)
                dve.wait_ge(s_wtc, 1)
                dve.tensor_copy(wiq[:], bank[:, 0:4, :].rearrange("p (h a) n -> p h (a n)", h=KD)).then_inc(s_wtc, 1)
                dve.wait_ge(s_xa, 1)
                scales(own, dve, xa[:], xm[:], xis[:], xs[:], his[:], 32767.0)
                dve.tensor_scalar(isf[:], isc[:, 0], his[:], None, ALU.mult).then_inc(s_is, 1)
                flat = xq[:].rearrange("p h n -> p (h n)")
                quantize(own, dve, flat, xs[:], -32768.0, 32767.0)
                own.link(dve.memset(xm[:], 0.0))
                dve.memset(xm[:], 0.0).then_inc(s_xq, 1)
                for i in range(B * FT):
                    dve.wait_ge(s_g, i + 1)
                    dve.reduce_max(hm[:, i:i + 1], hT[:, i // FT, i % FT, :], axis=AX,
                                   apply_absolute_value=True).then_inc(s_hm, 1)
                dve.wait_ge(s_hm, B * FT)
                dve.reduce_max(hm1[:], hm[:], axis=AX).then_inc(s_hm1, 1)
                for t in range(TT * B // 4):
                    own.link(dve.tensor_tensor(k.x[:, 4 * t:4 * t + 4, :], k.x[:, 4 * t:4 * t + 4, :],
                                               bc(bo[:].unsqueeze(1), [P, 4, D]), ALU.add))
                dve.wait_ge(s_ha, 1)
                scales(own, dve, ha[:], hmf[:, 0:1], hmf[:, 1:2], hs[:], his[:], 32767.0)
                for b in range(B):
                    h = hT[:, b].rearrange("p f n -> p (f n)")
                    own.link(dve.tensor_scalar(h, h, hs[:], ROUND, ALU.mult, ALU.add))
                    own.link(dve.tensor_scalar(h, h, ROUND, 32767.0, ALU.subtract, ALU.min))
                    own.link(dve.tensor_scalar(h, h, -32768.0, his[:], ALU.max, ALU.mult))
                    dve.memset(xm[:], 0.0).then_inc(s_hq, 1)
                for t in range(NT):
                    dve.wait_ge(s_o, t + 1)
                    dve.tensor_tensor(k.x[:, t, :], bank[:, t % 8, 0:D], k.x[:, t, :], ALU.add).then_inc(s_x, 1)
                dve.wait_ge(s_x, NT)
                own.end()

            @block.scalar
            def _(act):
                act.preload_act_table_set(EXP_LN)
                with act.Fori(0, B) as b:
                    ln.rstd_of(act, b)
                act.wait_ge(s_is, 1)
                for b in range(B):
                    for f in range(FT):
                        i = b * FT + f
                        act.wait_ge(s_h, i + 1)
                        act.activation(hT[:, b, f, :], bank[:, 4 + i % 4, :], ACT.Gelu, bias=bi[:, f:f + 1],
                                       scale=isf[:, f:f + 1]).then_inc(s_g, 1)


STAGES = [gated_attention, context_attention, experts, self_attention, cross_attention, quantized_ffn]


def program(nc, d, out, stages):
    k = Core()
    ctx = ExitStack()
    with ctx:
        constants(nc, k, d["x"], ctx)
        for stage in stages:
            taken = nc.snapshot_sems()
            stage(nc, k, d)
            nc.all_engine_barrier()
            nc.clear_and_free_semaphores(nc.allocated_since(taken))
            nc.all_engine_barrier()
        stored = nc.alloc_semaphore("stored")
        with nc.Block() as block:
            @block.sync
            def _(sp):
                sp.dma_start(out.rearrange("b (t p) d -> p (b t) d", p=P), k.x[:]).then_inc(stored, 16)
                sp.wait_ge(stored, 16)


def layout(i):
    f = {n: np.asarray(a) for n, a in i.items()}
    d = {"x": f["x"]}
    wq, wk, wv = f["L0_attn_Wq"], f["L0_attn_Wk"], f["L0_attn_Wv"]
    d["ga_w"] = np.stack([np.concatenate(
        [wq[:, 256 * j:256 * j + 256], wk[:, 64 * j:64 * j + 64], wk[:, 64 * j:64 * j + 64],
         wv[:, 64 * j:64 * j + 64], f["L0_attn_Wa"][:, 4 * j:4 * j + 4], f["L0_attn_Walpha"][:, 4 * j:4 * j + 4],
         f["L0_attn_Wb"][:, j:j + 1]], 1) for j in range(HKV)])
    c = f["L0_attn_Wconv"]
    d["ga_taps"] = np.stack([np.stack(
        [c[256 * j:256 * j + 128], c[256 * j + 128:256 * j + 256],
         np.concatenate([c[1024 + 64 * j:1088 + 64 * j]] * 2), np.concatenate([c[1280 + 64 * j:1344 + 64 * j]] * 2)],
        1) for j in range(HKV)])
    d["ga_rows"] = np.stack([np.tile(np.concatenate(
        [f["L0_attn_A_log"][4 * j:4 * j + 4], f["L0_attn_dt_bias"][4 * j:4 * j + 4]])[None], (P, 1))
        for j in range(HKV)])
    d["ga_wo"] = f["L0_attn_Wo"].reshape(HKV, 256, D)
    d["ga_normw"] = np.tile(f["L0_attn_norm_w"], 2)[:, None]
    d["ctxT"] = f["ctx_512"].transpose(0, 2, 1)
    d["ca_wq"], d["ca_wk"], d["ca_wv"] = (f[f"L0_xattn_W{x}"] for x in "qkv")
    d["ca_bq"], d["ca_bk"] = (f[f"L0_xattn_b{x}"].reshape(KD, P).T for x in "qk")
    d["ca_bv"] = np.tile(f["L0_xattn_bv"], (P, 1))
    d["ex_wr"] = f["L0_ffn_Wr"].T.reshape(KD, P, E).transpose(1, 0, 2)
    d["ex_br"] = np.tile(f["L0_ffn_br"], (P, 1))
    d["ex_b2"] = f["L0_ffn_b2"]
    d["ex_b1"] = f["L0_ffn_b1"].reshape(E, FT, P).transpose(0, 2, 1)
    d["ex_gamma"], d["ex_beta"] = (np.tile(f[f"L0_ffn_{x}"], (P, 1)) for x in ("gamma", "beta"))
    d["ex_w1"] = f["L0_ffn_W1"].transpose(0, 2, 1)
    d["ex_w2"] = f["L0_ffn_W2"].transpose(0, 2, 1)

    d["sa_w"] = f["L1_attn_Wqkv"].T
    d["sa_b"] = np.tile(f["L1_attn_bqkv"], (P, 1))
    d["sa_nw"] = np.tile(np.concatenate([np.tile(f["L1_attn_qn_w"], H), np.tile(f["L1_attn_kn_w"], H)]), (P, 1))
    d["sa_wp"] = f["L1_attn_Wproj"].T
    d["sa_bp"] = np.tile(f["L1_attn_bproj"], (P, 1))
    x = {n: f[f"L1_xattn_{n}"] for n in ("Wq", "bq", "Wk", "bk", "Wv", "bv", "Wcq", "bcq", "Wck", "bck", "Wcv", "bcv")}
    d["xa_w"] = np.concatenate([x["Wq"], x["Wk"], x["Wcq"], x["Wv"]], 1)
    d["xa_wc"] = np.concatenate([x["Wck"], x["Wcv"]], 1)
    d["xa_bcol"] = np.stack([x[n].reshape(KD, P) for n in ("bq", "bk", "bcq", "bck")]).transpose(2, 1, 0)
    d["xa_brow"] = np.tile(np.stack([x["bv"], x["bcv"]]), (P, 1, 1))
    d["xa_wp"] = f["L1_xattn_Wp"]
    d["xa_bp"] = np.tile(f["L1_xattn_bp"], (P, 1))
    d["qf_wi"] = f["L1_ffn_W_in"].T
    d["qf_wo"] = f["L1_ffn_W_out"]
    d["qf_bi"] = f["L1_ffn_b_in"].reshape(FT, P).T
    d["qf_bo"] = np.tile(f["L1_ffn_b_out"], (P, 1))
    return {n: np.ascontiguousarray(a) for n, a in d.items()}


def kernel(**inputs):
    import concourse.bacc as _bacc
    from concourse.bass_utils import run_bass_kernel_spmd as _run

    nc = _bacc.Bacc("TRN2", target_bir_lowering=False, num_devices=1)
    d = layout(inputs)
    arrays = {f"in_{n}": a for n, a in d.items()}
    aps = {n: nc.dram_tensor(f"in_{n}", a.shape, mybir.dt.from_np(a.dtype), kind="ExternalInput").ap()
           for n, a in d.items()}
    out = nc.dram_tensor("out_x", (B, T, D), F32, kind="ExternalOutput").ap()
    program(nc, aps, out, STAGES)
    r = _run(nc, [arrays], core_ids=[0])
    return r.results[0]["out_x"]
```

```python
from contextlib import ExitStack

import numpy as np
import concourse.bass as bass
from concourse import mybir

F32 = mybir.dt.float32
BF16 = mybir.dt.bfloat16
ALU = mybir.AluOpType
ACT = mybir.ActivationFunctionType
AX = mybir.AxisListType.X
RMAX = bass.bass_isa.ReduceOp.max

P = 128
B, T, D = 4, 512, 256
TT = T // P
NT = B * TT
KD = D // P
LN_EPS = 1e-5
EPS = 1e-6
EXP_LN = "natural_log_exp_and_others"
NEG = -1e30
PRIMED = 1

HQ, HKV, HK, KW = 16, 4, 64, 4
G4 = HQ // HKV
CW = G4 * HK + 3 * HK
SMALL = 2 * HQ + HKV
DAMP = 0.25

LC, CD = 1601, 128
CT = -(-LC // P)
CLAST = LC - (CT - 1) * P

H, HD, SH = 16, 16, 32
NG = 4
SW = 4 * SH

E, F = 8, 1024
FT = F // P


class Chain:

    def __init__(self, eng, sem, per):
        self.eng, self.sem, self.per, self.n, self.k = eng, sem, per, 0, 0

    def begin(self, n):
        self.n, self.k = n, 0

    def done(self, ins):
        ins.then_inc(self.sem, 1)
        self.k += 1

    def wait(self):
        self.eng.wait_ge(self.sem, self.n * self.per + self.k)

    def link(self, ins):
        self.done(ins)
        self.wait()

    def end(self):
        assert self.k == self.per, (self.sem, self.k)


class Core:
    pass


def bc(ap, shape):
    return ap.to_broadcast(shape)


def tools(nc, ctx, stage):
    def sb(name, shape, dt=F32):
        return ctx.enter_context(nc.sbuf_tensor(f"{stage}_{name}", shape, dt))

    def ps(name, shape, dt=F32):
        return ctx.enter_context(nc.psum_tensor(f"{stage}_{name}", shape, dt))

    def sem(name):
        return nc.alloc_semaphore(f"{stage}_{name}")

    return sb, ps, sem


def constants(nc, k, x_in, ctx):
    sb, ps, sem = tools(nc, ctx, "c")
    k.x = sb("x", [P, NT, D])
    k.ident = sb("ident", [P, P])
    k.identb = sb("identb", [P, P], BF16)
    k.mask_kq = sb("mask_kq", [P, P], BF16)
    k.mask_qk = sb("mask_qk", [P, P], BF16)
    k.tri = sb("tri", [P, P])
    k.ln_eps = sb("ln_eps", [P, 1])
    k.eps = sb("eps", [P, 1])
    k.tiny = sb("tiny", [P, 1])
    k.one = sb("one", [P, 1])
    loaded, filled, made = sem("loaded"), sem("filled"), sem("made")
    with nc.Block() as block:
        @block.sync
        def _(sp):
            sp.dma_start(k.x[:], x_in.rearrange("b (t p) d -> p (b t) d", p=P)).then_inc(loaded, 16)
            sp.wait_ge(loaded, 16)

        @block.gpsimd
        def _(pool):
            for tile, value in ((k.ident, 0.0), (k.identb, 0.0), (k.mask_kq, 0.0), (k.mask_qk, 0.0), (k.tri, 1.0),
                                (k.ln_eps, LN_EPS), (k.eps, EPS), (k.tiny, 1e-18), (k.one, 1.0)):
                pool.memset(tile[:], value).then_inc(filled, 1)
            pool.wait_ge(filled, 9)
            for tile in (k.ident, k.identb):
                pool.affine_select(out=tile[:], in_=tile[:], compare_op=ALU.not_equal, fill=1.0, base=0,
                                   pattern=[[-1, P]], channel_multiplier=1).then_inc(made, 1)
            for tile, fill in ((k.mask_kq, NEG), (k.tri, 0.0)):
                pool.affine_select(out=tile[:], in_=tile[:], compare_op=ALU.is_ge, fill=fill, base=0,
                                   pattern=[[1, P]], channel_multiplier=-1).then_inc(made, 1)
            pool.affine_select(out=k.mask_qk[:], in_=k.mask_qk[:], compare_op=ALU.is_ge, fill=NEG, base=0,
                               pattern=[[-1, P]], channel_multiplier=1).then_inc(made, 1)
            pool.wait_ge(made, 5)


class Norm:

    def __init__(self, nc, k, sb, sem):
        self.nc, self.k = nc, k
        self.st = sb("ln_st", [P, TT, 6])
        self.mv = sb("ln_mv", [P, TT, 2])
        self.spare = sb("ln_spare", [P, 1])
        self.lnv = sb("ln_lnv", [P, TT])
        self.rstd = sb("ln_rstd", [P, TT])
        self.xn = sb("ln_xn", [P, TT, D])
        self.xT = sb("ln_xT", [P, KD, T])
        self.s_bn, self.s_mv, self.s_ln, self.s_rstd = (sem(f"ln_{x}") for x in ("bn", "mv", "log", "rstd"))
        self.s_xn = sem("ln_xn")

    def stats(self, dve, b, n):
        for t in range(TT):
            dve.bn_stats(self.st[:, t, :], self.k.x[:, b * TT + t, :]).then_inc(self.s_bn, 1)
        dve.wait_ge(self.s_bn, n * TT + TT)
        dve.memset(self.spare[:], 0.0)
        for t in range(TT):
            dve.bn_aggr(self.mv[:, t, :], self.st[:, t, :]).then_inc(self.s_mv, 1)

    def rstd_of(self, act, n):
        act.wait_ge(self.s_mv, n * TT + TT)
        act.activation(self.lnv[:], self.mv[:, :, 1], ACT.Ln, bias=self.k.ln_eps[:]).then_inc(self.s_ln, 1)
        act.wait_ge(self.s_ln, n + 1)
        act.activation(self.rstd[:], self.lnv[:], ACT.Exp, scale=-0.5).then_inc(self.s_rstd, 1)

    def scale(self, dve, b, n):
        dve.wait_ge(self.s_rstd, n + 1)
        for t in range(TT):
            dve.tensor_scalar(self.xn[:, t, :], self.k.x[:, b * TT + t, :], self.mv[:, t, 0:1],
                              self.rstd[:, t:t + 1], ALU.subtract, ALU.mult).then_inc(self.s_xn, 1)


class WholeNorm:

    def __init__(self, k, sb, sem, xn, xT, banks):
        self.k, self.xn, self.xT, self.banks = k, xn, xT, banks
        self.st, self.mv = sb("ln_st", [P, NT, 6]), sb("ln_mv", [P, NT, 2])
        self.lnv, self.rstd_ = sb("ln_lnv", [P, NT]), sb("ln_rstd", [P, NT])
        self.s_bn, self.s_mv, self.s_ln, self.s_rstd, self.s_xn, self.s_turned, self.s_xT = (
            sem(f"ln_{x}") for x in ("bn", "mv", "log", "rstd", "xn", "turned", "xT"))

    def stats(self, dve):
        for t in range(NT):
            dve.bn_stats(self.st[:, t, :], self.k.x[:, t, :]).then_inc(self.s_bn, 1)
        dve.wait_ge(self.s_bn, NT)
        for t in range(NT):
            dve.bn_aggr(self.mv[:, t, :], self.st[:, t, :]).then_inc(self.s_mv, 1)

    def rstd(self, act):
        act.wait_ge(self.s_mv, NT)
        act.activation(self.lnv[:], self.mv[:, :, 1], ACT.Ln, bias=self.k.ln_eps[:]).then_inc(self.s_ln, 1)
        act.wait_ge(self.s_ln, 1)
        act.activation(self.rstd_[:], self.lnv[:], ACT.Exp, scale=-0.5).then_inc(self.s_rstd, 1)

    def scale(self, dve):
        dve.wait_ge(self.s_rstd, 1)
        for t in range(NT):
            dve.tensor_scalar(self.xn[:, t, :], self.k.x[:, t, :], self.mv[:, t, 0:1], self.rstd_[:, t:t + 1],
                              ALU.subtract, ALU.mult).then_inc(self.s_xn, 1)

    def two_banks(self, b):
        return self.banks[:, 2 * (b % 2):2 * (b % 2) + 2, :]

    def turn(self, pe, b):
        pe.wait_ge(self.s_xn, (b + 1) * TT)
        if b >= 2:
            pe.wait_ge(self.s_xT, b - 1)
        for h in range(KD):
            for t in range(TT):
                mm = pe.transpose(self.two_banks(b)[:, h, t * P:(t + 1) * P],
                                  self.xn[:, b * TT + t, h * P:(h + 1) * P], self.k.ident[:])
        mm.then_inc(self.s_turned, 1)

    def keep(self, dve, b):
        dve.wait_ge(self.s_turned, b + 1)
        dve.tensor_copy(self.xT[:, :, b * T:(b + 1) * T], self.two_banks(b)).then_inc(self.s_xT, 1)


def gated_attention(nc, k, d):
    ctx = ExitStack()
    with ctx:
        sb, ps, sem = tools(nc, ctx, "ga")
        xn, xT = sb("xn", [P, NT, D]), sb("xT", [P, KD, NT * P])
        w = sb("w", [P, KD, CW])
        wsm = sb("wsm", [P, KD, SMALL])
        taps = sb("taps", [P, 4, KW])
        rows = sb("rows", [P, 2 * HQ])
        wo = sb("wo", [P, 2, D])
        wos = sb("wos", [P, 2, D])
        normw = sb("normw", [P, 1])
        cv = sb("cv", [P, 4, T])
        small = sb("small", [P, NT, SMALL])
        z, az, e1, l1, sp_ = (sb(x, [P, NT, HQ]) for x in ("z", "az", "e1", "l1", "sp"))
        ea = sb("ea", [P, HQ])
        eab = sb("eab", [P, NT, HQ + HKV])
        den = sb("den", [P, NT, HQ + HKV])
        gates = sb("gates", [P, NT, HQ + HKV])
        alpha, gall = sb("alpha", [P, B * HKV, TT, G4]), sb("gall", [P, B * HKV, TT, G4])
        beta = sb("beta", [P, B * HKV, TT])
        g = sb("g", [P, TT, G4])
        gd = sb("gd", [P, TT, G4, HK])
        negG = sb("negG", [P, TT, G4])
        X0 = sb("X0", [P, TT, 2, P])
        X1 = sb("X1", [P, TT, 2, P])
        Xs = sb("Xs", [P, TT, 2, P])
        kT = sb("kT", [P, T])
        vT = sb("vT", [HK, T])
        sq = sb("sq", [P, G4 * TT * HK])
        ssk, lnk, nk, nke, rk = (sb(x, [P, TT]) for x in ("ssk", "lnk", "nk", "nke", "rk"))
        KKV = sb("KKV", [P, TT, 3 * HK])
        kTn = sb("kTn", [P, 2, TT, P])
        Ed = sb("Ed", [P, TT, 2, P])
        Dm = sb("Dm", [P, 2, 2, 2, 2, P])
        KVw = sb("KVw", [P, TT - 1, 2, 2, 2 * HK])
        Hs = sb("Hs", [P, TT - 1, 2, 2 * HK])
        Hb = sb("Hb", [P, TT - 1, 2, 2, 2, HK])
        Wm = sb("Wm", [P, 2, 2, 2, 2, P])
        o = sb("o", [P, TT, G4, HK])
        on = sb("on", [P, TT, G4, HK])
        sso, lno, ro = (sb(x, [P, TT * G4]) for x in ("sso", "lno", "ro"))
        oT = sb("oT", [P, 2, TT, P])
        bank = ps("bank", [P, 8, 512])
        ln = WholeNorm(k, sb, sem, xn, xT, bank[:, 4:8, :])

        s_w, s_t, s_wo, s_nw = (sem(x) for x in ("w", "taps", "wo", "normw"))
        s_proj, s_small, s_conv, s_smallc, s_az, s_es, s_l1 = (
            sem(x) for x in ("proj", "small", "conv", "smallc", "az", "es", "l1"))
        s_g, s_G, s_Gc, s_E, s_Ee, s_D, s_De = (sem(x) for x in ("g", "G", "Gc", "E", "Ee", "D", "De"))
        s_silu, s_kvt, s_ssk, s_nk, s_kn, s_v, s_kT, s_kTc = (
            sem(x) for x in ("silu", "kvt", "ssk", "nk", "kn", "v", "kT", "kTc"))
        s_KVw, s_st, s_H, s_W, s_Wm, s_Y, s_X, s_Xs = (
            sem(x) for x in ("KVw", "st", "H", "W", "Wm", "Y", "X", "Xs"))
        s_O, s_o, s_sq, s_ss, s_ro, s_on, s_oT, s_oTc, s_out, s_x = (
            sem(x) for x in ("O", "o", "sq", "ss", "ro", "on", "oT", "oTc", "out", "x"))
        s_Hb, s_zero, s_lag = sem("Hb"), sem("zero"), sem("lag")
        c_gate, c_act_gate = sem("c_gate"), sem("c_act_gate")
        s_gd, s_wos, c_dve, c_act = sem("gd"), sem("wos"), sem("c_dve"), sem("c_act")

        kps = bank[:, 4, :].rearrange("p (c f) -> p c f", c=TT)
        vps = bank[:, 5, 0:TT * HK].rearrange("p (c f) -> p c f", c=TT)
        Eps = bank[:, 6:8, :].rearrange("p a (c i t) -> p (a c) i t", c=2, i=2)
        st = bank[:, 6:8, :].rearrange("p a (c i f) -> p (a c) i f", c=2, i=2)

        def pair(cc):
            return bank[:, 2 * cc:2 * cc + 2, :].rearrange("p q (c i t) -> p q c i t", c=2, i=2)

        def Y(cc):
            return bank[:, 4 + cc, :].rearrange("p (c i t) -> p c i t", c=2, i=2)

        O = bank[:, 6:8, :].rearrange("p a (c i q f) -> p (a c) i q f", c=2, i=2, q=2)

        with nc.Block() as block:
            @block.sync
            def _(sp):
                sp.dma_start(normw[:], d["ga_normw"]).then_inc(s_nw, 16)
                sp.dma_start(rows[:], d["ga_rows"]).then_inc(s_nw, 16)
                sp.dma_start(wsm[:], d["ga_small"].rearrange("(h p) n -> p h n", p=P)).then_inc(s_nw, 16)
                with sp.Fori(0, B) as b:
                    with sp.Fori(0, HKV) as j:
                        n = b * HKV + j
                        sp.wait_ge(s_proj, n * 4 + PRIMED)
                        sp.dma_start(w[:], d["ga_w"][j].rearrange("(h p) n -> p h n", p=P)).then_inc(s_w, 16)
                        sp.wait_ge(s_conv, n * 4 + PRIMED)
                        sp.dma_start(taps[:], d["ga_taps"][j]).then_inc(s_t, 16)
                        sp.wait_ge(s_wos, n + PRIMED)
                        sp.dma_start(wo[:], d["ga_wo"][j].rearrange("(h p) n -> p h n", p=P)).then_inc(s_wo, 16)

            @block.tensor
            def _(pe):
                pe.sem_inc(s_proj, PRIMED)
                pe.wait_ge(s_nw, 48)

                def project(n, b):
                    pe.wait_ge(s_w, n * 16 + 16)
                    for m in (2, 3, 0, 1):
                        M = P if m < 3 else HK
                        for h in range(KD):
                            mm = pe.matmul(bank[0:M, m, :], w[:, h, m * P:m * P + M], xT[:, h, bass.ds(b * T, T)],
                                           start=h == 0, stop=h == KD - 1)
                        mm.then_inc(s_proj, 1)

                def attend(n):
                    pe.wait_ge(s_silu, n * 4 + 2)
                    for c in range(TT):
                        pe.transpose(kps[:, c, :], kT[:, c * P:(c + 1) * P], k.ident[:]).then_inc(s_kvt, 1)
                    for c in range(TT):
                        pe.transpose(vps[:, c, :], vT[:, c * P:(c + 1) * P], k.ident[0:HK, 0:HK])\
                          .then_inc(s_kvt, 1)
                    pe.wait_ge(s_gd, n + 1)
                    pe.wait_ge(s_x, n + PRIMED)
                    for c in range(TT):
                        for i in range(2):
                            pe.matmul(Eps[:, c, i, :], gd[:, c, 2 * i:2 * i + 2, :].rearrange("p a f -> p (a f)"),
                                      k.tri[:], start=True, stop=True).then_inc(s_E, 1)
                    pe.wait_ge(s_silu, n * 4 + 4)
                    pe.wait_ge(s_conv, n * 4 + 4 + PRIMED)
                    pe.matmul(bank[:, 3, 0:TT * G4], k.tri[:], g[:].rearrange("p c h -> p (c h)"),
                              start=True, stop=True).then_inc(s_G, 1)
                    for cc in range(2):
                        if cc == 1:
                            pe.wait_ge(s_Gc, n + 1)
                        for q in range(2):
                            pe.matmul(bank[:, 2 * cc + q, :], k.identb[:],
                                      bc(k.mask_kq[:].unsqueeze(1), [P, 4, P]), start=True, stop=False)
                            for c in range(2):
                                for i in range(2):
                                    mm = pe.matmul(pair(cc)[:, q, c, i, :],
                                                   bc(g[:, 2 * cc + c, 2 * i + q:2 * i + q + 1], [P, P]),
                                                   k.tri[:], start=False, stop=c == 1 and i == 1)
                        mm.then_inc(s_D, 1)
                    pe.wait_ge(s_kn, n + 1)
                    for c in range(TT):
                        pe.transpose(kps[:, c, :], KKV[:, c, 0:P], k.ident[:]).then_inc(s_kT, 1)
                    pe.wait_ge(s_Ee, n + 1)
                    for c in range(TT - 1):
                        pe.wait_ge(s_KVw, n * (TT - 1) + c + 1)
                        for q in range(2):
                            mm = pe.matmul(st[q * HK:(q + 1) * HK, c], KKV[:, c, 0:HK],
                                           KVw[:, c, q], start=True, stop=True)
                    mm.then_inc(s_st, 1)
                    pe.wait_ge(s_kTc, n + 1)
                    pe.wait_ge(s_De, n * 2 + 2)
                    for r in range(3):
                        X = X0 if r == 0 else X1
                        for cc in range(2):
                            if r:
                                pe.wait_ge(s_X, n * 4 + 2 * (r - 1) + cc + 1)
                            for c in range(2 * cc, 2 * cc + 2):
                                for q in range(2):
                                    mm = pe.matmul(pair(cc)[:, q, c % 2], kTn[:, q, c, :], X[:, c],
                                                   start=True, stop=True)
                            mm.then_inc(s_W, 1)
                        for cc in range(2):
                            pe.wait_ge(s_Wm, n * 6 + 2 * r + cc + 1)
                            if cc == 0:
                                pe.wait_ge(s_Hb, n * 3 + 3)
                                pe.wait_ge(s_Xs, n * 6 + 2 * r + 1)
                            else:
                                pe.wait_ge(s_Xs, n * 6 + 2 * r + 2)
                            for c in range(2 * cc, 2 * cc + 2):
                                if r < 2:
                                    for q in range(2):
                                        mm = pe.matmul(Y(cc)[q * HK:(q + 1) * HK, c % 2], KKV[:, c, 0:HK],
                                                       Wm[:, cc, q, c % 2], start=True, stop=c == 0,
                                                       skip_group_check=True)
                                    for i in range(2 if c else 0):
                                        mm = pe.matmul(Y(cc)[:, c % 2, i, :],
                                                       Hb[:, c - 1, i, 0].rearrange("p q f -> p (q f)"),
                                                       Xs[:, c, i, :], start=False, stop=i == 1,
                                                       skip_group_check=True)
                                else:
                                    for i in range(2):
                                        if c:
                                            mm = pe.matmul(O[:, c, i].rearrange("p q f -> p (q f)"),
                                                           Xs[:, c, i, :],
                                                           Hb[:, c - 1, i, 1].rearrange("p q f -> p (q f)"),
                                                           start=True, stop=False, skip_group_check=True)
                                        for q in range(2):
                                            mm = pe.matmul(O[:, c, i, q], Wm[:, cc, q, c % 2, i, :],
                                                           KKV[:, c, P:], start=c == 0, stop=True,
                                                           skip_group_check=True)
                            mm.then_inc(s_Y if r < 2 else s_O, 1)

                def out(n):
                    pe.wait_ge(s_on, n + 1)
                    for h in range(2):
                        for c in range(TT):
                            pe.transpose(bank[:, 4 + h, c * P:(c + 1) * P],
                                         on[:, c, 2 * h:2 * h + 2, :].rearrange("p a f -> p (a f)"),
                                         k.ident[:]).then_inc(s_oT, 1)
                    pe.wait_ge(s_oTc, n + 1)
                    pe.wait_ge(s_wos, n + 1 + PRIMED)
                    for c in range(TT):
                        for h in range(2):
                            mm = pe.matmul(bank[:, 6 + c // 2, (c % 2) * D:(c % 2 + 1) * D], oT[:, h, c, :],
                                           wos[:, h, :], start=h == 0, stop=h == 1)
                    mm.then_inc(s_out, 1)

                for b in range(B):
                    ln.turn(pe, b)
                pe.wait_ge(ln.s_xT, B)
                for t in range(NT):
                    for h in range(KD):
                        mm = pe.matmul(bank[:, t // 8, (t % 8) * SMALL:(t % 8 + 1) * SMALL],
                                       xT[:, h, t * P:(t + 1) * P], wsm[:, h, :], start=h == 0, stop=h == KD - 1)
                mm.then_inc(s_small, 1)
                pe.wait_ge(s_smallc, 1)
                project(0, 0)

                def batch(b, last):
                    with pe.Fori(0, HKV - 1) as j:
                        n = b * HKV + j
                        attend(n)
                        project(n + 1, b)
                        out(n)
                    attend(b * HKV + (HKV - 1))
                    if not last:
                        project(b * HKV + HKV, b + 1)
                    out(b * HKV + (HKV - 1))

                with pe.Fori(0, B - 1) as b:
                    batch(b, False)
                batch(B - 1, True)

            @block.vector
            def _(dve):
                dve.memset(kTn[:], 0.0).then_inc(s_zero, 1)
                dve.memset(Hb[:], 0.0).then_inc(s_zero, 1)
                dve.sem_inc(s_conv, PRIMED)
                dve.sem_inc(s_wos, PRIMED)
                dve.sem_inc(s_x, PRIMED)
                own, gate_steps = Chain(dve, c_dve, 2), Chain(dve, c_gate, 4)
                dve.wait_ge(s_nw, 48)

                def convolve(n, lag, half):
                    if lag == 0 and half == 0:
                        dve.wait_ge(s_t, n * 16 + 16)
                    if lag:
                        dve.wait_ge(s_lag, n * (2 * (KW - 1)) + half * (KW - 1) + lag)
                    for a, m in enumerate(((2, 3), (0, 1))[half]):
                        M = P if m < 3 else HK
                        if lag == 0:
                            dve.wait_ge(s_proj, n * 4 + 2 * half + a + 1 + PRIMED)
                            ins = dve.tensor_scalar(cv[0:M, m, :], bank[0:M, m, :], taps[0:M, m, KW - 1:KW],
                                                    None, ALU.mult)
                        else:
                            ins = dve.scalar_tensor_tensor(
                                cv[0:M, m, lag:], bank[0:M, m, 0:T - lag], taps[0:M, m, KW - 1 - lag:KW - lag],
                                cv[0:M, m, lag:], ALU.mult, ALU.add)
                        if lag == KW - 1:
                            ins.then_inc(s_conv, 1)
                    if lag < KW - 1:
                        ins.then_inc(s_lag, 1)

                def gates_of_all():
                    gate_steps.begin(0)
                    dve.wait_ge(s_small, 1)
                    dve.tensor_copy(small[:].rearrange("p (a t) s -> p a t s", a=2),
                                    bank[:, 0:2, 0:8 * SMALL].rearrange("p a (t s) -> p a t s", s=SMALL))\
                       .then_inc(s_smallc, 1)
                    dve.wait_ge(s_smallc, 1)
                    gate_steps.link(dve.tensor_tensor(z[:], small[:, :, 0:HQ],
                                                      bc(rows[:, HQ:].unsqueeze(1), [P, NT, HQ]), ALU.add))
                    dve.scalar_tensor_tensor(az[:], z[:], -1.0, z[:], ALU.mult, ALU.max).then_inc(s_az, 1)
                    dve.wait_ge(s_es, 1)
                    gate_steps.link(dve.tensor_scalar(den[:], eab[:], 1.0, None, ALU.add))
                    gate_steps.link(dve.reciprocal(gates[:], den[:]))
                    dve.wait_ge(s_l1, 1)
                    gate_steps.link(dve.scalar_tensor_tensor(sp_[:], z[:], 0.0, l1[:], ALU.max, ALU.add))
                    for b in range(B):
                        t, by_group = slice(b * TT, (b + 1) * TT), "p t (j h) -> p j t h"
                        dve.tensor_scalar(alpha[:, b * HKV:(b + 1) * HKV],
                                          gates[:, t, 0:HQ].rearrange(by_group, h=G4), HK ** -0.5, None, ALU.mult)
                        dve.tensor_copy(beta[:, b * HKV:(b + 1) * HKV], gates[:, t, HQ:].rearrange("p t j -> p j t"))
                        for j in range(HKV):
                            ins = dve.scalar_tensor_tensor(
                                gall[:, b * HKV + j], sp_[:, t, j * G4:(j + 1) * G4], -1.0,
                                bc(ea[:, j * G4:(j + 1) * G4].unsqueeze(1), [P, TT, G4]), ALU.mult, ALU.mult)
                    ins.then_inc(s_g, 1)
                    dve.wait_ge(s_g, 1)
                    gate_steps.end()

                def group_gates(n):
                    of_n = gall[:, bass.ds(n, 1)].rearrange("p n t h -> p (n t) h")
                    dve.tensor_copy(g[:], of_n)
                    dve.tensor_copy(gd[:], bc(of_n.unsqueeze(3), [P, TT, G4, HK])).then_inc(s_gd, 1)

                def attend(n):
                    own.begin(n)
                    dve.wait_ge(s_kvt, n * 8 + 8)
                    dve.tensor_tensor(KKV[:, :, P:], vps, bc(beta[:, bass.ds(n, 1)].rearrange("p n t -> p (n t)").unsqueeze(2),
                                                                [P, TT, HK]), ALU.mult)\
                       .then_inc(s_v, 1)
                    dve.wait_ge(s_nk, n + 1)
                    own.link(dve.tensor_scalar(nke[:], nk[:], EPS, None, ALU.add))
                    own.link(dve.reciprocal(rk[:], nke[:]))
                    dve.tensor_tensor(KKV[:, :, 0:P], kps, bc(rk[:].unsqueeze(2), [P, TT, P]), ALU.mult)\
                       .then_inc(s_kn, 1)
                    dve.wait_ge(s_G, n + 1)
                    dve.tensor_scalar(negG[:].rearrange("p c h -> p (c h)"), bank[:, 3, 0:TT * G4], -1.0, None,
                                      ALU.mult).then_inc(s_Gc, 1)
                    dve.wait_ge(s_wo, n * 16 + 16)
                    dve.tensor_scalar(wos[:], wo[:], normw[:], None, ALU.mult).then_inc(s_wos, 1)
                    dve.wait_ge(s_kn, n + 1)
                    dve.wait_ge(s_v, n + 1)
                    for c in range(TT - 1):
                        if c % 2 == 0:
                            dve.wait_ge(s_De, n * 2 + c // 2 + 1)
                        for q in range(2):
                            ins = dve.tensor_tensor(
                                KVw[:, c, q], bc(KKV[:, c, HK:].unsqueeze(1), [P, 2, P]),
                                bc(Dm[:, c // 2, q, c % 2, :, P - 1:P], [P, 2, P]), ALU.mult)
                        ins.then_inc(s_KVw, 1)
                    dve.wait_ge(s_silu, n * 4 + 4)
                    dve.tensor_tensor(Xs[:, 1], X0[:, 1], Ed[:, 1], ALU.mult).then_inc(s_Xs, 1)
                    dve.tensor_tensor(Xs[:, 2:4], X0[:, 2:4], Ed[:, 2:4], ALU.mult).then_inc(s_Xs, 1)
                    dve.wait_ge(s_st, n + 1)
                    dve.tensor_copy(Hs[:, 0], st[:, 0]).then_inc(s_H, 1)
                    dve.wait_ge(s_H, n * 3 + 1)
                    for c in range(1, TT - 1):
                        for i in range(2):
                            ins = dve.scalar_tensor_tensor(Hs[:, c, i, :], Hs[:, c - 1, i, :],
                                                           Ed[:, c, i, P - 1:P], st[:, c, i, :],
                                                           ALU.mult, ALU.add)
                        ins.then_inc(s_H, 1)
                        if c < TT - 2:
                            dve.wait_ge(s_H, n * 3 + c + 1)
                    for r in range(3):
                        for cc in range(2):
                            dve.wait_ge(s_W, n * 6 + 2 * r + cc + 1)
                            dve.tensor_tensor(Wm[:, cc], pair(cc), Dm[:, cc], ALU.mult).then_inc(s_Wm, 1)
                        for cc in range(2 if r < 2 else 0):
                            dve.wait_ge(s_Y, n * 4 + 2 * r + cc + 1)
                            dve.scalar_tensor_tensor(
                                X1[:, 2 * cc:2 * cc + 2].rearrange("p c i t -> p (c i t)"), bank[:, 4 + cc, :],
                                -DAMP, X0[:, 2 * cc:2 * cc + 2].rearrange("p c i t -> p (c i t)"),
                                ALU.mult, ALU.add).then_inc(s_X, 1)
                            dve.wait_ge(s_X, n * 4 + 2 * r + cc + 1)
                            lo = max(1, 2 * cc)
                            dve.tensor_tensor(Xs[:, lo:2 * cc + 2], X1[:, lo:2 * cc + 2], Ed[:, lo:2 * cc + 2],
                                              ALU.mult).then_inc(s_Xs, 1)
                    dve.wait_ge(s_O, n * 2 + 2)
                    own.end()

                def out(n, b, following):
                    dve.tensor_tensor(o[:], O.rearrange("p c i q f -> p c (i q) f"),
                                      bc(alpha[:, bass.ds(n, 1)].rearrange("p n t h -> p (n t) h").unsqueeze(3),
                                         [P, TT, G4, HK]),
                                      ALU.mult).then_inc(s_o, 1)
                    if following:
                        group_gates(n + 1)
                    dve.wait_ge(s_sq, n + 1)
                    dve.reduce_sum(sso[:], sq[:].rearrange("p (a f) -> p a f", f=HK), axis=AX).then_inc(s_ss, 1)
                    if following:
                        convolve(n + 1, 0, 0)
                    dve.wait_ge(s_ro, n + 1)
                    dve.tensor_tensor(on[:].rearrange("p c h f -> p (c h) f"),
                                      o[:].rearrange("p c h f -> p (c h) f"),
                                      bc(ro[:].unsqueeze(2), [P, TT * G4, HK]), ALU.mult).then_inc(s_on, 1)
                    if following:
                        convolve(n + 1, 1, 0)
                        convolve(n + 1, 2, 0)
                    dve.wait_ge(s_oT, n * 8 + 8)
                    dve.tensor_copy(oT[:], bank[:, 4:6, :].rearrange("p h (c t) -> p h c t", c=TT))\
                       .then_inc(s_oTc, 1)
                    if following:
                        convolve(n + 1, 3, 0)
                        convolve(n + 1, 0, 1)
                        convolve(n + 1, 1, 1)
                    dve.wait_ge(s_out, n + 1)
                    xb = k.x[:, bass.ds(b * TT, TT), :].rearrange("p t n -> p (t n)")
                    dve.tensor_tensor(xb, bank[:, 6:8, :].rearrange("p a n -> p (a n)"), xb,
                                      ALU.add).then_inc(s_x, 1)
                    if following:
                        convolve(n + 1, 2, 1)
                        convolve(n + 1, 3, 1)
                    dve.wait_ge(s_x, n + 1 + PRIMED)

                ln.stats(dve)
                ln.scale(dve)
                for b in range(B):
                    ln.keep(dve, b)
                gates_of_all()
                group_gates(0)
                for half in range(2):
                    for lag in range(KW):
                        convolve(0, lag, half)

                def batch(b, last):
                    with dve.Fori(0, HKV - 1) as j:
                        n = b * HKV + j
                        attend(n)
                        out(n, b, True)
                    attend(b * HKV + (HKV - 1))
                    out(b * HKV + (HKV - 1), b, not last)

                with dve.Fori(0, B - 1) as b:
                    batch(b, False)
                batch(B - 1, True)

            @block.scalar
            def _(act):
                own, gate_steps = Chain(act, c_act, 3), Chain(act, c_act_gate, 1)
                act.preload_act_table_set(EXP_LN)
                ln.rstd(act)
                act.wait_ge(s_zero, 2)
                act.wait_ge(s_nw, 48)
                gate_steps.begin(0)
                act.wait_ge(s_az, 1)
                gate_steps.link(act.activation(e1[:], az[:], ACT.Exp, scale=-1.0))
                act.activation(ea[:], rows[:, 0:HQ], ACT.Exp)
                act.activation(eab[:], small[:, :, HQ:], ACT.Exp, scale=-1.0).then_inc(s_es, 1)
                act.activation(l1[:], e1[:], ACT.Ln, bias=1.0).then_inc(s_l1, 1)
                gate_steps.end()

                def silus(n):
                    for at, m in enumerate((2, 3, 0, 1)):
                        act.wait_ge(s_conv, n * 4 + at + 1 + PRIMED)
                        if m < 2:
                            act.activation(X0[:, :, m, :], cv[:, m, :].rearrange("p (c t) -> p c t", c=TT),
                                           ACT.Silu).then_inc(s_silu, 1)
                        else:
                            M, to = (P, kT) if m == 2 else (HK, vT)
                            act.activation(to[:], cv[0:M, m, :], ACT.Silu).then_inc(s_silu, 1)

                def attend(n):
                    own.begin(n)
                    act.preload_act_table_set(EXP_LN)
                    act.wait_ge(s_kvt, n * 8 + 4)
                    for c in range(TT):
                        ins = act.activation(sq[:, c * HK:(c + 1) * HK], kps[:, c, 0:HK], ACT.Square,
                                             accum_out=ssk[:, c:c + 1])
                    own.link(ins)
                    own.link(act.activation(lnk[:], ssk[:], ACT.Ln, bias=k.tiny[:]))
                    act.activation(nk[:], lnk[:], ACT.Exp, scale=0.5).then_inc(s_nk, 1)
                    act.wait_ge(s_E, n * 8 + 8)
                    act.activation(Ed[:].rearrange("p c i t -> p (c i t)"),
                                   bank[:, 6:8, :].rearrange("p a n -> p (a n)"), ACT.Exp).then_inc(s_Ee, 1)
                    act.wait_ge(s_Gc, n + 1)
                    for cc in range(2):
                        act.wait_ge(s_D, n * 2 + cc + 1)
                        for q in range(2):
                            for c in range(2):
                                for i in range(2):
                                    h = 2 * i + q
                                    ins = act.activation(Dm[:, cc, q, c, i, :], pair(cc)[:, q, c, i, :], ACT.Exp,
                                                         bias=negG[:, 2 * cc + c, h:h + 1])
                        ins.then_inc(s_De, 1)
                    act.wait_ge(s_kT, n * 4 + 4)
                    for q in range(2):
                        part = slice(q * HK, (q + 1) * HK)
                        ins = act.activation(kTn[part, q], kps[part], ACT.Copy)
                    ins.then_inc(s_kTc, 1)
                    for c in range(TT - 1):
                        act.wait_ge(s_H, n * 3 + c + 1)
                        for q in range(2):
                            part = slice(q * HK, (q + 1) * HK)
                            ins = act.activation(Hb[part, c, :, :, q, :],
                                                 Hs[part, c].rearrange("p i (a f) -> p i a f", a=2), ACT.Copy)
                        ins.then_inc(s_Hb, 1)

                def out(n):
                    act.wait_ge(s_o, n + 1)
                    act.activation(sq[:], o[:].rearrange("p c h f -> p (c h f)"), ACT.Square).then_inc(s_sq, 1)
                    act.wait_ge(s_ss, n + 1)
                    own.link(act.activation(lno[:], sso[:], ACT.Ln, bias=k.eps[:], scale=1.0 / HK))
                    act.activation(ro[:], lno[:], ACT.Exp, scale=-0.5).then_inc(s_ro, 1)
                    own.end()

                silus(0)

                def batch(b, last):
                    with act.Fori(0, HKV - 1) as j:
                        n = b * HKV + j
                        attend(n)
                        out(n)
                        silus(n + 1)
                    attend(b * HKV + (HKV - 1))
                    out(b * HKV + (HKV - 1))
                    if not last:
                        silus(b * HKV + HKV)

                with act.Fori(0, B - 1) as b:
                    batch(b, False)
                batch(B - 1, True)


def context_attention(nc, k, d):
    ctx = ExitStack()
    with ctx:
        sb, ps, sem = tools(nc, ctx, "ca")
        wq = sb("wq", [P, KD, D])
        wk, wv = sb("wk", [P, D]), sb("wv", [P, D])
        bq, bk = sb("bq", [P, KD]), sb("bk", [P, KD])
        bv = sb("bv", [P, D])
        cT = sb("cT", [P, LC])
        qT = sb("qT", [P, KD, T])
        kT = sb("kT", [P, KD, LC])
        V = sb("V", [P, CT + 1, D])
        Pr = sb("Pr", [P, LC])
        PT = sb("PT", [P, CT, P])
        nm = sb("nm", [P, NT])
        rsum, rinv = sb("rsum", [P, TT]), sb("rinv", [P, TT])
        bank = ps("bank", [P, 8, 512])
        xn, xT = sb("xn", [P, NT, D]), sb("xT", [P, KD, NT * P])
        ln = WholeNorm(k, sb, sem, xn, xT, bank[:, 4:8, :])
        s_w, s_c = sem("w"), sem("c")
        s_kp, s_k, s_qp, s_q, s_vp, s_v = (sem(x) for x in ("kp", "k", "qp", "q", "vp", "v"))
        s_S, s_m, s_e, s_tp, s_t, s_o, s_r, s_x = (sem(x) for x in ("S", "m", "e", "tp", "t", "o", "r", "x"))
        chunks = [(c * 512, min(512, LC - c * 512)) for c in range(4)]
        groups = [(g * 4, min(4, CT - g * 4)) for g in range(4)]
        VG = (CT + 1) // 2
        EARLY = VG // 2
        vbank = [6, 7, 4, 5]

        with nc.Block() as block:
            @block.sync
            def _(sp):
                sp.dma_start(wk[:], d["ca_wk"]).then_inc(s_w, 16)
                sp.dma_start(bk[:], d["ca_bk"]).then_inc(s_w, 16)
                sp.dma_start(wq[:], d["ca_wq"].rearrange("(h p) n -> p h n", p=P)).then_inc(s_w, 16)
                sp.dma_start(bq[:], d["ca_bq"]).then_inc(s_w, 16)
                sp.dma_start(wv[:], d["ca_wv"]).then_inc(s_w, 16)
                sp.dma_start(bv[:], d["ca_bv"]).then_inc(s_w, 16)
                with sp.Fori(0, B) as b:
                    sp.wait_ge(s_vp, b * VG + PRIMED)
                    sp.dma_start(cT[:], d["ctxT"][b]).then_inc(s_c, 16)

            @block.tensor
            def _(pe):
                pe.sem_inc(s_vp, PRIMED)
                for b in range(B):
                    ln.turn(pe, b)
                pe.wait_ge(ln.s_xT, B)
                pe.wait_ge(s_w, 6 * 16)
                with pe.Fori(0, B) as b:
                    pe.wait_ge(s_x, b * TT + PRIMED)
                    pe.wait_ge(s_c, b * 16 + 16)
                    for h in range(KD):
                        if h:
                            pe.wait_ge(s_k, b * 2 + 1)
                        for c, (at, N) in enumerate(chunks):
                            mm = pe.matmul(bank[:, c, 0:N], wk[:, h * P:(h + 1) * P], cT[:, at:at + N],
                                           start=True, stop=True)
                        mm.then_inc(s_kp, 1)
                        for g in range(KD):
                            mm = pe.matmul(bank[:, 4 + h, :], wq[:, g, h * P:(h + 1) * P],
                                           xT[:, g, bass.ds(b * T, T)], start=g == 0, stop=g == KD - 1)
                        mm.then_inc(s_qp, 1)
                    def values(g):
                        if g in (2, 3):
                            pe.wait_ge(s_q, b * 2 + g - 1)
                        if g >= 4:
                            pe.wait_ge(s_v, b * VG + g - 3)
                        for t in range(2 * g, min(2 * g + 2, CT)):
                            kn = P if t < CT - 1 else CLAST
                            mm = pe.matmul(bank[0:kn, vbank[g % 4], (t % 2) * D:(t % 2 + 1) * D],
                                           cT[:, t * P:t * P + kn], wv[:], start=True, stop=True)
                        mm.then_inc(s_vp, 1)

                    for g in range(EARLY):
                        values(g)
                    pe.wait_ge(s_k, b * 2 + 2)
                    pe.wait_ge(s_q, b * 2 + 2)

                    def scores(t):
                        if t:
                            pe.wait_ge(s_e, b * TT + t)
                        for c, (at, N) in enumerate(chunks):
                            for h in range(KD):
                                mm = pe.matmul(bank[:, c, 0:N], qT[:, h, t * P:(t + 1) * P], kT[:, h, at:at + N],
                                               start=h == 0, stop=h == KD - 1)
                        mm.then_inc(s_S, 1)

                    scores(0)
                    for g in range(EARLY, VG):
                        values(g)
                    for t in range(TT):
                        if t + 1 < TT:
                            scores(t + 1)
                        pe.wait_ge(s_e, b * TT + t + 1)
                        if t == 0:
                            pe.wait_ge(s_v, b * VG + VG)
                        for g, (at, count) in enumerate(groups):
                            if t or g >= 2:
                                pe.wait_ge(s_t, (b * TT + t) * 4 + g - 1)
                            for a in range(count):
                                kt = at + a
                                kn = P if kt < CT - 1 else CLAST
                                mm = pe.transpose(bank[0:kn, 4 + g % 2, a * P:(a + 1) * P],
                                                  Pr[:, kt * P:kt * P + kn], k.ident[:])
                            mm.then_inc(s_tp, 1)
                        for g, (at, count) in enumerate(groups):
                            pe.wait_ge(s_t, (b * TT + t) * 4 + g + 1)
                            if g == 0 and t:
                                pe.wait_ge(s_x, b * TT + t + PRIMED)
                            for kt in range(at, at + count):
                                kn = P if kt < CT - 1 else CLAST
                                mm = pe.matmul(bank[:, 6, 0:D], PT[0:kn, kt, :], V[0:kn, kt, :],
                                               start=kt == 0, stop=kt == CT - 1)
                        mm.then_inc(s_o, 1)

            @block.vector
            def _(dve):
                dve.sem_inc(s_x, PRIMED)
                ln.stats(dve)
                ln.scale(dve)
                for b in range(B):
                    ln.keep(dve, b)
                dve.wait_ge(s_w, 6 * 16)
                with dve.Fori(0, B) as b:
                    def values(g):
                        dve.wait_ge(s_vp, b * VG + g + 1 + PRIMED)
                        if g < VG - 1:
                            dve.tensor_tensor(V[:, 2 * g:2 * g + 2, :],
                                              bank[:, vbank[g % 4], :].rearrange("p (a n) -> p a n", a=2),
                                              bc(bv[:].unsqueeze(1), [P, 2, D]), ALU.add).then_inc(s_v, 1)
                        else:
                            dve.tensor_tensor(V[0:CLAST, 2 * g, :], bank[0:CLAST, vbank[g % 4], 0:D], bv[0:CLAST],
                                              ALU.add).then_inc(s_v, 1)

                    for g in range(EARLY):
                        values(g)

                    def top(t):
                        dve.wait_ge(s_S, b * TT + t + 1)
                        dve.reduce_max(nm[:, t:t + 1], bank[:, 0:4, :].rearrange("p a n -> p (a n)")[:, 0:LC],
                                       axis=AX, negate=True).then_inc(s_m, 1)

                    top(0)
                    for g in range(EARLY, VG):
                        values(g)
                    for t in range(TT):
                        if t + 1 < TT:
                            top(t + 1)
                        for g in (0, 2):
                            at, count = groups[g]
                            dve.wait_ge(s_tp, (b * TT + t) * 4 + g + 1)
                            if g == 2:
                                dve.wait_ge(s_t, (b * TT + t) * 4 + 2)
                            dve.tensor_copy(PT[:, at:at + count, :],
                                            bank[:, 4, :].rearrange("p (a n) -> p a n", a=4)).then_inc(s_t, 1)
                        dve.wait_ge(s_e, b * TT + t + 1)
                        dve.reciprocal(rinv[:, t:t + 1], rsum[:, t:t + 1]).then_inc(s_r, 1)
                        dve.wait_ge(s_r, b * TT + t + 1)
                        dve.wait_ge(s_o, b * TT + t + 1)
                        dve.scalar_tensor_tensor(k.x[:, b * TT + t, :], bank[:, 6, 0:D], rinv[:, t:t + 1],
                                                 k.x[:, b * TT + t, :], ALU.mult, ALU.add).then_inc(s_x, 1)
                    dve.wait_ge(s_x, b * TT + TT + PRIMED)

            @block.scalar
            def _(act):
                act.preload_act_table_set(EXP_LN)
                ln.rstd(act)
                act.wait_ge(s_w, 6 * 16)
                with act.Fori(0, B) as b:
                    for h in range(KD):
                        act.wait_ge(s_kp, b * 2 + h + 1)
                        act.activation(kT[:, h, :], bank[:, 0:4, :].rearrange("p a n -> p (a n)")[:, 0:LC],
                                       ACT.Identity, bias=bk[:, h:h + 1]).then_inc(s_k, 1)
                        act.wait_ge(s_qp, b * 2 + h + 1)
                        act.activation(qT[:, h, :], bank[:, 4 + h, :], ACT.Identity,
                                       bias=bq[:, h:h + 1]).then_inc(s_q, 1)

                    def exps(t):
                        act.wait_ge(s_m, b * TT + t + 1)
                        if t:
                            act.wait_ge(s_tp, (b * TT + t) * 4)
                        act.activation(Pr[:], bank[:, 0:4, :].rearrange("p a n -> p (a n)")[:, 0:LC], ACT.Exp,
                                       bias=nm[:, t:t + 1], accum_out=rsum[:, t:t + 1]).then_inc(s_e, 1)

                    exps(0)
                    for t in range(TT):
                        for g in (1, 3):
                            at, count = groups[g]
                            kn = P if g == 1 else CLAST
                            act.wait_ge(s_tp, (b * TT + t) * 4 + g + 1)
                            act.wait_ge(s_t, (b * TT + t) * 4 + g)
                            act.activation(PT[0:kn, at:at + count, :],
                                           bank[0:kn, 5, 0:count * P].rearrange("p (a n) -> p a n", n=P),
                                           ACT.Copy).then_inc(s_t, 1)
                        if t + 1 < TT:
                            exps(t + 1)


def experts(nc, k, d):
    ctx = ExitStack()
    with ctx:
        sb, ps, sem = tools(nc, ctx, "ex")
        xT = sb("xT", [P, KD, NT * P])
        acc = sb("acc", [P, NT, D])
        wr = sb("wr", [P, KD, E])
        br = sb("br", [P, E])
        b2 = sb("b2", [E, D])
        b1 = [sb(f"b1_{i}", [P, FT]) for i in range(2)]
        gamma, beta = sb("gamma", [P, D]), sb("beta", [P, D])
        iota = sb("iota", [P, E])
        iotaw = sb("iotaw", [P, E], mybir.dt.int32)
        lg = sb("lg", [P, NT, E])
        top = sb("top", [P, NT, E])
        idx = sb("idx", [P, NT, E], mybir.dt.uint32)
        idf = sb("idf", [P, NT, 2])
        dif, ex, de, w1s, w2s = (sb(x, [P, NT]) for x in ("dif", "exp", "den", "w1s", "w2s"))
        oh = sb("oh", [P, 2, NT, E])
        rw = sb("rw", [P, NT, E])
        rT = sb("rT", [E, NT, P])
        W1 = [sb(f"W1_{i}", [P, KD, F]) for i in range(2)]
        W2 = [sb(f"W2_{i}", [P, FT, D]) for i in range(2)]
        hT = [sb(f"hT_{i}", [P, FT, T]) for i in range(2)]
        gst, gmv = sb("gst", [P, NT, 6]), sb("gmv", [P, NT, 2])
        gln, grs = sb("gln", [P, NT]), sb("grs", [P, NT])
        spare = sb("spare", [P, 1])
        bank = ps("bank", [P, 8, 512])
        ln = WholeNorm(k, sb, sem, acc, xT, bank[:, 4:8, :])
        s_w = sem("w")
        s_w1, s_w2 = ([sem(f"{x}_{i}") for i in range(2)] for x in ("w1", "w2"))
        s_beta, s_lg, s_rw, s_rtp, s_rT, s_b2, s_acc0 = (
            sem(x) for x in ("beta", "lg", "rw", "rtp", "rT", "b2", "acc0"))
        s_dif, s_ex, s_io = sem("dif"), sem("ex"), sem("iota")
        s_h, s_hr, s_o, s_acc = sem("h"), sem("hr"), sem("o"), sem("acc")
        s_gmv, s_gln, s_grs = sem("gmv"), sem("gln"), sem("grs")
        c_dve = sem("c_dve")

        with nc.Block() as block:
            @block.sync
            def _(sp):
                for tile, name in ((br, "ex_br"), (b2, "ex_b2"), (gamma, "ex_gamma"),
                                   (beta, "ex_beta"), (wr, "ex_wr")):
                    sp.dma_start(tile[:], d[name]).then_inc(s_w, 16)
                def load(e, par):
                    sp.dma_start(W1[par][:], d["ex_w1"][e].rearrange("(h p) f -> p h f", p=P)).then_inc(s_w1[par], 16)
                    sp.dma_start(b1[par][:], d["ex_b1"][e]).then_inc(s_w1[par], 16)
                    sp.dma_start(W2[par][:], d["ex_w2"][e].rearrange("(f p) n -> p f n", p=P)).then_inc(s_w2[par], 16)

                for par in range(2):
                    load(par, par)
                with sp.Fori(0, E // 2 - 1) as e2:
                    for par in range(2):
                        sp.wait_ge(s_o, e2 * (2 * B * TT) + (par + 1) * B * TT)
                        load(e2 * 2 + 2 + par, par)

            @block.gpsimd
            def _(pool):
                pool.iota(iotaw[:], pattern=[[1, E]], base=0, channel_multiplier=0).then_inc(s_io, 1)
                pool.wait_ge(s_io, 1)
                pool.tensor_copy(iota[:], iotaw[:]).then_inc(s_io, 1)

            @block.tensor
            def _(pe):
                for b in range(B):
                    ln.turn(pe, b)
                pe.wait_ge(s_w, 5 * 16)
                for t in range(NT):
                    if t % TT == 0:
                        pe.wait_ge(ln.s_xT, t // TT + 1)
                    for h in range(KD):
                        mm = pe.matmul(bank[:, 0, t * E:(t + 1) * E], xT[:, h, t * P:(t + 1) * P], wr[:, h, :],
                                       start=h == 0, stop=h == KD - 1)
                mm.then_inc(s_lg, 1)
                pe.wait_ge(s_rw, 1)
                for t in range(NT):
                    mm = pe.transpose(bank[0:E, t // 4, (t % 4) * P:(t % 4 + 1) * P], rw[:, t, :], k.ident[:])
                mm.then_inc(s_rtp, 1)
                pe.wait_ge(s_rT, 1)
                for t in range(NT):
                    mm = pe.matmul(bank[:, t // 2, (t % 2) * D:(t % 2 + 1) * D], rT[:, t, :], b2[:],
                                   start=True, stop=True)
                mm.then_inc(s_b2, 1)
                pe.wait_ge(s_acc0, 1)
                with pe.Fori(0, E // 2) as e2:
                    for par in range(2):
                        pe.wait_ge(s_w1[par], e2 * 32 + 32)
                        pe.wait_ge(s_w2[par], e2 * 16 + 16)
                        for b in range(B):
                            u = b % 2
                            n = e2 * (2 * B) + par * B + b
                            for f in range(FT):
                                if f < 4:
                                    pe.wait_ge(s_hr, n * FT + PRIMED)
                                else:
                                    pe.wait_ge(s_hr, n * FT + f - 3 + PRIMED)
                                for h in range(KD):
                                    mm = pe.matmul(bank[:, f % 4, :], W1[par][:, h, f * P:(f + 1) * P],
                                                   xT[:, h, b * T:(b + 1) * T], start=h == 0, stop=h == KD - 1)
                                mm.then_inc(s_h, 1)
                            pe.wait_ge(s_acc, n * TT + PRIMED)
                            for t in range(TT):
                                for f in range(FT):
                                    if t == 0:
                                        pe.wait_ge(s_hr, n * FT + f + 1 + PRIMED)
                                    mm = pe.matmul(bank[:, 4 + t, 0:D], hT[u][:, f, t * P:(t + 1) * P],
                                                   W2[par][:, f, :], start=f == 0, stop=f == FT - 1)
                                mm.then_inc(s_o, 1)

            @block.vector
            def _(dve):
                dve.sem_inc(s_acc, PRIMED)
                own = Chain(dve, c_dve, 20)
                ln.stats(dve)
                ln.scale(dve)
                for b in range(B):
                    ln.keep(dve, b)
                dve.wait_ge(s_w, 5 * 16)
                own.begin(0)
                dve.wait_ge(s_lg, 1)
                own.link(dve.tensor_tensor(lg[:], bank[:, 0, 0:NT * E].rearrange("p (t e) -> p t e", e=E),
                                           bc(br[:].unsqueeze(1), [P, NT, E]), ALU.add))
                dve.tensor_tensor(k.x[:], k.x[:], bc(beta[:].unsqueeze(1), [P, NT, D]), ALU.add).then_inc(s_beta, 1)
                for t in range(NT):
                    ins = dve.max(top[:, t, :], lg[:, t, :])
                own.link(ins)
                for t in range(NT):
                    ins = dve.max_index(idx[:, t, :], top[:, t, :], lg[:, t, :])
                own.link(ins)
                own.link(dve.tensor_copy(idf[:], idx[:, :, 0:2]))
                dve.tensor_tensor(dif[:], top[:, :, 1], top[:, :, 0], ALU.subtract).then_inc(s_dif, 1)
                dve.wait_ge(s_ex, 1)
                own.link(dve.tensor_scalar(de[:], ex[:], 1.0, None, ALU.add))
                own.link(dve.reciprocal(w1s[:], de[:]))
                own.link(dve.tensor_tensor(w2s[:], w1s[:], ex[:], ALU.mult))
                dve.wait_ge(s_io, 2)
                for a in range(2):
                    own.link(dve.tensor_tensor(oh[:, a], bc(iota[:].unsqueeze(1), [P, NT, E]),
                                               bc(idf[:, :, a:a + 1], [P, NT, E]), ALU.is_equal))
                for a, ws in enumerate((w1s, w2s)):
                    own.link(dve.tensor_tensor(oh[:, a], oh[:, a], bc(ws[:].unsqueeze(2), [P, NT, E]), ALU.mult))
                dve.tensor_tensor(rw[:], oh[:, 0], oh[:, 1], ALU.add).then_inc(s_rw, 1)
                dve.wait_ge(s_rtp, 1)
                dve.tensor_copy(rT[:], bank[0:E, 0:4, :].rearrange("p a (t q) -> p (a t) q", q=P)).then_inc(s_rT, 1)
                dve.wait_ge(s_b2, 1)
                dve.tensor_tensor(acc[:].rearrange("p t n -> p (t n)"), bank[:].rearrange("p a n -> p (a n)"),
                                  acc[:].rearrange("p t n -> p (t n)"), ALU.add).then_inc(s_acc0, 1)
                dve.wait_ge(s_acc0, 1)

                def add(e2, par, b):
                    n = e2 * (2 * B) + par * B + b
                    dve.wait_ge(s_acc, n * TT + PRIMED)
                    for t in range(TT):
                        dve.wait_ge(s_o, n * TT + t + 1)
                        tile = b * TT + t
                        dve.scalar_tensor_tensor(acc[:, tile, :], bank[:, 4 + t, 0:D],
                                                 rw[:, tile, bass.ds(e2 * 2 + par, 1)],
                                                 acc[:, tile, :], ALU.mult, ALU.add).then_inc(s_acc, 1)

                def center(b):
                    dve.wait_ge(s_acc, ((E - 1) * B + b + 1) * TT + PRIMED)
                    tiles = range(b * TT, (b + 1) * TT)
                    for t in tiles:
                        ins = dve.bn_stats(gst[:, t, :], acc[:, t, :])
                    own.link(ins)
                    for t in tiles:
                        ins = dve.bn_aggr(gmv[:, t, :], gst[:, t, :])
                    ins.then_inc(s_gmv, 1)
                    dve.wait_ge(s_gmv, b + 1)
                    for t in tiles:
                        ins = dve.scalar_tensor_tensor(acc[:, t, :], acc[:, t, :], gmv[:, t, 0:1], gamma[:],
                                                       ALU.subtract, ALU.mult)
                    own.link(ins)

                def onto_x(b):
                    dve.wait_ge(s_grs, b + 1)
                    for t in range(b * TT, (b + 1) * TT):
                        ins = dve.scalar_tensor_tensor(k.x[:, t, :], acc[:, t, :], grs[:, t:t + 1], k.x[:, t, :],
                                                       ALU.mult, ALU.add)
                    return ins

                with dve.Fori(0, E // 2 - 1) as e2:
                    for par in range(2):
                        for b in range(B):
                            add(e2, par, b)
                for b in range(B):
                    add(E // 2 - 1, 0, b)
                dve.wait_ge(s_beta, 1)
                for b in range(B):
                    add(E // 2 - 1, 1, b)
                    center(b)
                    if b:
                        onto_x(b - 1)
                own.link(onto_x(B - 1))
                own.end()

            @block.scalar
            def _(act):
                act.sem_inc(s_hr, PRIMED)
                act.preload_act_table_set(EXP_LN)
                ln.rstd(act)
                act.wait_ge(s_dif, 1)
                act.activation(ex[:], dif[:], ACT.Exp).then_inc(s_ex, 1)

                def first_layer(e2, par, b):
                    n = e2 * (2 * B) + par * B + b
                    for f in range(FT):
                        act.wait_ge(s_h, n * FT + f + 1)
                        act.activation(hT[b % 2][:, f, :], bank[:, f % 4, :], ACT.Relu,
                                       bias=b1[par][:, f:f + 1]).then_inc(s_hr, 1)

                def rstd(b):
                    tiles = slice(b * TT, (b + 1) * TT)
                    act.wait_ge(s_gmv, b + 1)
                    act.activation(gln[:, tiles], gmv[:, tiles, 1], ACT.Ln, bias=k.ln_eps[:]).then_inc(s_gln, 1)
                    act.wait_ge(s_gln, b + 1)
                    act.activation(grs[:, tiles], gln[:, tiles], ACT.Exp, scale=-0.5).then_inc(s_grs, 1)

                with act.Fori(0, E // 2 - 1) as e2:
                    for par in range(2):
                        for b in range(B):
                            first_layer(e2, par, b)
                for b in range(B):
                    first_layer(E // 2 - 1, 0, b)
                for b in range(B):
                    first_layer(E // 2 - 1, 1, b)
                    if b:
                        rstd(b - 1)
                rstd(B - 1)


class Split:

    Q_PARTS = (0, 0, 0, 1, 1, 2)

    @staticmethod
    def store_queries(sp, dram, b, half, parts, stored):
        for slot, part in enumerate(Split.Q_PARTS):
            sp.dma_start(dram[b, half * 8:half * 8 + 8, slot], parts[:, part, :]).then_inc(stored, 16)

    @staticmethod
    def store_keys(sp, dram, b, half, parts, stored):
        for part in range(3):
            sp.dma_start(dram[b, half * 8:half * 8 + 8, part], parts[:, part, :]).then_inc(stored, 16)

    @staticmethod
    def load_queries(sp, dram, b, g, q, loaded):
        sp.dma_start(q[0:6 * HD], dram[b, 4 * g:4 * g + 4].rearrange("h r f t -> (r f) h t")).then_inc(loaded, 16)

    @staticmethod
    def load_keys(sp, dram, b, g, kk, loaded):
        for at, count in ((0, 3), (3, 2), (5, 1)):
            sp.dma_start(kk[at * HD:(at + count) * HD],
                         dram[b, 4 * g:4 * g + 4, 0:count].rearrange("h r f t -> (r f) h t")).then_inc(loaded, 16)

    STORES = 6 + 3
    LOADS = 1 + 3


class Heads:

    ROWS, FULL = 6 * HD, 6 * HD + 3

    def __init__(self, nc, sb, sem, name, keys, causal):
        self.keys, self.causal = keys, causal
        self.tiles = [(at, min(P, keys - at)) for at in range(0, keys, P)]
        self.U = 2 * len(self.tiles)
        parts = -(-keys // 512)
        cuts = [keys * c // parts for c in range(parts + 1)]
        self.chunks = [(cuts[c], cuts[c + 1] - cuts[c]) for c in range(parts)]
        self.NM = TT * 4 * parts
        self.q = [sb(f"{name}_q{u}", [P, 4, T], BF16) for u in range(2)]
        self.k = [sb(f"{name}_k{u}", [P, 4, keys], BF16) for u in range(2)]
        self.V = sb(f"{name}_V", [P, len(self.tiles), H, SH])
        self.y = sb(f"{name}_y", [P, TT, D])
        self.dq = nc.dram_tensor(f"{name}_q_parts", (B, H, 6, HD, T), BF16, kind="Internal").ap()
        self.dk = nc.dram_tensor(f"{name}_k_parts", (B, H, 3, HD, keys), BF16, kind="Internal").ap()
        self.loaded = [sem(f"{name}_loaded{u}") for u in range(2)]
        self.s_const = sem(f"{name}_const")

    def clear(self, pool):
        for u in range(2):
            pool.memset(self.k[u][self.ROWS:self.FULL], 1.0).then_inc(self.s_const, 1)
            pool.wait_ge(self.s_const, u + 1)
        pool.memset(self.V[:], 0.0).then_inc(self.s_const, 1)
        pool.wait_ge(self.s_const, 3)
        pool.memset(self.V[:, :, :, HD:HD + 1], 1.0).then_inc(self.s_const, 1)
        pool.wait_ge(self.s_const, 4)


class Call:

    def __init__(self, kind, g):
        self.kind, self.g, self.u = kind, g, g % 2


class Batch:

    def __init__(self, calls, prep, last):
        self.calls = [Call(*c) for c in calls]
        self.last = last
        side = -4
        self.prep_side = {}
        pairs = tiles = 0
        for i, c in enumerate(self.calls):
            c.pair0, c.tile0 = pairs, tiles
            pairs += c.kind.U
            tiles += c.kind.U // 2
            c.turn0, c.turned = side, side + 4
            side += 4
            if i:
                self.calls[i - 1].out0 = side
                side += 1
            maxima = self.calls[i + 1].kind.NM if i + 1 < len(calls) else 0
            c.preps = list(prep[i])
            c.beside0 = side
            c.beside = [("max", j) for j in range(maxima)]
            for at, u in enumerate(c.preps):
                c.beside.insert((at + 1) * maxima // (len(c.preps) + 1) + at, ("prep", u))
            for j, (what, u) in enumerate(c.beside):
                if what == "prep":
                    self.prep_side[u] = side + j
            side += len(c.beside)
        self.calls[-1].out0 = side
        self.first0 = side + 1
        self.sides = self.first0 + (0 if last else self.calls[0].kind.NM + 4)


class Attention:

    PAIRS, SIDES, PROBS = 2, 3, 4
    SCALE = HD ** -0.5
    LINKS = 4

    def __init__(self, k, sb, sem, bank, calls, prep, prep_at):
        self.k, self.bank, self.prep = k, bank, prep
        self.NC = len(calls)
        self.with_prep, self.alone = Batch(calls, prep_at, False), Batch(calls, [()] * self.NC, True)
        self.calls = self.alone.calls
        self.NU = sum(c.kind.U for c in self.calls)
        self.NK = self.NU // 2
        self.part = sb("at_part", [P, TT, 4, 4])
        self.mx, self.rest = sb("at_mx", [P, TT * 4]), sb("at_rest", [P, TT * 4])
        self.m3 = sb("at_m3", [P, TT * 4, 3], BF16)
        self.pr = sb("at_pr", [P, self.PROBS, 2, T])
        self.yT = sb("at_yT", [P, T])
        self.rec = sb("at_rec", [P, TT, 4])
        (self.side_full, self.side_free, self.s_m3, self.s_link, self.scored, self.weighed, self.summed,
         self.s_yT, self.s_rec) = (sem(f"at_{x}") for x in (
             "side_full", "side_free", "m3", "link", "scored", "weighed", "summed", "yT", "rec"))

    def before(self, b):
        return b * self.with_prep.sides + (self.prep.STEPS + self.calls[0].kind.NM + 4)

    def alone_done(self, u):
        return u + 1

    def done(self, b):
        return lambda u: self.before(b) + (self.with_prep.prep_side[u] + 1)


    def side_bank(self, pe, s0, j):
        if j >= self.SIDES:
            pe.wait_ge(self.side_free, s0 + (j - self.SIDES + 1))
        return self.bank[:, 4 + j % self.SIDES, :]

    def maximum_of(self, c, j):
        th, chunk = divmod(j, len(c.kind.chunks))
        t, h = divmod(th, 4)
        at, N = c.kind.chunks[chunk]
        if c.kind.causal:
            N = P * (t + 1)
        return t, h, chunk, at, N

    def pe_max(self, pe, b, s0, side, c, j):
        t, h, chunk, at, N = self.maximum_of(c, j)
        if j == 0:
            pe.wait_ge(c.kind.loaded[c.u], (b * (NG // 2) + c.g // 2 + 1) * Split.LOADS * 16)
        dst = self.side_bank(pe, s0, side)
        mm = pe.matmul(dst[:, 0:N], c.kind.q[c.u][0:Heads.ROWS, h, t * P:(t + 1) * P],
                       c.kind.k[c.u][0:Heads.ROWS, h, at:at + N], start=True, stop=True)
        if c.kind.causal:
            mm = pe.matmul(dst[:, N - P:N], self.k.identb[:], self.k.mask_qk[:], start=False, stop=True,
                           skip_group_check=True)
        mm.then_inc(self.side_full, 1)

    def pe_turn(self, pe, b, s0, i, turn0):
        for h in range(4):
            dst = self.side_bank(pe, s0, turn0 + h)
            pe.wait_ge(self.s_m3, b * self.NC + i + 1)
            for t in range(TT):
                mm = pe.matmul(dst[Heads.ROWS:Heads.FULL, t * P:(t + 1) * P], self.m3[:, t * 4 + h, :],
                               self.k.identb[:], start=True, stop=True)
            mm.then_inc(self.side_full, 1)

    def span(self, c, kt):
        return (kt * P, T) if c.kind.causal else (0, T)

    def pe_scores(self, pe, b, i, s):
        c = self.calls[i]
        kt, pp = divmod(s, 2)
        at, kn = c.kind.tiles[kt]
        lo, hi = self.span(c, kt)
        pair = c.pair0 + s
        if pair >= self.PAIRS:
            pe.wait_ge(self.weighed, b * self.NU + pair - self.PAIRS + 1)
        for a in range(2):
            mm = pe.matmul(self.bank[0:kn, 2 * (pair % self.PAIRS) + a, 0:hi - lo],
                           c.kind.k[c.u][0:Heads.FULL, 2 * pp + a, at:at + kn],
                           c.kind.q[c.u][0:Heads.FULL, 2 * pp + a, lo:hi], start=True, stop=True)
        if c.kind.causal:
            for a in range(2):
                mm = pe.matmul(self.bank[:, 2 * (pair % self.PAIRS) + a, 0:P], self.k.identb[:],
                               self.k.mask_kq[:], start=False, stop=True, skip_group_check=True)
        mm.then_inc(self.scored, 1)

    def pe_values(self, pe, b, i, kt, pp):
        c = self.calls[i]
        _, kn = c.kind.tiles[kt]
        lo, hi = self.span(c, kt)
        if kt == 0 and i and pp == 0:
            pe.wait_ge(self.s_yT, b * self.NC + i)
        if kt == 0 and pp == 0 and self.prep.values_of(c.kind, c.g):
            pe.wait_ge(self.prep.s_values, self.prep.values_of(c.kind, c.g) + b * self.prep.VALUES)
        pair = c.pair0 + 2 * kt + pp
        pe.wait_ge(self.weighed, b * self.NU + pair + 1)
        for h in range(2 * pp, 2 * pp + 2):
            mm = pe.matmul(self.bank[h * SH:(h + 1) * SH, 7, lo:hi], c.kind.V[0:kn, kt, 4 * c.g + h, :],
                           self.pr[0:kn, pair % self.PROBS, h % 2, 0:hi - lo], start=kt == 0,
                           stop=kt == len(c.kind.tiles) - 1, skip_group_check=True)
        if pp == 1:
            mm.then_inc(self.summed, 1)

    def pe_out(self, pe, b, s0, i, c):
        dst = self.side_bank(pe, s0, c.out0)
        pe.wait_ge(self.s_yT, b * self.NC + i + 1)
        for t in range(TT):
            mm = pe.transpose(dst[:, t * P:(t + 1) * P], self.yT[:, t * P:(t + 1) * P], self.k.ident[:])
        mm.then_inc(self.side_full, 1)

    def pe_prepare(self, pe, b):
        for u in range(self.prep.STEPS):
            self.prep.pe(pe, b, u, self.side_bank(pe, 0, u), self.side_free, self.alone_done)\
                .then_inc(self.side_full, 1)
        self.pe_first_max(pe, b, 0, self.prep.STEPS)
        self.pe_turn(pe, b, 0, 0, self.prep.STEPS + self.calls[0].kind.NM)

    def pe_first_max(self, pe, b, s0, side):
        for j in range(self.calls[0].kind.NM):
            self.pe_max(pe, b, s0, side + j, self.calls[0], j)

    def pe_batch(self, pe, b, s0, batch, projection, y, s_y):
        pe.wait_ge(self.side_free, s0)
        pe.wait_ge(projection.s_x, b + PRIMED)
        for i, c in enumerate(batch.calls):
            following = batch.calls[i + 1] if i + 1 < self.NC else None
            steps = c.kind.U + 2
            first, last, count = 4, 2 * steps - 10, len(c.beside)

            def beside(place):
                for j in range(count * min(max(place - first, 0), last - first) // (last - first),
                               count * min(max(place + 1 - first, 0), last - first) // (last - first)):
                    what, step = c.beside[j]
                    if what == "max":
                        self.pe_max(pe, b, s0, c.beside0 + j, following, step)
                    else:
                        self.prep.pe(pe, b + 1, step, self.side_bank(pe, s0, c.beside0 + j), self.side_free,
                                     self.done(b)).then_inc(self.side_full, 1)

            for s in range(steps):
                if s < 2 and i:
                    pe.wait_ge(self.side_free, s0 + (c.turned - 2 + 2 * s))
                if s == 2 and i:
                    self.pe_out(pe, b, s0, i - 1, batch.calls[i - 1])
                if s < c.kind.U:
                    self.pe_scores(pe, b, i, s)
                beside(2 * s if s % 2 == 0 else 2 * s - 1)
                if s == steps - 2 and following:
                    self.pe_turn(pe, b, s0, i + 1, following.turn0)
                if s % 2:
                    for pair in range(2):
                        if s >= 3:
                            self.pe_values(pe, b, i, (s - 3) // 2, pair)
                        beside(2 * s + pair)
        self.pe_out(pe, b, s0, self.NC - 1, batch.calls[-1])
        if not batch.last:
            self.pe_first_max(pe, b + 1, s0, batch.first0)
        pe.wait_ge(s_y, b + 1)
        projection.pe_turn(pe, y)
        if not batch.last:
            self.pe_turn(pe, b + 1, s0, 0, batch.first0 + self.calls[0].kind.NM)
        projection.pe_product(pe, b)


    def dve_prepare(self, dve, b):
        self.prep.dve_start(dve, b)
        for i, c in enumerate(self.with_prep.calls):
            for u in c.preps:
                dve.wait_ge(self.side_full, u + 1)
                self.prep.dve(dve, b, u, self.bank[:, 4 + u % self.SIDES, :]).then_inc(self.side_free, 1)
            self.prep.dve_between(dve, b, i)
        self.dve_first_max(dve, 0, self.prep.STEPS)
        self.dve_turn(dve, b, 0, 0, self.prep.STEPS + self.calls[0].kind.NM)

    def dve_first_max(self, dve, s0, side):
        for j in range(self.calls[0].kind.NM):
            self.dve_max(dve, s0, side + j, self.calls[0], j)

    def dve_max(self, dve, s0, side, c, step):
        t, h, chunk, _, N = self.maximum_of(c, step)
        dve.wait_ge(self.side_full, s0 + (side + 1))
        dve.reduce_max(self.part[:, t, h, chunk:chunk + 1], self.bank[:, 4 + side % self.SIDES, 0:N],
                       axis=AX).then_inc(self.side_free, 1)

    def dve_turn(self, dve, b, s0, i, turn0):
        c = self.calls[i]
        n = b * (self.NC * self.LINKS) + i * self.LINKS
        dve.wait_ge(self.side_free, s0 + turn0)
        dve.reduce_max(self.mx[:], self.part[:, :, :, 0:len(c.kind.chunks)].rearrange("p t h c -> p (t h) c"),
                       axis=AX, negate=True).then_inc(self.s_link, 1)
        dve.wait_ge(self.s_link, n + 1)
        dve.tensor_copy(self.m3[:, :, 0], self.mx[:]).then_inc(self.s_link, 1)
        dve.wait_ge(self.s_link, n + 2)
        dve.tensor_tensor(self.rest[:], self.mx[:], self.m3[:, :, 0], ALU.subtract).then_inc(self.s_link, 1)
        dve.wait_ge(self.s_link, n + 3)
        dve.tensor_copy(self.m3[:, :, 1], self.rest[:]).then_inc(self.s_link, 1)
        dve.wait_ge(self.s_link, n + 4)
        dve.tensor_tensor(self.m3[:, :, 2], self.rest[:], self.m3[:, :, 1], ALU.subtract).then_inc(self.s_m3, 1)
        for h in range(4):
            j = turn0 + h
            dve.wait_ge(self.side_full, s0 + (j + 1))
            dve.tensor_copy(c.kind.q[c.u][Heads.ROWS:Heads.FULL, h, :],
                            self.bank[Heads.ROWS:Heads.FULL, 4 + j % self.SIDES, :]).then_inc(self.side_free, 1)

    def dve_out(self, dve, b, s0, i, c):
        dve.wait_ge(self.summed, b * self.NK + c.tile0 + c.kind.U // 2)
        dve.tensor_copy(self.yT[:], self.bank[:, 7, :]).then_inc(self.s_yT, 1)
        dve.wait_ge(self.side_full, s0 + (c.out0 + 1))
        src = self.bank[:, 4 + c.out0 % self.SIDES, :].rearrange("p (t h f) -> p t h f", t=TT, h=4)
        dve.reciprocal(self.rec[:], src[:, :, :, HD]).then_inc(self.s_rec, 1)
        dve.wait_ge(self.s_rec, b * self.NC + i + 1)
        dve.tensor_tensor(c.kind.y[:, :, c.g * 64:(c.g + 1) * 64].rearrange("p t (h f) -> p t h f", f=HD),
                          src[:, :, :, 0:HD], bc(self.rec[:].unsqueeze(3), [P, TT, 4, HD]), ALU.mult)\
           .then_inc(self.side_free, 1)

    def dve_batch(self, dve, b, s0, batch, projection, add, s_y):
        if batch is self.with_prep:
            self.prep.dve_start(dve, b + 1)
        for i, c in enumerate(batch.calls):
            for j, (what, step) in enumerate(c.beside):
                side = c.beside0 + j
                if what == "max":
                    self.dve_max(dve, s0, side, batch.calls[i + 1], step)
                else:
                    dve.wait_ge(self.side_full, s0 + (side + 1))
                    self.prep.dve(dve, b + 1, step, self.bank[:, 4 + side % self.SIDES, :])\
                        .then_inc(self.side_free, 1)
            if i + 1 < self.NC:
                self.dve_turn(dve, b, s0, i + 1, batch.calls[i + 1].turn0)
            self.dve_out(dve, b, s0, i, c)
            if batch is self.with_prep:
                self.prep.dve_between(dve, b + 1, i)
        dve.wait_ge(self.side_free, s0 + batch.first0)
        add(dve).then_inc(s_y, 1)
        if not batch.last:
            self.dve_first_max(dve, s0, batch.first0)
        projection.dve_turn(dve, b)
        if not batch.last:
            self.dve_turn(dve, b + 1, s0, 0, batch.first0 + self.calls[0].kind.NM)
        projection.dve_add(dve, b)


    def act_prepare(self, act, b):
        self.prep.act_start(act, b)
        for i in range(self.NC):
            self.prep.act_between(act, b, i)

    def act_batch(self, act, b, batch):
        if batch is self.with_prep:
            self.prep.act_start(act, b + 1)
        for i, c in enumerate(batch.calls):
            if batch is self.with_prep:
                self.prep.act_between(act, b + 1, i)
            for s in range(c.kind.U):
                kt, pp = divmod(s, 2)
                _, kn = c.kind.tiles[kt]
                lo, hi = self.span(c, kt)
                pair = c.pair0 + s
                act.wait_ge(self.scored, b * self.NU + pair + 1)
                if pair >= self.PROBS:
                    act.wait_ge(self.summed, b * self.NK + (pair - self.PROBS) // 2 + 1)
                r = 2 * (pair % self.PAIRS)
                act.activation(self.pr[0:kn, pair % self.PROBS, :, 0:hi - lo], self.bank[0:kn, r:r + 2, 0:hi - lo],
                               ACT.Exp, scale=self.SCALE).then_inc(self.weighed, 1)


    def sp_load(self, sp, b, i, ahead=False, fresh=False):
        c = self.calls[i]
        for before in self.calls:
            if before.kind is c.kind and before.g == (c.g - 2) % NG and not fresh:
                scored = before.pair0 + before.kind.U
                sp.wait_ge(self.scored, (b + 1) * self.NU - (self.NU - scored) if ahead else b * self.NU + scored)
        dq, dk = (x[1:] if ahead else x for x in (c.kind.dq, c.kind.dk))
        Split.load_queries(sp, dq, b, c.g, c.kind.q[c.u], c.kind.loaded[c.u])
        Split.load_keys(sp, dk, b, c.g, c.kind.k[c.u], c.kind.loaded[c.u])


class Project:

    def __init__(self, nc, k, sb, sem, bank, name, yT):
        self.k, self.bank, self.yT = k, bank, yT
        self.w, self.bias = sb(f"{name}_w", [P, KD, D]), sb(f"{name}_b", [P, D])
        self.s_w, self.s_t, self.s_c, self.s_p, self.s_b, self.s_x = (
            sem(f"{name}_{x}") for x in ("w", "t", "c", "p", "b", "x"))

    def load(self, sp, w, bias):
        sp.dma_start(self.w[:], w.rearrange("(h p) n -> p h n", p=P)).then_inc(self.s_w, 16)
        sp.dma_start(self.bias[:], bias).then_inc(self.s_w, 16)

    def pe_turn(self, pe, y):
        pe.wait_ge(self.s_w, 32)
        for h in range(KD):
            for t in range(TT):
                mm = pe.transpose(self.bank[:, h, t * P:(t + 1) * P], y[:, t, h * P:(h + 1) * P], self.k.ident[:])
        mm.then_inc(self.s_t, 1)

    def pe_product(self, pe, n):
        pe.wait_ge(self.s_c, n + 1)
        for t in range(TT):
            for h in range(KD):
                mm = pe.matmul(self.bank[:, 2 + t // 2, (t % 2) * D:(t % 2 + 1) * D],
                               self.yT[:, h, t * P:(t + 1) * P], self.w[:, h, :], start=h == 0, stop=h == KD - 1)
        mm.then_inc(self.s_p, 1)

    def dve_turn(self, dve, n):
        dve.wait_ge(self.s_t, n + 1)
        dve.tensor_copy(self.yT[:], self.bank[:, 0:2, :]).then_inc(self.s_c, 1)

    def dve_add(self, dve, n):
        x = self.k.x[:, bass.ds(n * TT, TT), :]
        dve.wait_ge(self.s_w, 32)
        dve.tensor_tensor(x, x, bc(self.bias[:].unsqueeze(1), [P, TT, D]), ALU.add).then_inc(self.s_b, 1)
        dve.wait_ge(self.s_b, n + 1)
        dve.wait_ge(self.s_p, n + 1)
        dve.tensor_tensor(x.rearrange("p t n -> p (t n)"), self.bank[:, 2:4, :].rearrange("p a n -> p (a n)"),
                          x.rearrange("p t n -> p (t n)"), ALU.add).then_inc(self.s_x, 1)


class SelfPrep:

    TURN, QK, V = KD, TT, TT // 2
    STEPS = TURN + QK + V + 2 * KD
    POOL = 3 + 4 * KD
    VALUES = 1

    def __init__(self, nc, k, sb, sem, heads):
        self.k, self.heads = k, heads
        self.ln = Norm(nc, k, sb, sem)
        self.w, self.bias = sb("w", [P, KD, 3 * D]), sb("bias", [P, 3 * D])
        self.nw = sb("nw", [P, 2 * D])
        self.qk, self.sq = sb("qk", [P, TT, 2 * D]), sb("sq", [P, TT, 2 * D])
        self.ss, self.lg, self.rs = (sb(x, [P, TT, 2 * H]) for x in ("ss", "lg", "rs"))
        self.nv = sb("nv", [P, TT, D])
        self.full = sb("full", [P, 2 * KD, T])
        self.parts = sb("parts", [P, KD, 3, 2, T], BF16)
        self.s_w, self.s_ss, self.s_lg, self.s_rs, self.s_pool, self.s_values = (
            sem(x) for x in ("w", "ss", "lg", "rs", "pool", "values"))
        self.stored = [sem(f"stored{half}") for half in range(KD)]

    def values_of(self, kind, g):
        return 1 + PRIMED if g == 0 else 0

    def load(self, sp, d):
        sp.dma_start(self.w[:], d["sa_w"].rearrange("(h p) n -> p h n", p=P)).then_inc(self.s_w, 16)
        sp.dma_start(self.bias[:], d["sa_b"]).then_inc(self.s_w, 16)
        sp.dma_start(self.nw[:], d["sa_nw"]).then_inc(self.s_w, 16)

    def step(self, u):
        order = ([("turn", h) for h in range(self.TURN)] + [("q | k", t) for t in range(self.QK)]
                 + [("v", v) for v in range(self.V)] + [("normed", a) for a in range(2 * KD)])
        return order[u]

    def pe(self, pe, n, u, dst, side_free, done):
        ln = self.ln
        what, a = self.step(u)
        if what == "turn":
            if a == 0:
                pe.wait_ge(ln.s_xn, n * TT + TT)
            for t in range(TT):
                mm = pe.transpose(dst[:, t * P:(t + 1) * P], ln.xn[:, t, a * P:(a + 1) * P], self.k.ident[:])
        elif what == "q | k":
            if a == 0:
                pe.wait_ge(side_free, done(self.TURN - 1))
            for h in range(KD):
                mm = pe.matmul(dst, ln.xT[:, h, a * P:(a + 1) * P], self.w[:, h, 0:2 * D],
                               start=h == 0, stop=h == KD - 1)
        elif what == "v":
            for t in range(2 * a, 2 * a + 2):
                for h in range(KD):
                    mm = pe.matmul(dst[:, (t % 2) * D:(t % 2 + 1) * D], ln.xT[:, h, t * P:(t + 1) * P],
                                   self.w[:, h, 2 * D:], start=h == 0, stop=h == KD - 1)
        else:
            if a == 0:
                pe.wait_ge(self.s_pool, n * self.POOL + 3 + PRIMED)
            half, tensor = divmod(a, 2)
            at = tensor * D + half * P
            for t in range(TT):
                mm = pe.transpose(dst[:, t * P:(t + 1) * P], self.sq[:, t, at:at + P], self.k.ident[:])
        return mm

    def dve(self, dve, n, u, src):
        what, a = self.step(u)
        if what == "turn":
            return dve.tensor_copy(self.ln.xT[:, a, :], src)
        if what == "q | k":
            if a == 0:
                dve.wait_ge(self.s_pool, n * self.POOL + PRIMED)
            return dve.tensor_tensor(self.qk[:, a, :], src, self.bias[:, 0:2 * D], ALU.add)
        if what == "v":
            if a == 0:
                dve.wait_ge(self.s_values, n * self.VALUES + PRIMED)
            return dve.tensor_tensor(self.nv[:, 2 * a:2 * a + 2, :], src.rearrange("p (t n) -> p t n", n=D),
                                     bc(self.bias[:, 2 * D:].unsqueeze(1), [P, 2, D]), ALU.add)
        return dve.tensor_copy(self.full[:, a, :], src)

    def dve_start(self, dve, n):
        self.ln.stats(dve, n, n)
        self.ln.scale(dve, n, n)

    def dve_between(self, dve, n, i):
        if i == 0:
            dve.wait_ge(self.s_pool, n * self.POOL + 1 + PRIMED)
            dve.reduce_sum(self.ss[:], self.sq[:].rearrange("p t (a f) -> p t a f", f=HD), axis=AX)\
               .then_inc(self.s_ss, 1)

    def act_start(self, act, n):
        self.ln.rstd_of(act, n)

    def act_between(self, act, n, i):
        if i == 1:
            act.wait_ge(self.s_ss, n + 1)
            act.activation(self.lg[:], self.ss[:], ACT.Ln, bias=self.k.eps[:], scale=1.0 / HD).then_inc(self.s_lg, 1)
            act.wait_ge(self.s_lg, n + 1)
            act.activation(self.rs[:], self.lg[:], ACT.Exp, scale=-0.5).then_inc(self.s_rs, 1)

    def pool(self, pool, n, side_free, done):
        qk, sq, full, parts = self.qk, self.sq, self.full, self.parts
        by_head = "p t (a f) -> p t a f"
        made = n * self.POOL + PRIMED
        pool.wait_ge(side_free, done(self.TURN + self.QK - 1))
        pool.tensor_tensor(sq[:], qk[:], qk[:], ALU.mult).then_inc(self.s_pool, 1)
        pool.wait_ge(self.s_rs, n + 1)
        pool.tensor_tensor(sq[:].rearrange(by_head, f=HD), qk[:].rearrange(by_head, f=HD),
                           bc(self.rs[:].unsqueeze(3), [P, TT, 2 * H, HD]), ALU.mult).then_inc(self.s_pool, 1)
        pool.wait_ge(self.s_pool, made + 2)
        pool.tensor_tensor(sq[:], sq[:], bc(self.nw[:].unsqueeze(1), [P, TT, 2 * D]), ALU.mult)\
            .then_inc(self.s_pool, 1)
        ones = bc(self.k.one[:].unsqueeze(2), [P, 2, T])
        for half in range(KD):
            if not (isinstance(n, int) and n == 0):
                pool.wait_ge(self.stored[half], n * (16 * Split.STORES))
            f = full[:, 2 * half:2 * half + 2, :]
            at = 3 + 4 * half
            pool.wait_ge(side_free, done(self.TURN + self.QK + self.V + 2 * half + 1))
            pool.tensor_tensor(parts[:, half, 0], f, ones, ALU.mult).then_inc(self.s_pool, 1)
            pool.wait_ge(self.s_pool, made + (at + 1))
            pool.tensor_tensor(f, f, parts[:, half, 0], ALU.subtract).then_inc(self.s_pool, 1)
            pool.wait_ge(self.s_pool, made + (at + 2))
            pool.tensor_tensor(parts[:, half, 1], f, ones, ALU.mult).then_inc(self.s_pool, 1)
            pool.wait_ge(self.s_pool, made + (at + 3))
            pool.tensor_tensor(parts[:, half, 2], f, parts[:, half, 1], ALU.subtract).then_inc(self.s_pool, 1)

    def store(self, sp, n, half):
        sp.wait_ge(self.s_pool, n * self.POOL + (3 + 4 * (half + 1) + PRIMED))
        Split.store_queries(sp, self.heads.dq, n, half, self.parts[:, half, :, 0], self.stored[half])
        Split.store_keys(sp, self.heads.dk, n, half, self.parts[:, half, :, 1], self.stored[half])

    def act_values(self, act, n, side_free, done):
        act.wait_ge(side_free, done(self.TURN + self.QK + self.V - 1))
        act.activation(self.heads.V[:, :, :, 0:HD], self.nv[:].rearrange("p t (h f) -> p t h f", f=HD), ACT.Copy)\
           .then_inc(self.s_values, 1)


def self_attention(nc, k, d):
    ctx = ExitStack()
    with ctx:
        sb, ps, sem = tools(nc, ctx, "sa")
        bank = ps("bank", [P, 8, 512])
        heads = Heads(nc, sb, sem, "sa", T, False)
        prep = SelfPrep(nc, k, sb, sem, heads)
        first = prep.TURN + prep.QK
        prep_at = (range(first), range(first, first + prep.V), range(first + prep.V, prep.STEPS), ())
        at = Attention(k, sb, sem, bank, [(heads, g) for g in range(NG)], prep, prep_at)
        pr = Project(nc, k, sb, sem, bank, "pr", prep.ln.xT)
        s_y, spare = sem("y"), sb("spare", [P, 1])
        STORED = 16 * Split.STORES

        with nc.Block() as block:
            @block.sync
            def _(sp):
                prep.load(sp, d)
                pr.load(sp, d["sa_wp"], d["sa_bp"])
                prep.store(sp, 0, 0)
                sp.wait_ge(prep.stored[0], STORED)
                at.sp_load(sp, 0, 0, fresh=True)
                at.sp_load(sp, 0, 1, fresh=True)
                prep.store(sp, 0, 1)
                with sp.Fori(0, B - 1) as b:
                    sp.wait_ge(prep.stored[1], b * STORED + STORED)
                    at.sp_load(sp, b, 2)
                    at.sp_load(sp, b, 3)
                    prep.store(sp, b + 1, 0)
                    sp.wait_ge(prep.stored[0], (b + 2) * STORED)
                    at.sp_load(sp, b, 0, ahead=True)
                    at.sp_load(sp, b, 1, ahead=True)
                    prep.store(sp, b + 1, 1)
                sp.wait_ge(prep.stored[1], B * STORED)
                at.sp_load(sp, B - 1, 2)
                at.sp_load(sp, B - 1, 3)

            @block.gpsimd
            def _(pool):
                pool.sem_inc(prep.s_pool, PRIMED)
                heads.clear(pool)
                pool.wait_ge(prep.s_w, 48)
                prep.pool(pool, 0, at.side_free, at.alone_done)
                with pool.Fori(0, B - 1) as b:
                    prep.pool(pool, b + 1, at.side_free, at.done(b))

            @block.tensor
            def _(pe):
                pe.wait_ge(heads.s_const, 4)
                pe.wait_ge(prep.s_w, 48)
                at.pe_prepare(pe, 0)

                with pe.Fori(0, B - 1) as b:
                    at.pe_batch(pe, b, at.before(b), at.with_prep, pr, heads.y, s_y)
                at.pe_batch(pe, B - 1, at.before(B - 1), at.alone, pr, heads.y, s_y)

            @block.vector
            def _(dve):
                dve.sem_inc(pr.s_x, PRIMED)
                dve.wait_ge(heads.s_const, 4)
                dve.wait_ge(prep.s_w, 48)
                at.dve_prepare(dve, 0)

                def nothing_to_add(dve):
                    return dve.memset(spare[:], 0.0)

                with dve.Fori(0, B - 1) as b:
                    at.dve_batch(dve, b, at.before(b), at.with_prep, pr, nothing_to_add, s_y)
                at.dve_batch(dve, B - 1, at.before(B - 1), at.alone, pr, nothing_to_add, s_y)

            @block.scalar
            def _(act):
                act.sem_inc(prep.s_values, PRIMED)
                act.preload_act_table_set(EXP_LN)
                act.wait_ge(heads.s_const, 4)
                at.act_prepare(act, 0)
                prep.act_values(act, 0, at.side_free, at.alone_done)
                with act.Fori(0, B - 1) as b:
                    at.act_batch(act, b, at.with_prep)
                    act.wait_ge(at.summed, b * at.NK + at.NK)
                    prep.act_values(act, b + 1, at.side_free, at.done(b))
                at.act_batch(act, B - 1, at.alone)


class CrossPrep:

    TURN, QUERIES, CHUNKS = 2, 3, 4
    OWN_V, CON_V = TT // 2, -(-CT // 2)
    HALF = QUERIES + CHUNKS
    STEPS = TURN + 2 * HALF + OWN_V + CON_V
    VALUES = 2

    def __init__(self, nc, k, sb, sem, own, con):
        self.k, self.own, self.con = k, own, con
        self.ln = Norm(nc, k, sb, sem)
        self.w = sb("w", [P, KD, 4 * D])
        self.wc = sb("wc", [P, 2 * D])
        self.bcol = sb("bcol", [P, KD, 4])
        self.brow = sb("brow", [P, 2, D])
        self.cT = sb("cT", [P, LC])
        self.N = 3 * T + LC
        self.full = sb("full", [P, self.N])
        self.parts = sb("parts", [P, 3, self.N], BF16)
        self.nv, self.ncv = sb("nv", [P, TT, D]), sb("ncv", [P, CT, D])
        self.s_w, self.s_c, self.s_split, self.s_values = (sem(x) for x in ("w", "c", "split", "values"))
        self.stored = [sem(f"stored{half}") for half in range(KD)]

    def values_of(self, kind, g):
        return (1 if kind is self.own else 2) + PRIMED if g == 0 else 0

    def step(self, u):
        order = ([("turn", 0, h) for h in range(KD)]
                 + [("project", 0, a) for a in range(3)] + [("context", 0, a) for a in range(4)]
                 + [("value", 0, v) for v in range(self.OWN_V)] + [("context value", 0, v) for v in range(self.CON_V)]
                 + [("project", 1, a) for a in range(3)] + [("context", 1, a) for a in range(4)])
        return order[u]

    def load(self, sp, d):
        sp.dma_start(self.w[:], d["xa_w"].rearrange("(h p) n -> p h n", p=P)).then_inc(self.s_w, 16)
        sp.dma_start(self.wc[:], d["xa_wc"]).then_inc(self.s_w, 16)
        sp.dma_start(self.bcol[:], d["xa_bcol"]).then_inc(self.s_w, 16)
        sp.dma_start(self.brow[:], d["xa_brow"]).then_inc(self.s_w, 16)

    def pe(self, pe, n, u, dst, side_free, done):
        ln, w, wc, cT = self.ln, self.w, self.wc, self.cT
        what, half, a = self.step(u)
        if what == "turn":
            if a == 0:
                pe.wait_ge(ln.s_xn, n * TT + TT)
            for t in range(TT):
                mm = pe.transpose(dst[:, t * P:(t + 1) * P], ln.xn[:, t, a * P:(a + 1) * P], self.k.ident[:])
        elif what == "project":
            if half == 0 and a == 0:
                pe.wait_ge(side_free, done(self.TURN - 1))
            for h in range(KD):
                mm = pe.matmul(dst, w[:, h, a * D + half * P:a * D + (half + 1) * P], ln.xT[:, h, :],
                               start=h == 0, stop=h == KD - 1)
        elif what == "context":
            if half == 0 and a == 0:
                pe.wait_ge(self.s_c, n * 16 + 16)
            at, N = self.con.chunks[a]
            mm = pe.matmul(dst[:, 0:N], wc[:, half * P:(half + 1) * P], cT[:, at:at + N], start=True, stop=True)
        elif what == "value":
            for t in range(2 * a, 2 * a + 2):
                for h in range(KD):
                    mm = pe.matmul(dst[:, (t % 2) * D:(t % 2 + 1) * D], ln.xT[:, h, t * P:(t + 1) * P],
                                   w[:, h, 3 * D:], start=h == 0, stop=h == KD - 1)
        else:
            for t in range(2 * a, min(2 * a + 2, CT)):
                kn = min(P, LC - t * P)
                mm = pe.matmul(dst[0:kn, (t % 2) * D:(t % 2 + 1) * D], cT[:, t * P:t * P + kn], wc[:, D:],
                               start=True, stop=True)
        return mm

    def dve(self, dve, n, u, src):
        what, half, a = self.step(u)
        if what == "turn":
            return dve.tensor_copy(self.ln.xT[:, a, :], src)
        if what in ("project", "context"):
            if what == "project" and a == 0:
                dve.wait_ge(self.s_split, n * (KD * 8) + half * 8 + PRIMED)
            at, N = (a * T, T) if what == "project" else self.con.chunks[a]
            to = at if what == "project" else 3 * T + at
            col = a if what == "project" else 3
            return dve.tensor_scalar(self.full[:, to:to + N], src[:, 0:N], self.bcol[:, half, col:col + 1],
                                     None, ALU.add)
        if what == "value":
            if a == 0:
                dve.wait_ge(self.s_values, n * self.VALUES + PRIMED)
            return dve.tensor_tensor(self.nv[:, 2 * a:2 * a + 2, :], src.rearrange("p (t n) -> p t n", n=D),
                                     bc(self.brow[:, 0:1], [P, 2, D]), ALU.add)
        tiles = min(2, CT - 2 * a)
        kn = P if a < self.CON_V - 1 else CLAST
        return dve.tensor_tensor(self.ncv[0:kn, 2 * a:2 * a + tiles, :],
                                 src[0:kn, 0:tiles * D].rearrange("p (t n) -> p t n", n=D),
                                 bc(self.brow[0:kn, 1:2], [kn, tiles, D]), ALU.add)

    def dve_start(self, dve, n):
        self.ln.stats(dve, n, n)

    def dve_between(self, dve, n, i):
        if i == 0:
            self.ln.scale(dve, n, n)

    def act_start(self, act, n):
        self.ln.rstd_of(act, n)

    def act_between(self, act, n, i):
        pass

    def pool(self, pool, n, side_free, done):
        full, parts = self.full, self.parts
        for half in range(KD):
            if half:
                pool.wait_ge(self.stored[0], n * (32 * Split.STORES) + 32 * Split.STORES)
            elif not (isinstance(n, int) and n == 0):
                pool.wait_ge(self.stored[1], n * (32 * Split.STORES))
            first = self.TURN + half * (self.HALF + self.OWN_V + self.CON_V)
            for piece, (last, cols) in enumerate(((first + self.QUERIES - 1, slice(0, 3 * T)),
                                                  (first + self.HALF - 1, slice(3 * T, self.N)))):
                made = n * (KD * 8) + half * 8 + piece * 4 + PRIMED
                ones = bc(self.k.one[:], [P, cols.stop - cols.start])
                pool.wait_ge(side_free, done(last))
                pool.tensor_tensor(parts[:, 0, cols], full[:, cols], ones, ALU.mult).then_inc(self.s_split, 1)
                pool.wait_ge(self.s_split, made + 1)
                pool.tensor_tensor(full[:, cols], full[:, cols], parts[:, 0, cols], ALU.subtract)\
                    .then_inc(self.s_split, 1)
                pool.wait_ge(self.s_split, made + 2)
                pool.tensor_tensor(parts[:, 1, cols], full[:, cols], ones, ALU.mult).then_inc(self.s_split, 1)
                pool.wait_ge(self.s_split, made + 3)
                pool.tensor_tensor(parts[:, 2, cols], full[:, cols], parts[:, 1, cols], ALU.subtract)\
                    .then_inc(self.s_split, 1)

    def store(self, sp, n, half):
        made = n * (KD * 8) + half * 8 + PRIMED
        sp.wait_ge(self.s_split, made + 4)
        Split.store_queries(sp, self.own.dq, n, half, self.parts[:, :, 0:T], self.stored[half])
        Split.store_keys(sp, self.own.dk, n, half, self.parts[:, :, T:2 * T], self.stored[half])
        Split.store_queries(sp, self.con.dq, n, half, self.parts[:, :, 2 * T:3 * T], self.stored[half])
        sp.wait_ge(self.s_split, made + 8)
        Split.store_keys(sp, self.con.dk, n, half, self.parts[:, :, 3 * T:], self.stored[half])

    def act_values(self, act, n, side_free, done):
        by_head = "p t (h f) -> p t h f"
        last = self.TURN + self.HALF + self.OWN_V + self.CON_V - 1
        act.wait_ge(side_free, done(last))
        act.activation(self.own.V[:, :, :, 0:HD], self.nv[:].rearrange(by_head, f=HD), ACT.Copy)\
           .then_inc(self.s_values, 1)
        act.activation(self.con.V[0:CLAST, CT - 1, :, 0:HD],
                       self.ncv[0:CLAST, CT - 1].rearrange("p (h f) -> p h f", f=HD), ACT.Copy)
        act.activation(self.con.V[:, 0:CT - 1, :, 0:HD], self.ncv[:, 0:CT - 1].rearrange(by_head, f=HD), ACT.Copy)\
           .then_inc(self.s_values, 1)


def cross_attention(nc, k, d):
    ctx = ExitStack()
    with ctx:
        sb, ps, sem = tools(nc, ctx, "xa")
        bank = ps("bank", [P, 8, 512])
        own = Heads(nc, sb, sem, "own", T, True)
        con = Heads(nc, sb, sem, "con", LC, False)
        prep = CrossPrep(nc, k, sb, sem, own, con)
        calls = [(own, 0), (own, 1), (con, 0), (con, 1), (con, 2), (con, 3), (own, 2), (own, 3)]
        counts = (0, 0, 5, 5, 5, prep.STEPS - 15, 0, 0)
        prep_at = [range(sum(counts[:i]), sum(counts[:i + 1])) for i in range(len(calls))]
        at = Attention(k, sb, sem, bank, calls, prep, prep_at)
        pr = Project(nc, k, sb, sem, bank, "pr", prep.ln.xT)
        s_y = sem("y")
        STORED = 32 * Split.STORES

        with nc.Block() as block:
            @block.sync
            def _(sp):
                prep.load(sp, d)
                pr.load(sp, d["xa_wp"], d["xa_bp"])
                sp.dma_start(prep.cT[:], d["ctxT"][0]).then_inc(prep.s_c, 16)
                for half in range(KD):
                    prep.store(sp, 0, half)

                sp.wait_ge(prep.stored[0], STORED)
                for i in (0, 1, 2, 3):
                    at.sp_load(sp, 0, i, fresh=True)
                with sp.Fori(0, B - 1) as b:
                    sp.wait_ge(at.side_free, at.before(b))
                    sp.dma_start(prep.cT[:], d["ctxT"][b + 1]).then_inc(prep.s_c, 16)
                    sp.wait_ge(prep.stored[1], b * STORED + STORED)
                    for i in (6, 7, 4):
                        at.sp_load(sp, b, i)
                    prep.store(sp, b + 1, 0)
                    at.sp_load(sp, b, 5)
                    prep.store(sp, b + 1, 1)
                    for i in (0, 1, 2, 3):
                        at.sp_load(sp, b, i, ahead=True)
                sp.wait_ge(prep.stored[1], B * STORED)
                for i in (6, 7, 4, 5):
                    at.sp_load(sp, B - 1, i)

            @block.gpsimd
            def _(pool):
                pool.sem_inc(prep.s_split, PRIMED)
                own.clear(pool)
                con.clear(pool)
                prep.pool(pool, 0, at.side_free, at.alone_done)
                with pool.Fori(0, B - 1) as b:
                    prep.pool(pool, b + 1, at.side_free, at.done(b))

            @block.tensor
            def _(pe):
                pe.wait_ge(own.s_const, 4)
                pe.wait_ge(con.s_const, 4)
                pe.wait_ge(prep.s_w, 64)
                at.pe_prepare(pe, 0)

                with pe.Fori(0, B - 1) as b:
                    at.pe_batch(pe, b, at.before(b), at.with_prep, pr, own.y, s_y)
                at.pe_batch(pe, B - 1, at.before(B - 1), at.alone, pr, own.y, s_y)

            @block.vector
            def _(dve):
                dve.sem_inc(pr.s_x, PRIMED)
                dve.wait_ge(own.s_const, 4)
                dve.wait_ge(con.s_const, 4)
                dve.wait_ge(prep.s_w, 64)
                at.dve_prepare(dve, 0)

                def add_kinds(dve):
                    return dve.tensor_tensor(own.y[:], own.y[:], con.y[:], ALU.add)

                with dve.Fori(0, B - 1) as b:
                    at.dve_batch(dve, b, at.before(b), at.with_prep, pr, add_kinds, s_y)
                at.dve_batch(dve, B - 1, at.before(B - 1), at.alone, pr, add_kinds, s_y)

            @block.scalar
            def _(act):
                act.sem_inc(prep.s_values, PRIMED)
                act.preload_act_table_set(EXP_LN)
                act.wait_ge(own.s_const, 4)
                act.wait_ge(con.s_const, 4)
                at.act_prepare(act, 0)
                prep.act_values(act, 0, at.side_free, at.alone_done)
                with act.Fori(0, B - 1) as b:
                    at.act_batch(act, b, at.with_prep)
                    act.wait_ge(at.summed, b * at.NK + at.NK)
                    prep.act_values(act, b + 1, at.side_free, at.done(b))
                at.act_batch(act, B - 1, at.alone)


def quantized_ffn(nc, k, d):
    ROUND = 1.5 * 2.0 ** 23
    ctx = ExitStack()
    with ctx:
        sb, ps, sem = tools(nc, ctx, "qf")
        xq = sb("xq", [P, KD, NT * P])
        wi = sb("wi", [P, FT, D])
        wiq = sb("wiq", [P, KD, F])
        wo = sb("wo", [P, FT, D])
        bi = sb("bi", [P, FT])
        bo = sb("bo", [P, D])
        am, cl, rc, sc, isc = (sb(x, [P, 2, FT]) for x in ("am", "cl", "rc", "sc", "isc"))
        xm, xmf, xa = sb("xm", [P, 1]), sb("xmf", [P, 4]), sb("xa", [P, 1])
        xs, xis = sb("xs", [P, 1]), sb("xis", [P, 1])
        ha, hmf, hs, his = sb("ha", [P, 1]), sb("hmf", [P, 4]), sb("hs", [P, 1]), sb("his", [P, 1])
        hm = sb("hm", [P, B * FT])
        hm1 = sb("hm1", [P, 1])
        isf = sb("isf", [P, FT])
        hT = sb("hT", [P, B, FT, T])
        bank = ps("bank", [P, 8, 512])
        xn = hT[:].rearrange("p b f t -> p (b f t)")[:, 0:NT * D].rearrange("p (t n) -> p t n", n=D)
        ln = WholeNorm(k, sb, sem, xn, xq, bank[:, 4:8, :])
        s_w, s_wi, s_keep, s_wt, s_wtc = sem("w"), sem("wi"), sem("keep"), sem("wt"), sem("wtc")
        s_xm, s_xa, s_xq, s_is, s_h, s_g, s_hm, s_hm1, s_ha, s_hq, s_o, s_x = (
            sem(x) for x in ("xm", "xa", "xq", "is", "h", "g", "hm", "hm1", "ha", "hq", "o", "x"))
        c_dve = sem("c_dve")

        with nc.Block() as block:
            @block.sync
            def _(sp):
                sp.dma_start(wi[:], d["qf_wi"].rearrange("(f p) n -> p f n", p=P)).then_inc(s_wi, 16)
                sp.dma_start(wo[:], d["qf_wo"].rearrange("(f p) n -> p f n", p=P)).then_inc(s_w, 16)
                sp.dma_start(bi[:], d["qf_bi"]).then_inc(s_w, 16)
                sp.dma_start(bo[:], d["qf_bo"]).then_inc(s_w, 16)

            @block.gpsimd
            def _(pool):
                pool.wait_ge(s_xm, 1)
                pool.partition_all_reduce(xa[:], xm[:], P, RMAX).then_inc(s_xa, 1)
                pool.wait_ge(s_hm1, 1)
                pool.partition_all_reduce(ha[:], hm1[:], P, RMAX).then_inc(s_ha, 1)

            def scales(own, dve, amax, floor_to, rec, scale, inv, top):
                own.link(dve.tensor_scalar(floor_to, amax, 1e-8, None, ALU.max))
                own.link(dve.reciprocal(rec, floor_to))
                dve.tensor_scalar(inv, floor_to, 1.0 / top, None, ALU.mult)
                own.link(dve.tensor_scalar(scale, rec, top, None, ALU.mult))

            @block.tensor
            def _(pe):
                pe.wait_ge(s_wt, 1)
                for f in range(FT):
                    for h in range(KD):
                        mm = pe.transpose(bank[:, 2 * h + f // 4, (f % 4) * P:(f % 4 + 1) * P],
                                          wi[:, f, h * P:(h + 1) * P], k.ident[:])
                mm.then_inc(s_wtc, 1)
                for b in range(B):
                    ln.turn(pe, b)
                pe.wait_ge(ln.s_xT, B)
                pe.wait_ge(s_wtc, 2)
                for b in range(B):
                    pe.wait_ge(s_xq, b + 1)
                    for f in range(FT):
                        i = b * FT + f
                        if i >= 4:
                            pe.wait_ge(s_g, i - 3)
                        for h in range(KD):
                            mm = pe.matmul(bank[:, 4 + i % 4, :], wiq[:, h, f * P:(f + 1) * P],
                                           xq[:, h, b * T:(b + 1) * T], start=h == 0, stop=h == KD - 1)
                        mm.then_inc(s_h, 1)
                for t in range(NT):
                    pe.wait_ge(s_hq, t + 1)
                    if t >= 8:
                        pe.wait_ge(s_x, t - 7)
                    for f in range(FT):
                        mm = pe.matmul(bank[:, t % 8, 0:D], hT[:, t // TT, f, (t % TT) * P:(t % TT + 1) * P],
                                       wo[:, f, :], start=f == 0, stop=f == FT - 1)
                    mm.then_inc(s_o, 1)

            @block.vector
            def _(dve):
                own = Chain(dve, c_dve, 64)
                own.begin(0)

                def weight(w, a):
                    own.link(dve.reduce_max(am[:, a], w[:], axis=AX, apply_absolute_value=True))
                    scales(own, dve, am[:, a], cl[:, a], rc[:, a], sc[:, a], isc[:, a], 127.0)
                    for f in range(FT):
                        ins = dve.tensor_scalar(w[:, f, :], w[:, f, :], sc[:, a, f:f + 1], ROUND, ALU.mult, ALU.add)
                    own.link(ins)
                    own.link(dve.tensor_scalar(w[:], w[:], ROUND, 127.0, ALU.subtract, ALU.min))
                    return dve.tensor_scalar(w[:], w[:], -128.0, None, ALU.max)

                ln.stats(dve)
                dve.wait_ge(s_wi, 16)
                weight(wi, 0).then_inc(s_wt, 1)
                ln.scale(dve)
                for b in range(B):
                    ln.keep(dve, b)
                    dve.wait_ge(ln.s_xT, b + 1)
                    dve.reduce_max(xmf[:, b:b + 1], xq[:, :, b * T:(b + 1) * T], axis=mybir.AxisListType.XY,
                                   apply_absolute_value=True).then_inc(s_keep, 1)
                dve.wait_ge(s_keep, B)
                dve.reduce_max(xm[:], xmf[:], axis=AX).then_inc(s_xm, 1)
                dve.wait_ge(s_xa, 1)
                scales(own, dve, xa[:], xm[:], xis[:], xs[:], his[:], 32767.0)
                dve.tensor_scalar(isf[:], isc[:, 0], his[:], None, ALU.mult).then_inc(s_is, 1)
                for b in range(B):
                    x = xq[:, :, b * T:(b + 1) * T]
                    own.link(dve.tensor_scalar(x, x, xs[:], ROUND, ALU.mult, ALU.add))
                    own.link(dve.tensor_scalar(x, x, ROUND, 32767.0, ALU.subtract, ALU.min))
                    dve.tensor_scalar(x, x, -32768.0, None, ALU.max).then_inc(s_xq, 1)
                dve.wait_ge(s_w, 48)
                own.link(weight(wo, 1))
                for f in range(FT):
                    ins = dve.tensor_scalar(wo[:, f, :], wo[:, f, :], isc[:, 1, f:f + 1], None, ALU.mult)
                own.link(ins)
                for i in range(B * FT):
                    dve.wait_ge(s_g, i + 1)
                    dve.reduce_max(hm[:, i:i + 1], hT[:, i // FT, i % FT, :], axis=AX,
                                   apply_absolute_value=True).then_inc(s_hm, 1)
                    if i % FT == FT // 2:
                        tiles = slice(i // FT * TT, (i // FT + 1) * TT)
                        own.link(dve.tensor_tensor(k.x[:, tiles, :], k.x[:, tiles, :],
                                                   bc(bo[:].unsqueeze(1), [P, TT, D]), ALU.add))
                dve.wait_ge(s_hm, B * FT)
                dve.reduce_max(hm1[:], hm[:], axis=AX).then_inc(s_hm1, 1)
                dve.wait_ge(s_ha, 1)
                scales(own, dve, ha[:], hmf[:, 0:1], hmf[:, 1:2], hs[:], his[:], 32767.0)
                def output(t):
                    dve.wait_ge(s_o, t + 1)
                    dve.tensor_tensor(k.x[:, t, :], bank[:, t % 8, 0:D], k.x[:, t, :], ALU.add).then_inc(s_x, 1)

                BEHIND = 3
                for t in range(NT):
                    h = hT[:, t // TT, :, (t % TT) * P:(t % TT + 1) * P]
                    own.link(dve.tensor_scalar(h, h, hs[:], ROUND, ALU.mult, ALU.add))
                    own.link(dve.tensor_scalar(h, h, ROUND, 32767.0, ALU.subtract, ALU.min))
                    dve.tensor_scalar(h, h, -32768.0, his[:], ALU.max, ALU.mult).then_inc(s_hq, 1)
                    if t >= BEHIND:
                        output(t - BEHIND)
                for t in range(NT - BEHIND, NT):
                    output(t)
                dve.wait_ge(s_x, NT)
                own.end()

            @block.scalar
            def _(act):
                act.preload_act_table_set(EXP_LN)
                ln.rstd(act)
                act.wait_ge(s_wtc, 1)
                act.activation(wiq[:], bank[:, 0:4, :].rearrange("p (h a) n -> p h (a n)", h=KD), ACT.Copy)\
                   .then_inc(s_wtc, 1)
                act.wait_ge(s_w, 48)
                act.wait_ge(s_is, 1)
                for b in range(B):
                    for f in range(FT):
                        i = b * FT + f
                        act.wait_ge(s_h, i + 1)
                        act.activation(hT[:, b, f, :], bank[:, 4 + i % 4, :], ACT.Gelu, bias=bi[:, f:f + 1],
                                       scale=isf[:, f:f + 1]).then_inc(s_g, 1)


STAGES = [gated_attention, context_attention, experts, self_attention, cross_attention, quantized_ffn]


def program(nc, d, out, stages):
    k = Core()
    ctx = ExitStack()
    with ctx:
        constants(nc, k, d["x"], ctx)
        for stage in stages:
            taken = nc.snapshot_sems()
            stage(nc, k, d)
            nc.all_engine_barrier()
            nc.clear_and_free_semaphores(nc.allocated_since(taken))
            nc.all_engine_barrier()
        stored = nc.alloc_semaphore("stored")
        with nc.Block() as block:
            @block.sync
            def _(sp):
                sp.dma_start(out.rearrange("b (t p) d -> p (b t) d", p=P), k.x[:]).then_inc(stored, 16)
                sp.wait_ge(stored, 16)


def layout(i):
    f = {n: np.asarray(a) for n, a in i.items()}
    d = {"x": f["x"]}
    wq, wk, wv = f["L0_attn_Wq"], f["L0_attn_Wk"], f["L0_attn_Wv"]
    d["ga_w"] = np.stack([np.concatenate(
        [wq[:, 256 * j:256 * j + 256], wk[:, 64 * j:64 * j + 64], wk[:, 64 * j:64 * j + 64],
         wv[:, 64 * j:64 * j + 64]], 1) for j in range(HKV)])
    d["ga_small"] = np.concatenate([f["L0_attn_Wa"], f["L0_attn_Walpha"], f["L0_attn_Wb"]], 1)
    c = f["L0_attn_Wconv"]
    d["ga_taps"] = np.stack([np.stack(
        [c[256 * j:256 * j + 128], c[256 * j + 128:256 * j + 256],
         np.concatenate([c[1024 + 64 * j:1088 + 64 * j]] * 2), np.concatenate([c[1280 + 64 * j:1344 + 64 * j]] * 2)],
        1) for j in range(HKV)])
    d["ga_rows"] = np.tile(np.concatenate([f["L0_attn_A_log"], f["L0_attn_dt_bias"]]), (P, 1))
    d["ga_wo"] = f["L0_attn_Wo"].reshape(HKV, 256, D)
    d["ga_normw"] = np.tile(f["L0_attn_norm_w"], 2)[:, None]
    d["ctxT"] = f["ctx_512"].transpose(0, 2, 1)
    d["ca_wq"], d["ca_wk"], d["ca_wv"] = (f[f"L0_xattn_W{x}"] for x in "qkv")
    d["ca_bq"], d["ca_bk"] = (f[f"L0_xattn_b{x}"].reshape(KD, P).T for x in "qk")
    d["ca_bv"] = np.tile(f["L0_xattn_bv"], (P, 1))
    d["ex_wr"] = f["L0_ffn_Wr"].T.reshape(KD, P, E).transpose(1, 0, 2)
    d["ex_br"] = np.tile(f["L0_ffn_br"], (P, 1))
    d["ex_b2"] = f["L0_ffn_b2"]
    d["ex_b1"] = f["L0_ffn_b1"].reshape(E, FT, P).transpose(0, 2, 1)
    d["ex_gamma"], d["ex_beta"] = (np.tile(f[f"L0_ffn_{x}"], (P, 1)) for x in ("gamma", "beta"))
    d["ex_w1"] = f["L0_ffn_W1"].transpose(0, 2, 1)
    d["ex_w2"] = f["L0_ffn_W2"].transpose(0, 2, 1)

    d["sa_w"] = f["L1_attn_Wqkv"].T
    d["sa_b"] = np.tile(f["L1_attn_bqkv"], (P, 1))
    d["sa_nw"] = np.tile(np.concatenate([np.tile(f["L1_attn_qn_w"], H), np.tile(f["L1_attn_kn_w"], H)]), (P, 1))
    d["sa_wp"] = f["L1_attn_Wproj"].T
    d["sa_bp"] = np.tile(f["L1_attn_bproj"], (P, 1))
    x = {n: f[f"L1_xattn_{n}"] for n in ("Wq", "bq", "Wk", "bk", "Wv", "bv", "Wcq", "bcq", "Wck", "bck", "Wcv", "bcv")}
    d["xa_w"] = np.concatenate([x["Wq"], x["Wk"], x["Wcq"], x["Wv"]], 1)
    d["xa_wc"] = np.concatenate([x["Wck"], x["Wcv"]], 1)
    d["xa_bcol"] = np.stack([x[n].reshape(KD, P) for n in ("bq", "bk", "bcq", "bck")]).transpose(2, 1, 0)
    d["xa_brow"] = np.tile(np.stack([x["bv"], x["bcv"]]), (P, 1, 1))
    d["xa_wp"] = f["L1_xattn_Wp"]
    d["xa_bp"] = np.tile(f["L1_xattn_bp"], (P, 1))
    d["qf_wi"] = f["L1_ffn_W_in"].T
    d["qf_wo"] = f["L1_ffn_W_out"]
    d["qf_bi"] = f["L1_ffn_b_in"].reshape(FT, P).T
    d["qf_bo"] = np.tile(f["L1_ffn_b_out"], (P, 1))
    return {n: np.ascontiguousarray(a) for n, a in d.items()}


def kernel(**inputs):
    import concourse.bacc as _bacc
    from concourse.bass_utils import run_bass_kernel_spmd as _run

    nc = _bacc.Bacc("TRN2", target_bir_lowering=False, num_devices=1)
    d = layout(inputs)
    arrays = {f"in_{n}": a for n, a in d.items()}
    aps = {n: nc.dram_tensor(f"in_{n}", a.shape, mybir.dt.from_np(a.dtype), kind="ExternalInput").ap()
           for n, a in d.items()}
    out = nc.dram_tensor("out_x", (B, T, D), F32, kind="ExternalOutput").ap()
    program(nc, aps, out, STAGES)
    r = _run(nc, [arrays], core_ids=[0])
    return r.results[0]["out_x"]
```
